# Optimizing a Trainium2 kernel written in Bass

```python
import numpy as np
import jax
import jax.numpy as jnp

def _softmax(x, axis=-1):
    return jax.nn.softmax(x, axis=axis)

def _gelu(x):
    return jax.nn.gelu(x, approximate=True)

def _silu(x):
    return jax.nn.silu(x)

def _sigmoid(x):
    return jax.nn.sigmoid(x)

def _layernorm(x, axis=-1, eps=1e-05):
    m = jnp.mean(x, axis=axis, keepdims=True)
    v = jnp.var(x, axis=axis, keepdims=True)
    return (x - m) / jnp.sqrt(v + eps)

def _scatter_add(tgt, idx, src, axis=0):
    return tgt.at[idx].add(src)

def _segment_sum(src, seg, n):
    return jax.ops.segment_sum(src, seg, n)
kernel_name = 'mk_adaln_attn_ffn_d1_seqx_r8_0d362e'

def setup_inputs(seed: int=0):
    np.random.seed(seed)
    _w = jnp.asarray

    def _rec_inputs():
        import jax
        import jax.numpy as jnp
        _rk = jax.random.key(seed)
        x = 7.22e-05 + 1 * jax.random.normal(jax.random.fold_in(_rk, 1), (32, 128, 128), jnp.float32)
        _lenS = 128 - jax.random.randint(jax.random.fold_in(_rk, 7), (32,), 0, max(1, 128 // 4) + 1, jnp.int32)
        _lenS2 = 128 - jax.random.randint(jax.random.fold_in(_rk, 8), (32,), 0, max(1, 128 // 4) + 1, jnp.int32)
        cond_64 = -0.104238 + 1.01173 * jax.random.normal(jax.random.fold_in(_rk, 11), (32, 64), jnp.float32)
        fside_16xSxS_0 = -5.72187e-05 + 0.999849 * jax.random.normal(jax.random.fold_in(_rk, 12), (16, 128, 128), jnp.float32)
        _validS = jnp.arange(128)[None, :] < _lenS[:, None]
        _validS2 = jnp.arange(128)[None, :] < _lenS2[:, None]
        _causal = jnp.tril(jnp.ones((128, 128), dtype=bool))
        mask_BxS_bk0 = jnp.logical_not(jnp.broadcast_to(_validS[:, :], (32, 128)))
        return (x, cond_64, fside_16xSxS_0, mask_BxS_bk0)
    x, cond_64, fside_16xSxS_0, mask_BxS_bk0 = _rec_inputs()

    def _L0_cond_setup():
        import jax, jax.numpy as jnp
        import numpy as np
        B, S, H = (4, 256, 128)
        E = 8
        M = 64
        K = 2
        N_SHARED = 2
        SM = M * N_SHARED
        G = 64
        GE_TEMP = 1.0
        ALPHA = 0.001
        SEQ_AUX = True
        NORM_TOPK = True
        COS_TEMP = 0.78
        CONS_ALPHA = 0.01
        LEAKY_SLOPE = 0.01
        EPS_COS = 1e-08

        def _leaky(x):
            return jnp.where(x >= 0, x, LEAKY_SLOPE * x)

        def _moe_forward(hidden_states, g, wt, wg, w_gate, w_up, w_down, sw_gate, sw_up, sw_down):
            b, s, h = hidden_states.shape
            x = hidden_states.reshape(-1, h)
            T = x.shape[0]
            logits_h = x @ wt.T
            logits_g = g @ wg.T
            logits_g = jnp.repeat(logits_g, s, axis=0)
            logits = (logits_h + logits_g / GE_TEMP) / (1.0 + 1.0 / GE_TEMP)
            scores = jax.nn.softmax(logits, axis=-1)
            topk_w, topk_idx = jax.lax.top_k(scores, K)
            if K > 1 and NORM_TOPK:
                topk_w = topk_w / (topk_w.sum(-1, keepdims=True) + 1e-20)
            onehot = jax.nn.one_hot(topk_idx.reshape(b, s * K), E, dtype=jnp.float32)
            ce = onehot.sum(1) / (s * K / E)
            aux_loss = (ce * scores.reshape(b, s, E).mean(1)).sum(1).mean() * ALPHA
            gp = _leaky(jnp.einsum('th,ehm->etm', x, w_gate))
            up = jnp.einsum('th,ehm->etm', x, w_up)
            y_all = jnp.einsum('etm,emh->eth', gp * up, w_down)
            y_sel = y_all[topk_idx, jnp.arange(T)[:, None], :]
            y = (y_sel * topk_w[..., None]).sum(1).reshape(b, s, h)
            p = _leaky(hidden_states @ sw_gate) * (hidden_states @ sw_up) @ sw_down
            y = y + p
            num = jnp.sum(y * p, -1)
            den = jnp.maximum(jnp.linalg.norm(y, axis=-1), EPS_COS) * jnp.maximum(jnp.linalg.norm(p, axis=-1), EPS_COS)
            closs = CONS_ALPHA * jnp.mean(num / den / (1.0 + COS_TEMP))
            return (y, aux_loss + closs)
        key = jax.random.key(seed)
        ks = jax.random.split(key, 12)
        sh = 1.0 / np.sqrt(H)
        sm = 1.0 / np.sqrt(M)
        ssm = 1.0 / np.sqrt(SM)
        sg = 1.0 / np.sqrt(G)
        return {'hidden_states': jax.random.normal(ks[0], (B, S, H), jnp.float32), 'g': jax.random.normal(ks[1], (B, G), jnp.float32), 'wt': jax.random.uniform(ks[2], (E, H), jnp.float32, -sh, sh), 'wg': jax.random.uniform(ks[3], (E, G), jnp.float32, -sg, sg), 'w_gate': jax.random.uniform(ks[4], (E, H, M), jnp.float32, -sh, sh), 'w_up': jax.random.uniform(ks[5], (E, H, M), jnp.float32, -sh, sh), 'w_down': jax.random.uniform(ks[6], (E, M, H), jnp.float32, -sm, sm), 'sw_gate': jax.random.uniform(ks[7], (H, SM), jnp.float32, -sh, sh), 'sw_up': jax.random.uniform(ks[8], (H, SM), jnp.float32, -sh, sh), 'sw_down': jax.random.uniform(ks[9], (SM, H), jnp.float32, -ssm, ssm)}
    _L0_cond_all = _L0_cond_setup()
    _L0_cond_in = {k: v for k, v in _L0_cond_all.items() if k in ('wt', 'wg', 'w_gate', 'w_up', 'w_down', 'sw_gate', 'sw_up', 'sw_down')}
    del _L0_cond_all

    def _L0_attn_setup():
        import jax, jax.numpy as jnp
        import numpy as np
        import math
        N_EMBD = 128
        D_STATE = 16
        D_CONV = 4
        EXPAND = 2
        D_INNER = EXPAND * N_EMBD
        DT_RANK = math.ceil(N_EMBD / 16)
        B, L = (2, 256)
        LN_EPS = 1e-05

        def _selective_scan(u, delta, A, Bt, Ct, D):

            def step(h, inp):
                d_t, B_t, C_t, u_t = inp
                dA = jnp.exp(d_t[..., None] * A)
                dBu = d_t[..., None] * B_t[:, None, :] * u_t[..., None]
                h = dA * h + dBu
                y = jnp.einsum('bds,bs->bd', h, C_t)
                return (h, y)
            h0 = jnp.zeros((u.shape[0], A.shape[0], A.shape[1]), u.dtype)
            xs = (jnp.swapaxes(delta, 0, 1), jnp.swapaxes(Bt, 0, 1), jnp.swapaxes(Ct, 0, 1), jnp.swapaxes(u, 0, 1))
            _, ys = jax.lax.scan(step, h0, xs)
            return jnp.swapaxes(ys, 0, 1) + u * D
        key = jax.random.key(seed)
        ks = jax.random.split(key, 12)
        s = lambda fan_in: 1.0 / np.sqrt(fan_in)
        x = jax.random.normal(ks[0], (B, L, N_EMBD), dtype=jnp.float32)
        ln_g = jnp.ones((N_EMBD,), jnp.float32)
        ln_b = jnp.zeros((N_EMBD,), jnp.float32)
        in_proj_w = jax.random.normal(ks[1], (2 * D_INNER, N_EMBD), jnp.float32) * s(N_EMBD)
        conv_w = jax.random.normal(ks[2], (D_INNER, 1, D_CONV), jnp.float32) * s(D_CONV)
        conv_b = jax.random.normal(ks[3], (D_INNER,), jnp.float32) * s(D_CONV)
        x_proj_w = jax.random.normal(ks[4], (DT_RANK + 2 * D_STATE, D_INNER), jnp.float32) * s(D_INNER)
        dt_proj_w = jax.random.normal(ks[5], (D_INNER, DT_RANK), jnp.float32) * s(DT_RANK)
        dt = jnp.exp(jax.random.uniform(ks[6], (D_INNER,)) * (np.log(0.1) - np.log(0.001)) + np.log(0.001))
        dt_proj_b = dt + jnp.log(-jnp.expm1(-dt))
        A_log = jnp.log(jnp.tile(jnp.arange(1, D_STATE + 1, dtype=jnp.float32)[None, :], (D_INNER, 1)))
        D = jnp.ones((D_INNER,), jnp.float32)
        out_proj_w = jax.random.normal(ks[7], (N_EMBD, D_INNER), jnp.float32) * s(D_INNER)
        return {'x': x, 'ln_g': ln_g, 'ln_b': ln_b, 'in_proj_w': in_proj_w, 'conv_w': conv_w, 'conv_b': conv_b, 'x_proj_w': x_proj_w, 'dt_proj_w': dt_proj_w, 'dt_proj_b': dt_proj_b, 'A_log': A_log, 'D': D, 'out_proj_w': out_proj_w}
    _L0_attn_all = _L0_attn_setup()
    _L0_attn_in = {k: v for k, v in _L0_attn_all.items() if k in ('ln_g', 'ln_b', 'in_proj_w', 'conv_w', 'conv_b', 'x_proj_w', 'dt_proj_w', 'dt_proj_b', 'A_log', 'D', 'out_proj_w')}
    del _L0_attn_all

    def _L0_cond2_setup():
        import jax, jax.numpy as jnp
        import numpy as np
        B, N, DIM, H, DH = (2, 256, 128, 16, 64)
        INNER = H * DH
        EPS = 1e-05

        def layernorm(x, g):
            mean = jnp.mean(x, axis=-1, keepdims=True)
            var = jnp.var(x, axis=-1, keepdims=True)
            return (x - mean) * jax.lax.rsqrt(var + EPS) * g
        key = jax.random.key(seed)
        ks = jax.random.split(key, 10)
        x = jax.random.normal(ks[0], (B, N, DIM), dtype=jnp.float32)
        attn_bias = jax.random.normal(ks[1], (H, N, N), dtype=jnp.float32)
        mask = jax.random.randint(ks[2], (B, N), 0, 2).astype(bool)
        g_in = jnp.ones((DIM,), dtype=jnp.float32)
        null_attn_bias = jax.random.normal(ks[3], (H,), dtype=jnp.float32)
        null_kv = jax.random.normal(ks[4], (2, DH), dtype=jnp.float32)
        Wq = jax.random.normal(ks[5], (DIM, INNER), dtype=jnp.float32) * 0.02
        Wkv = jax.random.normal(ks[6], (DIM, 2 * DH), dtype=jnp.float32) * 0.02
        Wo = jax.random.normal(ks[7], (INNER, DIM), dtype=jnp.float32) * 0.02
        g_out = jnp.ones((DIM,), dtype=jnp.float32)
        return {'x': x, 'attn_bias': attn_bias, 'mask': mask, 'g_in': g_in, 'null_attn_bias': null_attn_bias, 'null_kv': null_kv, 'Wq': Wq, 'Wkv': Wkv, 'Wo': Wo, 'g_out': g_out}
    _L0_cond2_all = _L0_cond2_setup()
    _L0_cond2_in = {k: v for k, v in _L0_cond2_all.items() if k in ('g_in', 'null_attn_bias', 'Wq', 'Wkv', 'Wo', 'g_out')}
    del _L0_cond2_all

    def _L0_ffn_setup():
        import jax, jax.numpy as jnp
        import numpy as np
        B, L, D = (2, 256, 128)
        E = 15
        H = D * 1
        K = 3
        T = 1.0
        key = jax.random.key(seed)
        ks = jax.random.split(key, 12)
        s = 0.02
        return {'x': jax.random.normal(ks[0], (B, L, D), dtype=jnp.float32), 'router_W': jax.random.normal(ks[1], (D, E), dtype=jnp.float32) * s, 'router_b': jnp.zeros((E,), dtype=jnp.float32), 'sW1': jax.random.normal(ks[2], (D, H), dtype=jnp.float32) * s, 'sb1': jnp.zeros((H,), dtype=jnp.float32), 'sW2': jax.random.normal(ks[3], (H, D), dtype=jnp.float32) * s, 'sb2': jnp.zeros((D,), dtype=jnp.float32), 'eW1': jax.random.normal(ks[4], (E, D, H), dtype=jnp.float32) * s, 'eb1': jnp.zeros((E, H), dtype=jnp.float32), 'eW2': jax.random.normal(ks[5], (E, H, D), dtype=jnp.float32) * s, 'eb2': jnp.zeros((E, D), dtype=jnp.float32)}
    _L0_ffn_all = _L0_ffn_setup()
    _L0_ffn_in = {k: v for k, v in _L0_ffn_all.items() if k in ('router_W', 'router_b', 'sW1', 'sb1', 'sW2', 'sb2', 'eW1', 'eb1', 'eW2', 'eb2')}
    del _L0_ffn_all
    return {'x': x, 'cond_64': cond_64, 'fside_16xSxS_0': fside_16xSxS_0, 'mask_BxS_bk0': mask_BxS_bk0, 'L0_cond_wt': _L0_cond_in['wt'], 'L0_cond_wg': _L0_cond_in['wg'], 'L0_cond_w_gate': _L0_cond_in['w_gate'], 'L0_cond_w_up': _L0_cond_in['w_up'], 'L0_cond_w_down': _L0_cond_in['w_down'], 'L0_cond_sw_gate': _L0_cond_in['sw_gate'], 'L0_cond_sw_up': _L0_cond_in['sw_up'], 'L0_cond_sw_down': _L0_cond_in['sw_down'], 'L0_attn_ln_g': _L0_attn_in['ln_g'], 'L0_attn_ln_b': _L0_attn_in['ln_b'], 'L0_attn_in_proj_w': _L0_attn_in['in_proj_w'], 'L0_attn_conv_w': _L0_attn_in['conv_w'], 'L0_attn_conv_b': _L0_attn_in['conv_b'], 'L0_attn_x_proj_w': _L0_attn_in['x_proj_w'], 'L0_attn_dt_proj_w': _L0_attn_in['dt_proj_w'], 'L0_attn_dt_proj_b': _L0_attn_in['dt_proj_b'], 'L0_attn_A_log': _L0_attn_in['A_log'], 'L0_attn_D': _L0_attn_in['D'], 'L0_attn_out_proj_w': _L0_attn_in['out_proj_w'], 'L0_cond2_g_in': _L0_cond2_in['g_in'], 'L0_cond2_null_attn_bias': _L0_cond2_in['null_attn_bias'], 'L0_cond2_Wq': _L0_cond2_in['Wq'], 'L0_cond2_Wkv': _L0_cond2_in['Wkv'], 'L0_cond2_Wo': _L0_cond2_in['Wo'], 'L0_cond2_g_out': _L0_cond2_in['g_out'], 'L0_ffn_router_W': _L0_ffn_in['router_W'], 'L0_ffn_router_b': _L0_ffn_in['router_b'], 'L0_ffn_sW1': _L0_ffn_in['sW1'], 'L0_ffn_sb1': _L0_ffn_in['sb1'], 'L0_ffn_sW2': _L0_ffn_in['sW2'], 'L0_ffn_sb2': _L0_ffn_in['sb2'], 'L0_ffn_eW1': _L0_ffn_in['eW1'], 'L0_ffn_eb1': _L0_ffn_in['eb1'], 'L0_ffn_eW2': _L0_ffn_in['eW2'], 'L0_ffn_eb2': _L0_ffn_in['eb2']}

def reference(x, cond_64, fside_16xSxS_0, mask_BxS_bk0, L0_cond_wt, L0_cond_wg, L0_cond_w_gate, L0_cond_w_up, L0_cond_w_down, L0_cond_sw_gate, L0_cond_sw_up, L0_cond_sw_down, L0_attn_ln_g, L0_attn_ln_b, L0_attn_in_proj_w, L0_attn_conv_w, L0_attn_conv_b, L0_attn_x_proj_w, L0_attn_dt_proj_w, L0_attn_dt_proj_b, L0_attn_A_log, L0_attn_D, L0_attn_out_proj_w, L0_cond2_g_in, L0_cond2_null_attn_bias, L0_cond2_Wq, L0_cond2_Wkv, L0_cond2_Wo, L0_cond2_g_out, L0_ffn_router_W, L0_ffn_router_b, L0_ffn_sW1, L0_ffn_sb1, L0_ffn_sW2, L0_ffn_sb2, L0_ffn_eW1, L0_ffn_eb1, L0_ffn_eW2, L0_ffn_eb2):
    import jax
    import jax.numpy as jnp

    def _L0_cond_ref(hidden_states, g, wt, wg, w_gate, w_up, w_down, sw_gate, sw_up, sw_down):
        import jax, jax.numpy as jnp
        import numpy as np
        B, S, H = (4, 256, 128)
        E = 8
        M = 64
        K = 2
        N_SHARED = 2
        SM = M * N_SHARED
        G = 64
        GE_TEMP = 1.0
        ALPHA = 0.001
        SEQ_AUX = True
        NORM_TOPK = True
        COS_TEMP = 0.78
        CONS_ALPHA = 0.01
        LEAKY_SLOPE = 0.01
        EPS_COS = 1e-08

        def _leaky(x):
            return jnp.where(x >= 0, x, LEAKY_SLOPE * x)

        def _moe_forward(hidden_states, g, wt, wg, w_gate, w_up, w_down, sw_gate, sw_up, sw_down):
            b, s, h = hidden_states.shape
            x = hidden_states.reshape(-1, h)
            T = x.shape[0]
            logits_h = x @ wt.T
            logits_g = g @ wg.T
            logits_g = jnp.repeat(logits_g, s, axis=0)
            logits = (logits_h + logits_g / GE_TEMP) / (1.0 + 1.0 / GE_TEMP)
            scores = jax.nn.softmax(logits, axis=-1)
            topk_w, topk_idx = jax.lax.top_k(scores, K)
            if K > 1 and NORM_TOPK:
                topk_w = topk_w / (topk_w.sum(-1, keepdims=True) + 1e-20)
            onehot = jax.nn.one_hot(topk_idx.reshape(b, s * K), E, dtype=jnp.float32)
            ce = onehot.sum(1) / (s * K / E)
            aux_loss = (ce * scores.reshape(b, s, E).mean(1)).sum(1).mean() * ALPHA
            gp = _leaky(jnp.einsum('th,ehm->etm', x, w_gate))
            up = jnp.einsum('th,ehm->etm', x, w_up)
            y_all = jnp.einsum('etm,emh->eth', gp * up, w_down)
            y_sel = y_all[topk_idx, jnp.arange(T)[:, None], :]
            y = (y_sel * topk_w[..., None]).sum(1).reshape(b, s, h)
            p = _leaky(hidden_states @ sw_gate) * (hidden_states @ sw_up) @ sw_down
            y = y + p
            num = jnp.sum(y * p, -1)
            den = jnp.maximum(jnp.linalg.norm(y, axis=-1), EPS_COS) * jnp.maximum(jnp.linalg.norm(p, axis=-1), EPS_COS)
            closs = CONS_ALPHA * jnp.mean(num / den / (1.0 + COS_TEMP))
            return (y, aux_loss + closs)
        y, _ = _moe_forward(hidden_states, g, wt, wg, w_gate, w_up, w_down, sw_gate, sw_up, sw_down)
        return y

    def _L0_attn_ref(x, ln_g, ln_b, in_proj_w, conv_w, conv_b, x_proj_w, dt_proj_w, dt_proj_b, A_log, D, out_proj_w):
        import jax, jax.numpy as jnp
        import numpy as np
        import math
        N_EMBD = 128
        D_STATE = 16
        D_CONV = 4
        EXPAND = 2
        D_INNER = EXPAND * N_EMBD
        DT_RANK = math.ceil(N_EMBD / 16)
        B, L = (2, 256)
        LN_EPS = 1e-05

        def _selective_scan(u, delta, A, Bt, Ct, D):

            def step(h, inp):
                d_t, B_t, C_t, u_t = inp
                dA = jnp.exp(d_t[..., None] * A)
                dBu = d_t[..., None] * B_t[:, None, :] * u_t[..., None]
                h = dA * h + dBu
                y = jnp.einsum('bds,bs->bd', h, C_t)
                return (h, y)
            h0 = jnp.zeros((u.shape[0], A.shape[0], A.shape[1]), u.dtype)
            xs = (jnp.swapaxes(delta, 0, 1), jnp.swapaxes(Bt, 0, 1), jnp.swapaxes(Ct, 0, 1), jnp.swapaxes(u, 0, 1))
            _, ys = jax.lax.scan(step, h0, xs)
            return jnp.swapaxes(ys, 0, 1) + u * D
        mu = jnp.mean(x, axis=-1, keepdims=True)
        var = jnp.var(x, axis=-1, keepdims=True)
        x_norm = (x - mu) * jax.lax.rsqrt(var + LN_EPS) * ln_g + ln_b
        xz = jnp.einsum('bld,ed->ble', x_norm, in_proj_w)
        u, res = jnp.split(xz, 2, axis=-1)
        u_c = jnp.swapaxes(u, 1, 2)
        u_c = jax.lax.conv_general_dilated(u_c, conv_w, window_strides=(1,), padding=[(D_CONV - 1, 0)], dimension_numbers=('NCH', 'OIH', 'NCH'), feature_group_count=D_INNER)
        u_c = jax.nn.silu(jnp.swapaxes(u_c, 1, 2) + conv_b)
        x_dbl = jnp.einsum('bld,ed->ble', u_c, x_proj_w)
        dt, Bt, Ct = jnp.split(x_dbl, [DT_RANK, DT_RANK + D_STATE], axis=-1)
        delta = jax.nn.softplus(jnp.einsum('blr,dr->bld', dt, dt_proj_w) + dt_proj_b)
        A = -jnp.exp(A_log)
        y = _selective_scan(u_c, delta, A, Bt, Ct, D)
        y = y * jax.nn.silu(res)
        out = jnp.einsum('bld,ed->ble', y, out_proj_w)
        return x + out

    def _L0_cond2_ref(x, attn_bias, mask, g_in, null_attn_bias, null_kv, Wq, Wkv, Wo, g_out):
        import jax, jax.numpy as jnp
        import numpy as np
        B, N, DIM, H, DH = (2, 256, 128, 16, 64)
        INNER = H * DH
        EPS = 1e-05

        def layernorm(x, g):
            mean = jnp.mean(x, axis=-1, keepdims=True)
            var = jnp.var(x, axis=-1, keepdims=True)
            return (x - mean) * jax.lax.rsqrt(var + EPS) * g
        b, n, _ = x.shape
        scale = DH ** (-0.5)
        xn = layernorm(x, g_in)
        q = (xn @ Wq).reshape(b, n, H, DH).transpose(0, 2, 1, 3) * scale
        kv = xn @ Wkv
        k, v = (kv[..., :DH], kv[..., DH:])
        nk = jnp.broadcast_to(null_kv[0], (b, 1, DH))
        nv = jnp.broadcast_to(null_kv[1], (b, 1, DH))
        k = jnp.concatenate([nk, k], axis=1)
        v = jnp.concatenate([nv, v], axis=1)
        sim = jnp.einsum('bhid,bjd->bhij', q, k)
        null_col = jnp.broadcast_to(null_attn_bias[:, None, None], (H, n, 1))
        bias = jnp.concatenate([null_col, attn_bias], axis=-1)
        sim = sim + bias
        neg = -jnp.finfo(sim.dtype).max
        j = n + 1
        causal_mask = jnp.triu(jnp.ones((n, j), dtype=bool), k=j - n + 1)
        sim = jnp.where(causal_mask, neg, sim)
        mask_p = jnp.pad(mask, ((0, 0), (1, 0)), constant_values=True)
        sim = jnp.where(mask_p[:, None, None, :], sim, neg)
        attn = jax.nn.softmax(sim, axis=-1)
        out = jnp.einsum('bhij,bjd->bhid', attn, v)
        out = out.transpose(0, 2, 1, 3).reshape(b, n, INNER)
        out = out @ Wo
        return layernorm(out, g_out)

    def _L0_ffn_ref(x, router_W, router_b, sW1, sb1, sW2, sb2, eW1, eb1, eW2, eb2):
        import jax, jax.numpy as jnp
        import numpy as np
        B, L, D = (2, 256, 128)
        E = 15
        H = D * 1
        K = 3
        T = 1.0
        b, l, d = x.shape
        n = b * l
        xt = x.reshape(n, d)
        shared = jax.nn.relu(xt @ sW1 + sb1) @ sW2 + sb2
        logits = xt @ router_W + router_b
        probs = jax.nn.softmax(logits / T, axis=-1)
        top_p, top_i = jax.lax.top_k(probs, K)
        cw = jnp.zeros((n, E), dtype=probs.dtype)
        cw = cw.at[jnp.arange(n)[:, None], top_i].set(top_p)
        h = jax.nn.relu(jnp.einsum('nd,edh->neh', xt, eW1) + eb1)
        ye = jnp.einsum('neh,ehd->ned', h, eW2) + eb2
        routed = jnp.einsum('ned,ne->nd', ye, cw)
        return (shared + routed).reshape(b, l, d)
    x = x + _L0_attn_ref(_L0_cond_ref(x, cond_64, L0_cond_wt, L0_cond_wg, L0_cond_w_gate, L0_cond_w_up, L0_cond_w_down, L0_cond_sw_gate, L0_cond_sw_up, L0_cond_sw_down), L0_attn_ln_g, L0_attn_ln_b, L0_attn_in_proj_w, L0_attn_conv_w, L0_attn_conv_b, L0_attn_x_proj_w, L0_attn_dt_proj_w, L0_attn_dt_proj_b, L0_attn_A_log, L0_attn_D, L0_attn_out_proj_w)
    x = x + _L0_ffn_ref(_L0_cond2_ref(x, fside_16xSxS_0, mask_BxS_bk0, L0_cond2_g_in, L0_cond2_null_attn_bias, cond_64, L0_cond2_Wq, L0_cond2_Wkv, L0_cond2_Wo, L0_cond2_g_out), L0_ffn_router_W, L0_ffn_router_b, L0_ffn_sW1, L0_ffn_sb1, L0_ffn_sW2, L0_ffn_sb2, L0_ffn_eW1, L0_ffn_eb1, L0_ffn_eW2, L0_ffn_eb2)
    return x

_drawn_inputs = setup_inputs


def setup_inputs(seed=0):
    import zlib

    import numpy as np

    out = dict(_drawn_inputs(seed))
    spreads = {'L0_attn_ln_g': (1.0, 0.2),
     'L0_attn_ln_b': (0.0, 0.1),
     'L0_attn_D': (1.0, 0.2),
     'L0_cond2_g_in': (1.0, 0.6),
     'L0_cond2_g_out': (1.0, 0.6),
     'L0_ffn_router_b': (0.0, 0.8),
     'L0_ffn_sb1': (0.0, 0.613),
     'L0_ffn_sb2': (0.0, 0.1),
     'L0_ffn_eb1': (0.0, 0.8),
     'L0_ffn_eb2': (0.0, 0.525)}
    factors = {'fside_16xSxS_0': 8.0,
     'L0_cond2_null_attn_bias': 7.692,
     'L0_cond2_Wq': 8.0,
     'L0_cond2_Wkv': 8.0,
     'L0_ffn_router_W': 4.114,
     'L0_ffn_eW1': 8.0,
     'L0_ffn_eW2': 8.0}
    for name, (base, spread) in spreads.items():
        noise = np.random.default_rng([zlib.crc32(name.encode()), seed]).standard_normal(out[name].shape)
        drawn = base * np.exp(spread * noise) if base else spread * noise
        out[name] = jnp.asarray(drawn.astype(out[name].dtype))
    for name, factor in factors.items():
        out[name] = (out[name] * factor).astype(out[name].dtype)
    return out
```

```python
from contextlib import ExitStack

import concourse.bass as bass
from concourse import mybir

ALU = mybir.AluOpType
ACT = mybir.ActivationFunctionType
AX = mybir.AxisListType
F32 = mybir.dt.float32
BF16 = mybir.dt.bfloat16
U8 = mybir.dt.uint8


P = 128
GB = 4
T = GB * P
EPS = 1e-5
NEG = -1.0e30
TAPS = 4
NS = 16
NH, DH = 16, 64
EA, KA = 8, 2
ED, KD = 15, 3
DTR = 8
LEAK = 0.01
CLAMP = 30.0
SENT = -1.0


def head_at(pos):
    quad, j = divmod(pos, 4)
    return 8 * (quad // 2) + 2 * j + quad % 2


class Steps:

    def __init__(self, sem, names):
        self.sem, self.names, self.no, self.next = sem, names, {n: i for i, n in enumerate(names)}, 0
        assert len(self.no) == len(names)

    def done(self, name):
        assert self.names[self.next] == name, (self.names[self.next], name)
        self.next = (self.next + 1) % len(self.names)
        return self.sem, 1

    def at(self, name, g=0):
        return self.sem, g * len(self.names) + self.no[name] + 1


class WorkBanks:

    def __init__(self, uses, before=None):
        self.bank = {u: i % 3 for i, u in enumerate(uses)}
        assert len(self.bank) == len(uses)
        self.prev = {u: uses[i - 3] if i >= 3 else (before[i - 3] if before else None)
                     for i, u in enumerate(uses)}
        self.is_first = {u: i < 3 for i, u in enumerate(uses)}


SETUP_USES = ["s_conv0", "s_conv1", "s_res", "s_out", "s_xp", "s_dt", "s_small", "s_cond", "s_crow"]
MIX_USES = (["xT", "lgA", "cwA"]
            + [f"{w}{k}" for k in range(4) for w in ("gate", "up", "wide")] + ["gate4", "up4"]
            + ["moe", "xnT", "u0", "u1", "r0", "r1", "bc", "d0", "d1"])
ATT_USES = (["op", "xn2T"] + [f"q{k}" for k in range(8)] + ["k", "v"]
            + [f"{w}_{b}" for b in range(GB) for w in
               ["s0", "s1", "s2", "s3", "t0", "t1", "t2", "t3", "pv0", "pv1", "pv2", "o0", "o1", "wo"]])
FFN_USES = (["xfT", "lgD", "cwD", "z15"] + [f"{w}{e}" for e in range(ED) for w in ("z", "cw")] + ["fin"])
PV_HEADS = [(0, 6), (6, 11), (11, 16)]


def router_steps(k):
    return (["lg", "mx", "ls"] + [f"top{b}" for b in range(GB)] + ["cut"] + [f"rest{b}" for b in range(GB)]
            + ["sel", "z"] + (["d", "ds"] if k == KA else []) + ["ri", "cw", "hi", "r", "mid", "lo"])


def mixture_block_kernel(nc, A, out):
    x, cond_64, fside, mask = A["x"], A["cond_64"], A["fside_16xSxS_0"], A["mask_BxS_bk0"]
    NB = x.shape[0]
    NG = NB // GB
    assert x.shape[1] == P and x.shape[2] == P and NB % GB == 0

    with ExitStack() as ctx:
        def sb(name, shape, dt=F32):
            return ctx.enter_context(nc.sbuf_tensor(name, shape, dt))

        def sem(name):
            return ctx.enter_context(nc.semaphore(name))

        work = [ctx.enter_context(nc.psum_tensor(f"work{i}", [P, 512], F32)) for i in range(3)]
        b_wide = ctx.enter_context(nc.psum_tensor("b_wide", [P, 512], F32))
        c_wide = ctx.enter_context(nc.psum_tensor("c_wide", [P, 512], F32))
        y_sum = [ctx.enter_context(nc.psum_tensor(f"y_sum{i}", [P, 512], F32)) for i in range(2)]
        ffn_sum = ctx.enter_context(nc.psum_tensor("ffn_sum", [P, 512], F32))

        ident = sb("ident", [P, P])
        ident_bf = sb("ident_bf", [P, P], BF16)
        ones_row = sb("ones_row", [1, P])
        ones_bf = sb("ones_bf", [P, P], BF16)
        eps_col = sb("eps_col", [P, 1])
        idn = sb("idn", [P, 64])
        sel_bc = sb("sel_bc", [96, 32], BF16)
        sel_a = sb("sel_a", [3 * EA, EA, 64], BF16)
        sel_d = sb("sel_d", [3 * ED, ED, P], BF16)
        w_gate = sb("w_gate", [P, EA, 64])
        w_up = sb("w_up", [P, EA, 64])
        w_down = sb("w_down", [P, 4, P])
        sw_gate = sb("sw_gate", [P, P])
        sw_up = sb("sw_up", [P, P])
        sw_down = sb("sw_down", [P, P])
        wt_n = sb("wt_n", [EA, P])
        wg_n = sb("wg_n", [EA, 64])
        cond_n = sb("cond_n", [NB, 64])
        wt_t = sb("wt_t", [P, EA])
        wg_t = sb("wg_t", [64, EA])
        cond_t = sb("cond_t", [64, NB])
        cond_logits = sb("cond_logits", [P, NB, EA])
        in_n = sb("in_n", [P, 4, P])
        conv_w = sb("conv_w", [P, 2, TAPS])
        conv_t = sb("conv_t", [P, TAPS, 2, P])
        res_t = sb("res_t", [P, 2, P])
        out_n = sb("out_n", [P, 2, P])
        out_t = sb("out_t", [P, 2, P])
        xp_n = sb("xp_n", [104, 2, P])
        xp_t = sb("xp_t", [P, 2, 104])
        dtw_n = sb("dtw_n", [P, 2, 104])
        dtw_t = sb("dtw_t", [104, 2, P])
        a_neg = sb("a_neg", [P, 2, NS])
        cols = sb("cols", [P, 12])
        conv_b, dt_b, d_skip = cols[:, 0:2], cols[:, 2:4], cols[:, 4:6]
        ln_g, ln_b, g_in, g_out, sb1, sb2 = (cols[:, i:i + 1] for i in range(6, 12))
        w_q = sb("w_q", [P, NH * DH])
        w_k2 = sb("w_k2", [P, 2, DH])
        w_vn = sb("w_vn", [P, DH + NH])
        null_k = sb("null_k", [P, DH])
        null_sum = sb("null_sum", [P, NH])
        null_v = sb("null_v", [P, 1])
        vn_row = sb("vn_row", [1, DH + NH])
        w_o = sb("w_o", [P, 8, P])
        o_row = sb("o_row", [1, P])
        bias = sb("bias", [P, NH, P])
        mask_u8 = sb("mask_u8", [P, NB * P], U8)
        r_w = sb("r_w", [P, ED])
        r_b = sb("r_b", [1, ED])
        f_w1 = sb("f_w1", [P, ED, P])
        f_w2 = sb("f_w2", [P, ED, P])
        fs_w1 = sb("fs_w1", [P, P])
        fs_w2 = sb("fs_w2", [P, P])
        f_b1 = sb("f_b1", [P, ED])
        eb2_r = sb("eb2_r", [3 * ED, P])
        eb_rest = sb("eb_rest", [3 * ED, P])
        eb2_p = sb("eb2_p", [3 * ED, 3, P], BF16)

        x_n = sb("x_n", [P, GB, P])
        x_t = sb("x_t", [P, T])
        stats = sb("stats", [P, GB, 6])
        mv = sb("mv", [P, GB, 2])
        rstd = sb("rstd", [P, GB])
        lg = sb("lg", [P, GB, 16])
        gap = sb("gap", [P, 7])
        mx = sb("mx", [P, GB])
        zs = sb("zs", [P, GB])
        ds_ = sb("ds_", [P, GB])
        pr_a = sb("pr_a", [P, GB, 16])
        pr_d = sb("pr_d", [P, GB, 24])
        top8 = sb("top8", [P, GB, 8])
        rest = sb("rest", [P, GB, 24])
        cw = sb("cw", [P, GB, 16])
        cwr = sb("cwr", [P, GB, 16])
        cw3 = sb("cw3", [P, GB, P], BF16)
        cw3_t = sb("cw3_t", [3 * ED, T], BF16)
        gate_s = sb("gate_s", [P, 2, T])
        hid = sb("hid", [P, 5, T])
        y_n = sb("y_n", [P, GB, P])
        xn_n = sb("xn_n", [P, GB, P])
        xn_t = sb("xn_t", [P, GB, TAPS - 1 + P])
        u_c = sb("u_c", [P, 2, T])
        res_s = sb("res_s", [P, 2, T])
        bc3 = sb("bc3", [96, T], BF16)
        bc_r = sb("bc_r", [64, T])
        dt_s = sb("dt_s", [104, T])
        delta = sb("delta", [P, 2, T])
        du = sb("du", [P, 2, T])
        decay = sb("decay", [P, 2, 2 * T])
        chain = sb("chain", [P, 3, 2 * T])
        x2_n = sb("x2_n", [P, GB, P])
        x2n_t = sb("x2n_t", [P, T])
        q_t = sb("q_t", [P, 8, T])
        k_t = sb("k_t", [P, T])
        v_a = sb("v_a", [P, GB, DH + 1])
        s_null = sb("s_null", [P, GB, NH])
        key_mask = sb("key_mask", [P, T], BF16)
        sc = sb("sc", [P, 2, NH, P])
        smax = sb("smax", [P, 2, NH])
        p_null = sb("p_null", [P, 2, NH])
        p_t = sb("p_t", [P, NH, P])
        den = sb("den", [P, NH])
        o_n = sb("o_n", [P, NH, DH])
        o_t = sb("o_t", [P, 8, P])
        a_n = sb("a_n", [P, GB, P])
        xf_t = sb("xf_t", [P, T])
        ff_t = sb("ff_t", [P, T])
        conv_sc = chain[:, 0, :].rearrange("p (k h m) -> p k h m", k=TAPS, h=2)
        null_prod = chain[:, 1, :].rearrange("p (h d) -> p h d", h=NH)
        y_out = sb("y_out", [P, GB, P])

        loaded = sem("loaded")
        consts = sem("consts")
        x_loaded = sem("x_loaded")
        stored = sem("stored")

        act_set = Steps(sem("act_set"), ["a_exp", "ident_bf", "a_neg", "conv0", "conv1", "res", "out", "xp", "dt",
                                         "wt", "wg", "cond", "logits", "crow", "eb_hi", "eb_mid"])
        dve_set = Steps(sem("dve_set"), [f"conv{i}" for i in range(8)]
                        + ["idn0", "idn1", "sel_bc", "ida0", "ida1", "sel_a", "idd0", "idd1", "sel_d",
                           "null_p", "null_s"] + [f"wn{i}" for i in range(4)] + ["neg_v", "eb_r", "eb_lo"])
        pe_set = Steps(sem("pe_set"), list(SETUP_USES))
        pe_mix = Steps(sem("pe_mix"), list(MIX_USES))
        act_mix = Steps(sem("act_mix"), ["xT", "exp", "cw3"] + [f"gate{k}" for k in range(5)]
                        + ["y", "lnv", "rstd", "xnT", "u0", "u1", "r0", "r1", "bc_hi", "dt", "bc_mid",
                           "e0", "sp0", "e1", "sp1"])
        dve_mix = Steps(sem("dve_mix"), router_steps(KA)
                        + [f"{w}{k}" for k in range(4) for w in ("lk", "gu", "h")] + ["lk4", "h4"]
                        + [f"st{b}" for b in range(GB)] + [f"mv{b}" for b in range(GB)]
                        + [f"xn{b}" for b in range(GB)]
                        + ["bc_r", "bc_lo", "cl0", "cl1", "de0", "de1", "du"])
        pe_scan = Steps(sem("pe_scan"), [w for s in range(NS) for w in
                                         ([f"b{s}", f"c{s}"] + ([f"y{s - 1}"] if s else []))] + [f"y{NS - 1}"])
        act_scan = Steps(sem("act_scan"), [f"decay{s}" for s in range(NS)])
        dve_scan = Steps(sem("dve_scan"), ["drive0"] + [w for s in range(NS) for w in
                                                        ([f"state{s}"] + ([f"drive{s + 1}"] if s + 1 < NS else [])
                                                         + [f"read{s}"])] + ["yd0", "yd1", "yg"])
        pe_att = Steps(sem("pe_att"), list(ATT_USES))
        act_att = Steps(sem("act_att"), ["lnv", "rstd", "xnT"] + [f"q{k}" for k in range(8)] + ["k", "v", "null"]
                        + [f"{w}_{b}" for b in range(GB) for w in
                           ["p", "pn", "t0", "t1", "t2", "t3", "o0", "o1", "wo"]])
        dve_att = Steps(sem("dve_att"), ["x2a", "x2"] + [f"st{b}" for b in range(GB)] + [f"mv{b}" for b in range(GB)]
                        + [f"xn{b}" for b in range(GB)] + ["mask"]
                        + [f"{w}_{b}" for b in range(GB) for w in
                           ["s0", "s1", "s2", "s3", "mx", "mn"] + [f"{v}{i}" for i in range(3) for v in
                                                                   ("den", "rden", "on")]])
        pool_att = Steps(sem("pool_att"), [f"{w}_{b}" for b in range(GB) for w in ("null", "sub")])
        pe_ffn = Steps(sem("pe_ffn"), ["xfT", "lgD", "cwD", "z15"]
                       + [w for e in range(ED) for w in (f"z{e}", f"cw{e}", f"acc{e - 1}")] + ["acc14", "fin"])
        act_ffn = Steps(sem("act_ffn"), ["lnv", "rstd", "xfT", "exp", "cw3", "h15"] + [f"h{e}" for e in range(ED)]
                        + ["ff"])
        dve_ffn = Steps(sem("dve_ffn"), [f"st{b}" for b in range(GB)] + [f"mv{b}" for b in range(GB)]
                        + [f"xn{b}" for b in range(GB)] + router_steps(KD) + [f"c{e}" for e in range(ED)] + ["out"])

        released = {
            **{u: (act_set, n) for u, n in zip(SETUP_USES, ["conv0", "conv1", "res", "out", "xp", "dt", "cond",
                                                            "logits", "crow"])},
            "xT": (act_mix, "xT"), "lgA": (dve_mix, "lg"), "cwA": (act_mix, "cw3"),
            **{f"gate{k}": (dve_mix, f"lk{k}") for k in range(5)},
            **{f"up{k}": (dve_mix, f"gu{k}") for k in range(4)}, "up4": (dve_mix, "h4"),
            **{f"wide{k}": (dve_mix, f"h{k}") for k in range(4)},
            "moe": (act_mix, "y"), "xnT": (act_mix, "xnT"),
            **{u: (act_mix, u) for u in ("u0", "u1", "r0", "r1")},
            "bc": (dve_mix, "bc_r"), "d0": (dve_mix, "de0"), "d1": (dve_mix, "de1"),
            "op": (dve_att, "x2a"), "xn2T": (act_att, "xnT"), **{f"q{k}": (act_att, f"q{k}") for k in range(8)},
            "k": (act_att, "k"), "v": (act_att, "null"),
            **{f"{w}_{b}": (dve_att, f"{w}_{b}") for b in range(GB) for w in ("s0", "s1", "s2", "s3")},
            **{f"{w}_{b}": (act_att, f"{w}_{b}") for b in range(GB) for w in ("t0", "t1", "t2", "t3", "o0", "o1", "wo")},
            **{f"pv{i}_{b}": (dve_att, f"on{i}_{b}") for b in range(GB) for i in range(3)},
            "xfT": (act_ffn, "xfT"), "lgD": (dve_ffn, "lg"), "cwD": (act_ffn, "cw3"), "z15": (act_ffn, "h15"),
            **{f"z{e}": (act_ffn, f"h{e}") for e in range(ED)}, **{f"cw{e}": (dve_ffn, f"c{e}") for e in range(ED)},
            "fin": (dve_ffn, "out"),
        }
        group_uses = MIX_USES + ATT_USES + FFN_USES
        assert len(SETUP_USES) % 3 == 0
        set_banks = WorkBanks(SETUP_USES)
        banks = WorkBanks(group_uses, group_uses)

        block = ctx.enter_context(nc.Block())

        def row(ap):
            return ap.rearrange("(a n) -> a n", a=1)

        ip = A["L0_attn_in_proj_w"]
        xp = A["L0_attn_x_proj_w"]
        wkv = A["L0_cond2_Wkv"]
        wo = A["L0_cond2_Wo"]
        loads = [
            (in_n[:], ip.rearrange("(t p) f -> p t f", p=P)),
            (conv_w[:], A["L0_attn_conv_w"].rearrange("(h p) o k -> p h (o k)", p=P)),
            (w_gate[:], A["L0_cond_w_gate"].rearrange("e h m -> h e m")),
            (w_up[:], A["L0_cond_w_up"].rearrange("e h m -> h e m")),
            (w_down[:], A["L0_cond_w_down"].rearrange("e m h -> (e m) h").rearrange("(k p) h -> p k h", p=P)),
            (sw_gate[:], A["L0_cond_sw_gate"]),
            (sw_up[:], A["L0_cond_sw_up"]),
            (sw_down[:], A["L0_cond_sw_down"]),
            (wt_n[:], A["L0_cond_wt"]),
            (wg_n[:], A["L0_cond_wg"]),
            (cond_n[:], cond_64),
            (out_n[:], A["L0_attn_out_proj_w"].rearrange("e (h p) -> e h p", h=2)),
            (a_neg[:], A["L0_attn_A_log"].rearrange("(h p) s -> p h s", p=P)),
            (w_q[:], A["L0_cond2_Wq"]),
            (w_k2[:, 0, :], wkv[:, 0:DH]),
            (w_k2[:, 1, :], wkv[:, 0:DH]),
            (w_vn[:, 0:DH], wkv[:, DH:2 * DH]),
            (null_k[:], cond_64[0:1, :].to_broadcast([P, DH])),
            (null_v[0:DH, :], cond_64[1, :].rearrange("(p a) -> p a", a=1)),
            (null_v[DH:P, :], cond_64[1, :].rearrange("(p a) -> p a", a=1)),
            (vn_row[:, 0:DH], cond_64[1:2, :]),
            (mask_u8[:], mask.rearrange("(o b) s -> o (b s)", o=1).to_broadcast([P, NB * P])),
            (r_w[:], A["L0_ffn_router_W"]),
            (r_b[:], row(A["L0_ffn_router_b"])),
            (f_w1[:], A["L0_ffn_eW1"].rearrange("e d h -> d e h")),
            (f_w2[:], A["L0_ffn_eW2"].rearrange("e h d -> h e d")),
            (fs_w1[:], A["L0_ffn_sW1"]),
            (fs_w2[:], A["L0_ffn_sW2"]),
            (f_b1[:], A["L0_ffn_eb1"].rearrange("e h -> h e")),
        ]
        for i in range(3):
            loads.append((xp_n[32 * i:32 * i + 2 * NS, :, :], xp[DTR:DTR + 2 * NS, :].rearrange("r (h p) -> r h p", h=2)))
            loads.append((eb2_r[ED * i:ED * i + ED, :], A["L0_ffn_eb2"]))
        loads.append((xp_n[96:104, :, :], xp[0:DTR, :].rearrange("r (h p) -> r h p", h=2)))
        loads.append((dtw_n[:, :, 96:104], A["L0_attn_dt_proj_w"].rearrange("(h p) r -> p h r", p=P)))
        for i, name in ((0, "L0_attn_conv_b"), (2, "L0_attn_dt_proj_b"), (4, "L0_attn_D")):
            loads.append((cols[:, i:i + 2], A[name].rearrange("(h p) -> p h", p=P)))
        for i, name in ((6, "L0_attn_ln_g"), (7, "L0_attn_ln_b"), (8, "L0_cond2_g_in"), (9, "L0_cond2_g_out"),
                        (10, "L0_ffn_sb1"), (11, "L0_ffn_sb2")):
            loads.append((cols[:, i:i + 1], A[name].rearrange("(p a) -> p a", a=1)))
        for quad in range(4):
            h0 = head_at(4 * quad)
            loads.append((bias[:, 4 * quad:4 * quad + 4, :], fside[h0:h0 + 7:2, :, :].rearrange("h i j -> i h j")))
            loads.append((vn_row[:, DH + 4 * quad:DH + 4 * quad + 4], row(A["L0_cond2_null_attn_bias"])[:, h0:h0 + 7:2]))
        for pos in range(NH):
            h = head_at(pos)
            loads.append((w_o[DH * (pos % 2):DH * (pos % 2) + DH, pos // 2, :], wo[h * DH:(h + 1) * DH, :]))
        ALL_LOADED = 16 * len(loads)
        CONSTS = 13

        @block.sync
        def _(sp):
            with nc.allow_non_contiguous_dma(reason="vectors of a value a partition, once"):
                for dst, src in loads:
                    sp.dma_start(dst, src).then_inc(loaded, 16)

            def group(g, first):
                if not first:
                    sp.wait_ge(*dve_att.at("x2", g - 1))
                sp.dma_start(x_n[:], x[bass.ds(g * GB, GB), :, :].rearrange("b s d -> s b d")).then_inc(x_loaded, 16)
                sp.wait_ge(*dve_ffn.at("out", g))
                sp.dma_start(out[bass.ds(g * GB, GB), :, :].rearrange("b s d -> s b d"), y_out[:]).then_inc(stored, 16)

            group(0, True)
            with sp.Fori(1, NG) as g:
                group(g, False)
            sp.wait_ge(stored, 16 * NG)

        @block.gpsimd
        def _(pool):
            pool.memset(ident[:], 0.0).then_inc(consts, 1)
            for t, v in ((ones_row, 1.0), (ones_bf, 1.0), (eps_col, EPS), (pr_a, SENT), (pr_d, SENT),
                         (xn_t, 0.0), (cw3, 0.0), (v_a, 1.0), (decay, 0.0)):
                pool.memset(t[:], v).then_inc(consts, 1)
            pool.memset(dtw_n[:, :, 0:96], 0.0).then_inc(consts, 1)
            pool.wait_ge(consts, 1)
            pool.affine_select(out=ident[:], in_=ident[:], compare_op=ALU.not_equal, fill=1.0, base=0,
                               pattern=[[-1, P]], channel_multiplier=1).then_inc(consts, 1)
            pool.wait_ge(loaded, ALL_LOADED)
            pool.affine_select(out=bias[:], in_=bias[:], compare_op=ALU.is_ge, fill=NEG, base=0,
                               pattern=[[0, NH], [-1, P]], channel_multiplier=1).then_inc(consts, 1)

            def attention(g):
                for b in range(GB):
                    s = b % 2
                    pool.wait_ge(*dve_att.at(f"mn_{b}", g))
                    pool.tensor_tensor(p_null[:, s, :], s_null[:, b, :], smax[:, s, :],
                                       ALU.subtract).then_inc(*pool_att.done(f"null_{b}"))
                    pool.tensor_tensor(sc[:, s], sc[:, s], smax[:, s, :].unsqueeze(2).to_broadcast([P, NH, P]),
                                       ALU.subtract).then_inc(*pool_att.done(f"sub_{b}"))

            attention(0)
            with pool.Fori(1, NG) as g:
                attention(g)

        @block.scalar
        def _(act):
            copy = ACT.Copy
            act.preload_act_table_set("natural_log_exp_and_others")
            act.wait_ge(loaded, ALL_LOADED)
            act.wait_ge(consts, CONSTS)
            act.activation(a_neg[:], a_neg[:], ACT.Exp).then_inc(*act_set.done("a_exp"))
            act.activation(ident_bf[:], ident[:], copy).then_inc(*act_set.done("ident_bf"))
            act.wait_ge(*act_set.at("a_exp"))
            act.activation(a_neg[:], a_neg[:], copy, scale=-1.0).then_inc(*act_set.done("a_neg"))
            flat = conv_t[:].rearrange("p k h m -> p (k h m)")
            for use, step, dst, src in (
                    ("s_conv0", "conv0", flat[:, 0:512], work[set_banks.bank["s_conv0"]][:]),
                    ("s_conv1", "conv1", flat[:, 512:1024], work[set_banks.bank["s_conv1"]][:]),
                    ("s_res", "res", res_t[:].rearrange("p h m -> p (h m)"), work[set_banks.bank["s_res"]][:, 0:256]),
                    ("s_out", "out", out_t[:].rearrange("p h m -> p (h m)"), work[set_banks.bank["s_out"]][:, 0:256]),
                    ("s_xp", "xp", xp_t[:].rearrange("p h m -> p (h m)"), work[set_banks.bank["s_xp"]][:, 0:208]),
                    ("s_dt", "dt", dtw_t[96:104].rearrange("p h m -> p (h m)"),
                     work[set_banks.bank["s_dt"]][96:104, 0:256]),
                    ("s_small", "wt", wt_t[:], work[set_banks.bank["s_small"]][:, 0:EA]),
                    ("s_small", "wg", wg_t[:], work[set_banks.bank["s_small"]][0:64, 128:128 + EA]),
                    ("s_small", "cond", cond_t[:], work[set_banks.bank["s_small"]][0:64, 256:256 + NB]),
                    ("s_cond", "logits", cond_logits[:].rearrange("p b e -> p (b e)"),
                     work[set_banks.bank["s_cond"]][:, 0:NB * EA]),
                    ("s_crow", "crow", o_row[:], work[set_banks.bank["s_crow"]][0:1, 0:P])):
                act.wait_ge(*pe_set.at(use))
                act.activation(dst, src, copy).then_inc(*act_set.done(step))
            act.activation(eb2_p[:, 0, :], eb2_r[:], copy).then_inc(*act_set.done("eb_hi"))
            act.wait_ge(*dve_set.at("eb_r"))
            act.activation(eb2_p[:, 1, :], eb_rest[:], copy).then_inc(*act_set.done("eb_mid"))

            def out_of(use):
                return work[banks.bank[use]]

            def norm_scale(pe_none, dve, mine, g):
                act.wait_ge(*dve.at(f"mv{GB - 1}", g))
                act.activation(rstd[:], mv[:, :, 1], ACT.Ln, bias=eps_col[:]).then_inc(*mine.done("lnv"))
                act.wait_ge(*mine.at("lnv", g))
                act.activation(rstd[:], rstd[:], ACT.Exp, scale=-0.5).then_inc(*mine.done("rstd"))

            def mixture(g):
                act.wait_ge(*pe_mix.at("xT", g))
                act.activation(x_t[:], out_of("xT")[:], copy).then_inc(*act_mix.done("xT"))
                act.wait_ge(*dve_mix.at("ls", g))
                act.activation(pr_a[:, :, 0:EA], lg[:, :, 0:EA], ACT.Exp, scale=0.5).then_inc(*act_mix.done("exp"))
                act.wait_ge(*pe_mix.at("cwA", g))
                act.activation(cw3_t[0:3 * EA, :], out_of("cwA")[:].bitcast(BF16)[0:3 * EA, 0:T],
                               copy).then_inc(*act_mix.done("cw3"))
                for k in range(5):
                    act.wait_ge(*pe_mix.at(f"gate{k}", g))
                    if k >= 2:
                        act.wait_ge(*dve_mix.at(f"h{k - 2}", g))
                    act.activation(gate_s[:, k % 2, :], out_of(f"gate{k}")[:],
                                   copy).then_inc(*act_mix.done(f"gate{k}"))
                act.wait_ge(*pe_mix.at("moe", g))
                act.activation(y_n[:].rearrange("p b d -> p (b d)"), out_of("moe")[:],
                               copy).then_inc(*act_mix.done("y"))
                norm_scale(None, dve_mix, act_mix, g)
                act.wait_ge(*pe_mix.at("xnT", g))
                act.activation(xn_t[:, :, TAPS - 1:], out_of("xnT")[:].rearrange("p (b s) -> p b s", b=GB),
                               ACT.Identity, scale=ln_g, bias=ln_b).then_inc(*act_mix.done("xnT"))
                for h in range(2):
                    act.wait_ge(*pe_mix.at(f"u{h}", g))
                    act.activation(u_c[:, h, :], out_of(f"u{h}")[:], ACT.Silu,
                                   bias=conv_b[:, h:h + 1]).then_inc(*act_mix.done(f"u{h}"))
                for h in range(2):
                    act.wait_ge(*pe_mix.at(f"r{h}", g))
                    act.activation(res_s[:, h, :], out_of(f"r{h}")[:], ACT.Silu).then_inc(*act_mix.done(f"r{h}"))
                act.preload_act_table_set("natural_log_exp_and_others")
                act.wait_ge(*pe_mix.at("bc", g))
                act.activation(bc3[:], out_of("bc")[0:96, :], copy).then_inc(*act_mix.done("bc_hi"))
                act.activation(dt_s[96:104, :], out_of("bc")[96:104, :], copy).then_inc(*act_mix.done("dt"))
                act.wait_ge(*dve_mix.at("bc_r", g))
                act.activation(bc3[0:64, :], bc_r[:], copy).then_inc(*act_mix.done("bc_mid"))
                for h in range(2):
                    act.wait_ge(*dve_mix.at(f"cl{h}", g))
                    act.activation(delta[:, h, :], delta[:, h, :], ACT.Exp).then_inc(*act_mix.done(f"e{h}"))
                    act.wait_ge(*act_mix.at(f"e{h}", g))
                    act.activation(delta[:, h, :], delta[:, h, :], ACT.Ln, bias=1.0).then_inc(*act_mix.done(f"sp{h}"))

            def scan(g, first):
                act.wait_ge(*dve_mix.at("de1", g))
                for s in range(NS):
                    if s >= 2:
                        act.wait_ge(*dve_scan.at(f"state{s - 2}", g))
                    elif not first:
                        act.wait_ge(*dve_scan.at(f"state{NS - 2 + s}", g - 1))
                    for h in range(2):
                        view = decay[:, s % 2, h * T:(h + 1) * T].rearrange("p (b l) -> p b l", b=GB)
                        ins = act.activation(view[:, :, 1:], delta[:, h, :].rearrange("p (b l) -> p b l", b=GB)[:, :, 1:],
                                             ACT.Exp, scale=a_neg[:, h, s:s + 1])
                    ins.then_inc(*act_scan.done(f"decay{s}"))

            def attention(g):
                norm_scale(None, dve_att, act_att, g)
                act.wait_ge(*pe_att.at("xn2T", g))
                act.activation(x2n_t[:], out_of("xn2T")[:], copy, scale=g_in).then_inc(*act_att.done("xnT"))
                for k in range(8):
                    act.wait_ge(*pe_att.at(f"q{k}", g))
                    act.activation(q_t[:, k, :], out_of(f"q{k}")[:], copy,
                                   scale=DH ** -0.5).then_inc(*act_att.done(f"q{k}"))
                act.wait_ge(*pe_att.at("k", g))
                act.activation(k_t[:], out_of("k")[:], copy).then_inc(*act_att.done("k"))
                act.wait_ge(*pe_att.at("v", g))
                vn = out_of("v")[:, 0:GB * (DH + NH)].rearrange("p (b n) -> p b n", b=GB)
                act.activation(v_a[:, :, 0:DH], vn[:, :, 0:DH], copy).then_inc(*act_att.done("v"))
                act.activation(s_null[:], vn[:, :, DH:], copy).then_inc(*act_att.done("null"))
                for b in range(GB):
                    s = b % 2
                    act.wait_ge(*pool_att.at(f"sub_{b}", g))
                    act.activation(sc[:, s], sc[:, s], ACT.Exp).then_inc(*act_att.done(f"p_{b}"))
                    act.activation(p_null[:, s, :], p_null[:, s, :], ACT.Exp).then_inc(*act_att.done(f"pn_{b}"))
                    for i in range(4):
                        act.wait_ge(*pe_att.at(f"t{i}_{b}", g))
                        act.activation(p_t[:, 4 * i:4 * i + 4, :].rearrange("p h i -> p (h i)"),
                                       out_of(f"t{i}_{b}")[:], copy).then_inc(*act_att.done(f"t{i}_{b}"))
                    for i in range(2):
                        act.wait_ge(*pe_att.at(f"o{i}_{b}", g))
                        act.activation(o_t[:, 4 * i:4 * i + 4, :].rearrange("p k i -> p (k i)"),
                                       out_of(f"o{i}_{b}")[:], copy).then_inc(*act_att.done(f"o{i}_{b}"))
                    act.wait_ge(*pe_att.at(f"wo_{b}", g))
                    act.activation(a_n[:, b, :], out_of(f"wo_{b}")[:, 0:P], copy).then_inc(*act_att.done(f"wo_{b}"))

            def last_mixture(g):
                norm_scale(None, dve_ffn, act_ffn, g)
                act.wait_ge(*pe_ffn.at("xfT", g))
                act.activation(xf_t[:], out_of("xfT")[:], copy, scale=g_out).then_inc(*act_ffn.done("xfT"))
                act.wait_ge(*dve_ffn.at("ls", g))
                act.activation(pr_d[:, :, 0:ED], lg[:, :, 0:ED], ACT.Exp).then_inc(*act_ffn.done("exp"))
                act.wait_ge(*pe_ffn.at("cwD", g))
                act.activation(cw3_t[0:3 * ED, :], out_of("cwD")[:].bitcast(BF16)[0:3 * ED, 0:T],
                               copy).then_inc(*act_ffn.done("cw3"))
                act.wait_ge(*pe_ffn.at("z15", g))
                act.activation(hid[:, 4, :], out_of("z15")[:], ACT.Relu, bias=sb1).then_inc(*act_ffn.done("h15"))
                for e in range(ED):
                    act.wait_ge(*pe_ffn.at(f"z{e}", g))
                    if e >= 2:
                        act.wait_ge(*dve_ffn.at(f"c{e - 2}", g))
                    act.activation(hid[:, e % 2, :], out_of(f"z{e}")[:], ACT.Relu,
                                   bias=f_b1[:, e:e + 1]).then_inc(*act_ffn.done(f"h{e}"))
                act.wait_ge(*pe_ffn.at("acc14", g))
                act.activation(ff_t[:], ffn_sum[:], ACT.Identity, bias=sb2).then_inc(*act_ffn.done("ff"))

            def group(g, first):
                mixture(g)
                scan(g, first)
                attention(g)
                last_mixture(g)

            group(0, True)
            with act.Fori(1, NG) as g:
                group(g, False)

        @block.vector
        def _(dve):
            dve.wait_ge(loaded, ALL_LOADED)
            dve.wait_ge(consts, CONSTS)
            for i in range(8):
                k, h = divmod(i, 2)
                dve.tensor_scalar(conv_sc[:, k, h, :], in_n[:, h, :], conv_w[:, h, k:k + 1], None,
                                  ALU.mult).then_inc(*dve_set.done(f"conv{i}"))
            for tag, n, sel, width in (("n", 32, sel_bc, 0), ("a", EA, sel_a, 64), ("d", ED, sel_d, P)):
                dve.tensor_tensor(idn[0:3 * n, 0:n], ident[0:3 * n, 0:n], ident[0:3 * n, n:2 * n],
                                  ALU.add).then_inc(*dve_set.done(f"id{tag}0"))
                dve.wait_ge(*dve_set.at(f"id{tag}0"))
                dve.tensor_tensor(idn[0:3 * n, 32:32 + n], idn[0:3 * n, 0:n], ident[0:3 * n, 2 * n:3 * n],
                                  ALU.add).then_inc(*dve_set.done(f"id{tag}1"))
                dve.wait_ge(*dve_set.at(f"id{tag}1"))
                src = idn[0:3 * n, 32:32 + n]
                dve.tensor_copy(sel[:], src.unsqueeze(2).to_broadcast([3 * n, n, width]) if width else src
                                ).then_inc(*dve_set.done({"n": "sel_bc", "a": "sel_a", "d": "sel_d"}[tag]))
                dve.wait_ge(*dve_set.at({"n": "sel_bc", "a": "sel_a", "d": "sel_d"}[tag]))
            dve.tensor_tensor(null_prod, w_q[:].rearrange("p (h d) -> p h d", h=NH),
                              null_k[:].unsqueeze(1).to_broadcast([P, NH, DH]), ALU.mult).then_inc(*dve_set.done("null_p"))
            dve.wait_ge(*dve_set.at("null_p"))
            dve.tensor_reduce(null_sum[:], null_prod, AX.X, ALU.add).then_inc(*dve_set.done("null_s"))
            dve.wait_ge(*dve_set.at("null_s"))
            for quad in range(4):
                h0 = head_at(4 * quad)
                dve.tensor_scalar(w_vn[:, DH + 4 * quad:DH + 4 * quad + 4], null_sum[:, h0:h0 + 7:2], DH ** -0.5, None,
                                  ALU.mult).then_inc(*dve_set.done(f"wn{quad}"))
            dve.tensor_scalar(vn_row[:, 0:DH], vn_row[:, 0:DH], -1.0, None, ALU.mult).then_inc(*dve_set.done("neg_v"))
            dve.wait_ge(*act_set.at("eb_hi"))
            dve.tensor_tensor(eb_rest[:], eb2_r[:], eb2_p[:, 0, :], ALU.subtract).then_inc(*dve_set.done("eb_r"))
            dve.wait_ge(*act_set.at("eb_mid"))
            dve.tensor_tensor(eb2_p[:, 2, :], eb_rest[:], eb2_p[:, 1, :], ALU.subtract).then_inc(*dve_set.done("eb_lo"))

            def out_of(use):
                return work[banks.bank[use]]

            def norm(src, g, mine, act_steps, gaps):
                for b in range(GB):
                    dve.bn_stats(stats[:, b, :], src[:, b, :]).then_inc(*mine.done(f"st{b}"))
                dve.wait_ge(*mine.at(f"st{GB - 1}", g))
                dve.memset(gap[:, gaps:gaps + 1], 0.0)
                for b in range(GB):
                    dve.bn_aggr(mv[:, b, :], stats[:, b, :]).then_inc(*mine.done(f"mv{b}"))
                dve.wait_ge(*act_steps.at("rstd", g))
                for b in range(GB):
                    dve.tensor_scalar(xn_n[:, b, :], src[:, b, :], mv[:, b, 0:1], rstd[:, b:b + 1],
                                      ALU.subtract, ALU.mult).then_inc(*mine.done(f"xn{b}"))

            def router(g, E, K, pr, mine, act_steps, gaps):
                w = pr.shape[2]
                dve.wait_ge(*mine.at("lg", g))
                dve.tensor_reduce(mx[:], lg[:, :, 0:E], AX.X, ALU.max).then_inc(*mine.done("mx"))
                dve.wait_ge(*mine.at("mx", g))
                dve.tensor_tensor(lg[:, :, 0:E], lg[:, :, 0:E], mx[:].unsqueeze(2).to_broadcast([P, GB, E]),
                                  ALU.subtract).then_inc(*mine.done("ls"))
                dve.wait_ge(*act_steps.at("exp", g))
                dve.memset(gap[:, gaps:gaps + 1], 0.0)
                for b in range(GB):
                    dve.max(top8[:, b, :], pr[:, b, :]).then_inc(*mine.done(f"top{b}"))
                dve.wait_ge(*mine.at(f"top{GB - 1}", g))
                dve.memset(top8[:, :, K:8], SENT).then_inc(*mine.done("cut"))
                dve.wait_ge(*mine.at("cut", g))
                dve.memset(gap[:, gaps + 1:gaps + 2], 0.0)
                for b in range(GB):
                    dve.match_replace(rest[:, b, 0:w], top8[:, b, :], pr[:, b, :], 0.0).then_inc(*mine.done(f"rest{b}"))
                dve.wait_ge(*mine.at(f"rest{GB - 1}", g))
                dve.tensor_tensor(cw[:, :, 0:E], pr[:, :, 0:E], rest[:, :, 0:E], ALU.subtract).then_inc(*mine.done("sel"))
                dve.tensor_reduce(zs[:], pr[:, :, 0:E], AX.X, ALU.add).then_inc(*mine.done("z"))
                if K == KA:
                    dve.wait_ge(*mine.at("sel", g))
                    dve.tensor_reduce(ds_[:], cw[:, :, 0:E], AX.X, ALU.add).then_inc(*mine.done("d"))
                    dve.wait_ge(*mine.at("d", g))
                    dve.scalar_tensor_tensor(out=zs[:], in0=zs[:], scalar=1e-20, in1=ds_[:], op0=ALU.mult,
                                             op1=ALU.add).then_inc(*mine.done("ds"))
                dve.wait_ge(*mine.at("ds" if K == KA else "z", g))
                dve.reciprocal(zs[:], zs[:]).then_inc(*mine.done("ri"))
                dve.wait_ge(*mine.at("ri", g))
                dve.tensor_tensor(cw[:, :, 0:E], cw[:, :, 0:E], zs[:].unsqueeze(2).to_broadcast([P, GB, E]),
                                  ALU.mult).then_inc(*mine.done("cw"))
                dve.wait_ge(*mine.at("cw", g))
                dve.tensor_copy(cw3[:, :, 0:E], cw[:, :, 0:E]).then_inc(*mine.done("hi"))
                dve.wait_ge(*mine.at("hi", g))
                dve.tensor_tensor(cwr[:, :, 0:E], cw[:, :, 0:E], cw3[:, :, 0:E], ALU.subtract).then_inc(*mine.done("r"))
                dve.wait_ge(*mine.at("r", g))
                dve.tensor_copy(cw3[:, :, E:2 * E], cwr[:, :, 0:E]).then_inc(*mine.done("mid"))
                dve.wait_ge(*mine.at("mid", g))
                dve.tensor_tensor(cw3[:, :, 2 * E:3 * E], cwr[:, :, 0:E], cw3[:, :, E:2 * E],
                                  ALU.subtract).then_inc(*mine.done("lo"))

            def mixture(g):
                dve.wait_ge(*pe_mix.at("lgA", g))
                dve.tensor_tensor(lg[:, :, 0:EA], out_of("lgA")[:, 0:GB * EA].rearrange("p (b e) -> p b e", b=GB),
                                  cond_logits[:, bass.ds(g * GB, GB), :], ALU.add).then_inc(*dve_mix.done("lg"))
                router(g, EA, KA, pr_a, dve_mix, act_mix, 3)
                for k in range(5):
                    dve.wait_ge(*act_mix.at(f"gate{k}", g))
                    dve.scalar_tensor_tensor(out=gate_s[:, k % 2, :], in0=out_of(f"gate{k}")[:], scalar=LEAK,
                                             in1=gate_s[:, k % 2, :], op0=ALU.mult,
                                             op1=ALU.max).then_inc(*dve_mix.done(f"lk{k}"))
                    dve.wait_ge(*dve_mix.at(f"lk{k}", g))
                    dve.wait_ge(*pe_mix.at(f"up{k}", g))
                    dst = gate_s[:, k % 2, :] if k < 4 else hid[:, 4, :]
                    dve.tensor_tensor(dst, gate_s[:, k % 2, :], out_of(f"up{k}")[:],
                                      ALU.mult).then_inc(*dve_mix.done(f"gu{k}" if k < 4 else "h4"))
                    if k < 4:
                        dve.wait_ge(*dve_mix.at(f"gu{k}", g))
                        dve.wait_ge(*pe_mix.at(f"wide{k}", g))
                        dve.tensor_tensor(hid[:, k, :], gate_s[:, k % 2, :], out_of(f"wide{k}")[:],
                                          ALU.mult).then_inc(*dve_mix.done(f"h{k}"))
                dve.wait_ge(*act_mix.at("y", g))
                norm(y_n, g, dve_mix, act_mix, 0)
                dve.wait_ge(*act_mix.at("dt", g))
                dve.tensor_tensor(bc_r[:], out_of("bc")[0:64, :], bc3[0:64, :],
                                  ALU.subtract).then_inc(*dve_mix.done("bc_r"))
                dve.wait_ge(*act_mix.at("bc_mid", g))
                dve.tensor_tensor(bc3[0:32, :], bc_r[0:32, :], bc3[0:32, :],
                                  ALU.subtract).then_inc(*dve_mix.done("bc_lo"))
                for h in range(2):
                    dve.wait_ge(*pe_mix.at(f"d{h}", g))
                    dve.tensor_scalar(delta[:, h, :], out_of(f"d{h}")[:], dt_b[:, h:h + 1], CLAMP, ALU.add,
                                      ALU.min).then_inc(*dve_mix.done(f"cl{h}"))
                for h in range(2):
                    dve.wait_ge(*act_mix.at(f"sp{h}", g))
                    dve.scalar_tensor_tensor(out=delta[:, h, :], in0=out_of(f"d{h}")[:], scalar=dt_b[:, h:h + 1],
                                             in1=delta[:, h, :], op0=ALU.add, op1=ALU.max).then_inc(*dve_mix.done(f"de{h}"))
                dve.wait_ge(*dve_mix.at("de1", g))
                dve.tensor_tensor(du[:], delta[:], u_c[:], ALU.mult).then_inc(*dve_mix.done("du"))

            def scan(g, first):
                def drive_of(s):
                    dve.wait_ge(*pe_scan.at(f"b{s}", g))
                    if s >= 3:
                        dve.wait_ge(*pe_scan.at(f"y{s - 3}", g))
                    dve.tensor_tensor(chain[:, s % 3, :].rearrange("p (h t) -> p h t", h=2), du[:],
                                      b_wide[:].unsqueeze(1).to_broadcast([P, 2, T]),
                                      ALU.mult).then_inc(*dve_scan.done(f"drive{s}"))

                dve.wait_ge(*dve_mix.at("du", g))
                drive_of(0)
                for s in range(NS):
                    dve.wait_ge(*dve_scan.at(f"drive{s}", g))
                    dve.wait_ge(*act_scan.at(f"decay{s}", g))
                    dve.tensor_tensor_scan(chain[:, s % 3, :], decay[:, s % 2, :], chain[:, s % 3, :], 0.0,
                                           ALU.mult, ALU.add).then_inc(*dve_scan.done(f"state{s}"))
                    if s + 1 < NS:
                        drive_of(s + 1)
                    dve.wait_ge(*dve_scan.at(f"state{s}", g))
                    dve.wait_ge(*pe_scan.at(f"c{s}", g))
                    dve.tensor_tensor(chain[:, s % 3, :].rearrange("p (h t) -> p h t", h=2),
                                      chain[:, s % 3, :].rearrange("p (h t) -> p h t", h=2),
                                      c_wide[:].unsqueeze(1).to_broadcast([P, 2, T]),
                                      ALU.mult).then_inc(*dve_scan.done(f"read{s}"))
                dve.wait_ge(*pe_scan.at(f"y{NS - 1}", g))
                for h in range(2):
                    dve.scalar_tensor_tensor(out=u_c[:, h, :], in0=u_c[:, h, :], scalar=d_skip[:, h:h + 1],
                                             in1=y_sum[h][:], op0=ALU.mult, op1=ALU.add).then_inc(*dve_scan.done(f"yd{h}"))
                dve.wait_ge(*dve_scan.at("yd1", g))
                dve.tensor_tensor(u_c[:], u_c[:], res_s[:], ALU.mult).then_inc(*dve_scan.done("yg"))

            def attention(g):
                dve.wait_ge(*pe_att.at("op", g))
                dve.tensor_tensor(x2_n[:], out_of("op")[:].rearrange("p (b d) -> p b d", b=GB), y_n[:],
                                  ALU.add).then_inc(*dve_att.done("x2a"))
                dve.wait_ge(*dve_att.at("x2a", g))
                dve.wait_ge(x_loaded, 16 * (g + 1))
                dve.tensor_tensor(x2_n[:], x2_n[:], x_n[:], ALU.add).then_inc(*dve_att.done("x2"))
                dve.wait_ge(*dve_att.at("x2", g))
                norm(x2_n, g, dve_att, act_att, 1)
                dve.tensor_scalar(key_mask[:], mask_u8[:, bass.ds(g * T, T)], -1.0, -NEG, ALU.add,
                                  ALU.mult).then_inc(*dve_att.done("mask"))
                for b in range(GB):
                    s = b % 2
                    for i in range(4):
                        dve.wait_ge(*pe_att.at(f"s{i}_{b}", g))
                        dve.tensor_tensor(sc[:, s, 4 * i:4 * i + 4, :],
                                          out_of(f"s{i}_{b}")[:].rearrange("p (h j) -> p h j", h=4),
                                          bias[:, 4 * i:4 * i + 4, :], ALU.add).then_inc(*dve_att.done(f"s{i}_{b}"))
                    dve.wait_ge(*dve_att.at(f"s3_{b}", g))
                    dve.tensor_reduce(smax[:, s, :], sc[:, s], AX.X, ALU.max).then_inc(*dve_att.done(f"mx_{b}"))
                    dve.wait_ge(*dve_att.at(f"mx_{b}", g))
                    dve.wait_ge(*act_att.at("null", g))
                    dve.tensor_tensor(smax[:, s, :], smax[:, s, :], s_null[:, b, :],
                                      ALU.max).then_inc(*dve_att.done(f"mn_{b}"))
                    dve.wait_ge(*act_att.at(f"pn_{b}", g))
                    for i, (h0, h1) in enumerate(PV_HEADS):
                        n = h1 - h0
                        dve.wait_ge(*pe_att.at(f"pv{i}_{b}", g))
                        pv = out_of(f"pv{i}_{b}")[:, 0:n * (DH + 1)].rearrange("p (h d) -> p h d", h=n)
                        dve.tensor_tensor(den[:, h0:h1], pv[:, :, DH], p_null[:, s, h0:h1],
                                          ALU.add).then_inc(*dve_att.done(f"den{i}_{b}"))
                        dve.wait_ge(*dve_att.at(f"den{i}_{b}", g))
                        dve.reciprocal(den[:, h0:h1], den[:, h0:h1]).then_inc(*dve_att.done(f"rden{i}_{b}"))
                        dve.wait_ge(*dve_att.at(f"rden{i}_{b}", g))
                        dve.tensor_tensor(o_n[:, h0:h1, :], pv[:, :, 0:DH],
                                          den[:, h0:h1].unsqueeze(2).to_broadcast([P, n, DH]),
                                          ALU.mult).then_inc(*dve_att.done(f"on{i}_{b}"))

            def last_mixture(g, first):
                dve.wait_ge(*act_att.at(f"wo_{GB - 1}", g))
                norm(a_n, g, dve_ffn, act_ffn, 2)
                dve.wait_ge(*pe_ffn.at("lgD", g))
                dve.tensor_copy(lg[:, :, 0:ED],
                                out_of("lgD")[:, 0:GB * ED].rearrange("p (b e) -> p b e", b=GB)
                                ).then_inc(*dve_ffn.done("lg"))
                router(g, ED, KD, pr_d, dve_ffn, act_ffn, 5)
                for e in range(ED):
                    dve.wait_ge(*act_ffn.at(f"h{e}", g))
                    dve.wait_ge(*pe_ffn.at(f"cw{e}", g))
                    if e >= 2:
                        dve.wait_ge(*pe_ffn.at(f"acc{e - 2}", g))
                    dve.tensor_tensor(hid[:, 2 + e % 2, :], hid[:, e % 2, :], out_of(f"cw{e}")[:],
                                      ALU.mult).then_inc(*dve_ffn.done(f"c{e}"))
                dve.wait_ge(*pe_ffn.at("fin", g))
                if not first:
                    dve.wait_ge(stored, 16 * g)
                dve.tensor_tensor(y_out[:], out_of("fin")[:].rearrange("p (b d) -> p b d", b=GB), x2_n[:],
                                  ALU.add).then_inc(*dve_ffn.done("out"))

            def group(g, first):
                mixture(g)
                scan(g, first)
                attention(g)
                last_mixture(g, first)

            group(0, True)
            with dve.Fori(1, NG) as g:
                group(g, False)

        @block.tensor
        def _(pe):
            pe.wait_ge(loaded, ALL_LOADED)
            pe.wait_ge(consts, CONSTS)

            def set_claim(use):
                prev = set_banks.prev[use]
                if prev:
                    steps, name = released[prev]
                    pe.wait_ge(*steps.at(name))
                return work[set_banks.bank[use]]

            for i in range(2):
                o = set_claim(f"s_conv{i}")
                pe.wait_ge(*dve_set.at(f"conv{4 * i + 3}"))
                for j in range(4):
                    k, h = divmod(4 * i + j, 2)
                    ins = pe.transpose(o[:, j * P:(j + 1) * P], conv_sc[:, k, h, :], ident[:])
                ins.then_inc(*pe_set.done(f"s_conv{i}"))
            o = set_claim("s_res")
            for h in range(2):
                ins = pe.transpose(o[:, h * P:(h + 1) * P], in_n[:, 2 + h, :], ident[:])
            ins.then_inc(*pe_set.done("s_res"))
            o = set_claim("s_out")
            for h in range(2):
                ins = pe.transpose(o[:, h * P:(h + 1) * P], out_n[:, h, :], ident[:])
            ins.then_inc(*pe_set.done("s_out"))
            o = set_claim("s_xp")
            for h in range(2):
                ins = pe.transpose(o[:, h * 104:(h + 1) * 104], xp_n[:, h, :], ident[0:104, 0:104])
            ins.then_inc(*pe_set.done("s_xp"))
            o = set_claim("s_dt")
            for h in range(2):
                ins = pe.transpose(o[0:104, h * P:(h + 1) * P], dtw_n[:, h, :], ident[:])
            ins.then_inc(*pe_set.done("s_dt"))
            o = set_claim("s_small")
            pe.transpose(o[:, 0:EA], wt_n[:], ident[0:EA, 0:EA])
            pe.transpose(o[0:64, 128:128 + EA], wg_n[:], ident[0:EA, 0:EA])
            pe.transpose(o[0:64, 256:256 + NB], cond_n[:], ident[0:NB, 0:NB]).then_inc(*pe_set.done("s_small"))
            o = set_claim("s_cond")
            pe.wait_ge(*act_set.at("cond"))
            for b in range(NB):
                ins = pe.matmul(o[:, b * EA:(b + 1) * EA], cond_t[:, b:b + 1].to_broadcast([64, P]), wg_t[:],
                                start=True, stop=True)
            ins.then_inc(*pe_set.done("s_cond"))
            o = set_claim("s_crow")
            for k in range(8):
                ins = pe.matmul(o[0:1, 0:P], null_v[:], w_o[:, k, :], start=(k == 0), stop=(k == 7))
            ins.then_inc(*pe_set.done("s_crow"))
            pe.wait_ge(*act_set.at("eb_mid"))
            pe.wait_ge(*dve_set.at("eb_lo"))

            def claim(use, g, first):
                steps, name = released[banks.prev[use]]
                if not banks.is_first[use]:
                    pe.wait_ge(*steps.at(name, g))
                elif not first:
                    pe.wait_ge(*steps.at(name, g - 1))
                return work[banks.bank[use]]

            def seq(t, b):
                return t[:, b * P:(b + 1) * P]

            def to_features(use, mine, src, g, first):
                o = claim(use, g, first)
                for b in range(GB):
                    ins = pe.transpose(seq(o, b), src[:, b, :], ident[:])
                ins.then_inc(*mine.done(use))

            def parts_to_rows(use, mine, n, g, first):
                o = claim(use, g, first)[:].bitcast(BF16)
                for b in range(GB):
                    ins = pe.transpose(o[:, b * P:(b + 1) * P], cw3[:, b, :], ident_bf[:])
                ins.then_inc(*mine.done(use))

            def product(use, mine, lhsT, rhs, g, first):
                o = claim(use, g, first)
                pe.matmul(o[:], lhsT, rhs, start=True, stop=True).then_inc(*mine.done(use))

            def mixture(g, first):
                pe.wait_ge(x_loaded, 16 * (g + 1))
                to_features("xT", pe_mix, x_n, g, first)
                o = claim("lgA", g, first)
                pe.wait_ge(*act_mix.at("xT", g))
                for b in range(GB):
                    ins = pe.matmul(o[:, b * EA:(b + 1) * EA], seq(x_t, b), wt_t[:], start=True, stop=True)
                ins.then_inc(*pe_mix.done("lgA"))
                pe.wait_ge(*dve_mix.at("lo", g))
                parts_to_rows("cwA", pe_mix, 3 * EA, g, first)
                for k in range(4):
                    pair = slice(2 * k, 2 * k + 2)
                    product(f"gate{k}", pe_mix, w_gate[:, pair, :].rearrange("p e m -> p (e m)"), x_t[:], g, first)
                    product(f"up{k}", pe_mix, w_up[:, pair, :].rearrange("p e m -> p (e m)"), x_t[:], g, first)
                    if k == 0:
                        pe.wait_ge(*act_mix.at("cw3", g))
                    product(f"wide{k}", pe_mix, sel_a[:, pair, :].rearrange("p e m -> p (e m)"), cw3_t[0:3 * EA, :],
                            g, first)
                product("gate4", pe_mix, sw_gate[:], x_t[:], g, first)
                product("up4", pe_mix, sw_up[:], x_t[:], g, first)
                o = claim("moe", g, first)
                pe.wait_ge(*dve_mix.at("h4", g))
                for b in range(GB):
                    for k in range(5):
                        ins = pe.matmul(seq(o, b), hid[:, k, b * P:(b + 1) * P], w_down[:, k, :] if k < 4 else sw_down[:],
                                        start=(k == 0), stop=(k == 4))
                ins.then_inc(*pe_mix.done("moe"))
                pe.wait_ge(*dve_mix.at(f"xn{GB - 1}", g))
                to_features("xnT", pe_mix, xn_n, g, first)
                pe.wait_ge(*act_mix.at("xnT", g))
                for h in range(2):
                    o = claim(f"u{h}", g, first)
                    for k in range(TAPS):
                        ins = pe.matmul(o[:].rearrange("p (b s) -> p b s", b=GB), conv_t[:, k, h, :],
                                        xn_t[:, :, k:k + P], start=(k == 0), stop=(k == TAPS - 1))
                    ins.then_inc(*pe_mix.done(f"u{h}"))
                for h in range(2):
                    o = claim(f"r{h}", g, first)
                    pe.matmul(o[:].rearrange("p (b s) -> p b s", b=GB), res_t[:, h, :], xn_t[:, :, TAPS - 1:],
                              start=True, stop=True).then_inc(*pe_mix.done(f"r{h}"))
                o = claim("bc", g, first)
                pe.wait_ge(*act_mix.at("u1", g))
                for h in range(2):
                    ins = pe.matmul(o[0:104, :], xp_t[:, h, :], u_c[:, h, :], start=(h == 0), stop=(h == 1))
                ins.then_inc(*pe_mix.done("bc"))
                for h in range(2):
                    o = claim(f"d{h}", g, first)
                    pe.wait_ge(*act_mix.at("dt", g))
                    pe.matmul(o[:], dtw_t[96:104, h, :], dt_s[96:104, :], start=True,
                              stop=True, tile_position=(96, 0)).then_inc(*pe_mix.done(f"d{h}"))

            def scan(g, first):
                def sum_state(s):
                    if s == 0 and not first:
                        pe.wait_ge(*dve_scan.at("yd1", g - 1))
                    pe.wait_ge(*dve_scan.at(f"read{s}", g))
                    for h in range(2):
                        ins = pe.matmul(y_sum[h][:], ident[:], chain[:, s % 3, h * T:(h + 1) * T],
                                        start=(s == 0), stop=(s == NS - 1))
                    ins.then_inc(*pe_scan.done(f"y{s}"))

                pe.wait_ge(*dve_mix.at("bc_lo", g))
                for s in range(NS):
                    if s:
                        pe.wait_ge(*dve_scan.at(f"drive{s - 1}", g))
                    elif not first:
                        pe.wait_ge(*dve_scan.at(f"drive{NS - 1}", g - 1))
                    pe.matmul(b_wide[:], sel_bc[:, s:s + 1].to_broadcast([96, P]), bc3[:], start=True, stop=True).then_inc(*pe_scan.done(f"b{s}"))
                    if s:
                        pe.wait_ge(*dve_scan.at(f"read{s - 1}", g))
                    elif not first:
                        pe.wait_ge(*dve_scan.at(f"read{NS - 1}", g - 1))
                    pe.matmul(c_wide[:], sel_bc[:, NS + s:NS + s + 1].to_broadcast([96, P]), bc3[:], start=True,
                              stop=True).then_inc(*pe_scan.done(f"c{s}"))
                    if s:
                        sum_state(s - 1)
                sum_state(NS - 1)

            def attention(g, first):
                o = claim("op", g, first)
                pe.wait_ge(*dve_scan.at("yg", g))
                for b in range(GB):
                    for h in range(2):
                        ins = pe.matmul(seq(o, b), u_c[:, h, b * P:(b + 1) * P], out_t[:, h, :],
                                        start=(h == 0), stop=(h == 1))
                ins.then_inc(*pe_att.done("op"))
                pe.wait_ge(*dve_att.at(f"xn{GB - 1}", g))
                to_features("xn2T", pe_att, xn_n, g, first)
                pe.wait_ge(*act_att.at("xnT", g))
                for k in range(8):
                    product(f"q{k}", pe_att, w_q[:, k * P:(k + 1) * P], x2n_t[:], g, first)
                product("k", pe_att, w_k2[:].rearrange("p a d -> p (a d)"), x2n_t[:], g, first)
                o = claim("v", g, first)
                n = DH + NH
                for b in range(GB):
                    pe.matmul(o[:, b * n:(b + 1) * n], seq(x2n_t, b), w_vn[:], start=True, stop=False)
                    ins = pe.matmul(o[:, b * n:(b + 1) * n], ones_row[:], vn_row[:], start=False, stop=True)
                ins.then_inc(*pe_att.done("v"))
                pe.wait_ge(*dve_att.at("mask", g))
                for b in range(GB):
                    s = b % 2
                    tok = slice(b * P, (b + 1) * P)
                    for i in range(4):
                        o = claim(f"s{i}_{b}", g, first)
                        if b == 0 and i == 0:
                            pe.wait_ge(*act_att.at("k", g))
                        r = 64 * (i % 2)
                        pe.matmul(o[:].rearrange("p (h j) -> p h j", h=4), ones_bf[r:r + 1, :],
                                  key_mask[r:r + 1, tok].unsqueeze(1).to_broadcast([1, 4, P]), start=True, stop=False)
                        for j in range(4):
                            ins = pe.matmul(o[:, j * P:(j + 1) * P], q_t[r:r + 64, head_at(4 * i + j) // 2, tok],
                                            k_t[r:r + 64, tok], start=False, stop=(j == 3))
                        ins.then_inc(*pe_att.done(f"s{i}_{b}"))
                    pe.wait_ge(*act_att.at(f"p_{b}", g))
                    for i in range(4):
                        o = claim(f"t{i}_{b}", g, first)
                        for j in range(4):
                            ins = pe.transpose(seq(o, j), sc[:, s, 4 * i + j, :], ident[:])
                        ins.then_inc(*pe_att.done(f"t{i}_{b}"))
                    for i, (h0, h1) in enumerate(PV_HEADS):
                        o = claim(f"pv{i}_{b}", g, first)
                        pe.wait_ge(*act_att.at(f"t{(h1 - 1) // 4}_{b}", g))
                        for h in range(h0, h1):
                            ins = pe.matmul(o[:, (h - h0) * (DH + 1):(h - h0 + 1) * (DH + 1)], p_t[:, h, :],
                                            v_a[:, b, :], start=True, stop=True)
                        ins.then_inc(*pe_att.done(f"pv{i}_{b}"))
                    for i in range(2):
                        o = claim(f"o{i}_{b}", g, first)
                        pe.wait_ge(*dve_att.at(f"on{i + 1}_{b}", g))
                        for j in range(4):
                            k = 4 * i + j
                            ins = pe.transpose(seq(o, j), o_n[:, 2 * k:2 * k + 2, :].rearrange("p h d -> p (h d)"),
                                               ident[:])
                        ins.then_inc(*pe_att.done(f"o{i}_{b}"))
                    o = claim(f"wo_{b}", g, first)
                    pe.wait_ge(*act_att.at(f"o1_{b}", g))
                    for k in range(8):
                        pe.matmul(o[:, 0:P], o_t[:, k, :], w_o[:, k, :], start=(k == 0), stop=False)
                    pe.matmul(o[:, 0:P], ones_row[:], o_row[:], start=False, stop=True).then_inc(*pe_att.done(f"wo_{b}"))

            def last_mixture(g, first):
                pe.wait_ge(*dve_ffn.at(f"xn{GB - 1}", g))
                to_features("xfT", pe_ffn, xn_n, g, first)
                o = claim("lgD", g, first)
                pe.wait_ge(*act_ffn.at("xfT", g))
                for b in range(GB):
                    pe.matmul(o[:, b * ED:(b + 1) * ED], seq(xf_t, b), r_w[:], start=True, stop=False)
                    ins = pe.matmul(o[:, b * ED:(b + 1) * ED], ones_row[:], r_b[:], start=False, stop=True)
                ins.then_inc(*pe_ffn.done("lgD"))
                pe.wait_ge(*dve_ffn.at("lo", g))
                parts_to_rows("cwD", pe_ffn, 3 * ED, g, first)
                product("z15", pe_ffn, fs_w1[:], xf_t[:], g, first)

                def accumulate(e):
                    if e < 0:
                        if not first:
                            pe.wait_ge(*act_ffn.at("ff", g - 1))
                        for part in range(3):
                            pe.matmul(ffn_sum[:], eb2_p[:, part, :], cw3_t[:], start=(part == 0), stop=False)
                        pe.wait_ge(*act_ffn.at("h15", g))
                        ins = pe.matmul(ffn_sum[:], fs_w2[:], hid[:, 4, :], start=False, stop=False)
                    else:
                        pe.wait_ge(*dve_ffn.at(f"c{e}", g))
                        ins = pe.matmul(ffn_sum[:], f_w2[:, e, :], hid[:, 2 + e % 2, :], start=False, stop=(e == ED - 1))
                    ins.then_inc(*pe_ffn.done(f"acc{e}"))

                pe.wait_ge(*act_ffn.at("cw3", g))
                for e in range(ED):
                    product(f"z{e}", pe_ffn, f_w1[:, e, :], xf_t[:], g, first)
                    product(f"cw{e}", pe_ffn, sel_d[:, e, :], cw3_t[:], g, first)
                    accumulate(e - 1)
                accumulate(ED - 1)
                o = claim("fin", g, first)
                pe.wait_ge(*act_ffn.at("ff", g))
                for b in range(GB):
                    ins = pe.transpose(seq(o, b), seq(ff_t, b), ident[:])
                ins.then_inc(*pe_ffn.done("fin"))

            def group(g, first):
                mixture(g, first)
                scan(g, first)
                attention(g, first)
                last_mixture(g, first)

            group(0, True)
            with pe.Fori(1, NG) as g:
                group(g, False)


def kernel(**inputs):
    import numpy as _np
    import concourse.bacc as _bacc
    from concourse import mybir as _mybir
    from concourse.bass_utils import run_bass_kernel_spmd as _run

    nc = _bacc.Bacc("TRN2", target_bir_lowering=False, num_devices=1)
    arrays, args = {}, {}
    for name, value in inputs.items():
        a = _np.ascontiguousarray(value)
        arrays[f"in_{name}_dram"] = a
        args[name] = nc.dram_tensor(f"in_{name}_dram", a.shape, _mybir.dt.from_np(a.dtype), kind="ExternalInput").ap()
    shape = inputs["x"].shape
    out = nc.dram_tensor("out_0_dram", shape, _mybir.dt.from_np(_np.dtype("float32")), kind="ExternalOutput").ap()
    mixture_block_kernel(nc, args, out)
    r = _run(nc, [arrays], core_ids=[0])
    return r.results[0]["out_0_dram"]
```

```python
from contextlib import ExitStack

import concourse.bass as bass
from concourse import mybir

ALU = mybir.AluOpType
ACT = mybir.ActivationFunctionType
AX = mybir.AxisListType
F32 = mybir.dt.float32
BF16 = mybir.dt.bfloat16
U8 = mybir.dt.uint8


P = 128
GB = 4
T = GB * P
EPS = 1e-5
NEG = -1.0e30
TAPS = 4
NS = 16
NH, DH = 16, 64
EA, KA = 8, 2
ED, KD = 15, 3
DTR = 8
LEAK = 0.01
CLAMP = 30.0
SENT = -1.0


def head_at(pos):
    quad, j = divmod(pos, 4)
    return 8 * (quad // 2) + 2 * j + quad % 2


class Steps:

    def __init__(self, sem, names):
        self.sem, self.names, self.no, self.next = sem, names, {n: i for i, n in enumerate(names)}, 0
        assert len(self.no) == len(names)

    def done(self, name):
        assert self.names[self.next] == name, (self.names[self.next], name)
        self.next = (self.next + 1) % len(self.names)
        return self.sem, 1

    def at(self, name, g=0):
        return self.sem, g * len(self.names) + self.no[name] + 1


class WorkBanks:

    def __init__(self, uses, before=()):
        n = len(uses)
        assert len(set(uses)) == n and n >= 3
        self.last = uses[-3:]
        self.bank = {u: (i - n) % 3 for i, u in enumerate(uses)}
        self.prev = {}
        holder = {i: (u, True) for i, u in enumerate(before)}
        for u in uses:
            self.prev[u] = holder.get(self.bank[u])
            holder[self.bank[u]] = (u, False)


SHIFT = {"mix": 3, "pre": 2, "scan": 2, "att": 1, "ffn": 0}
STAGES = ("mix", "pre", "scan", "att", "ffn")

SLOTS = [
    [("ffn", "acc-1"), ("ffn", "e0"), ("att", "q3"), ("att", "q4"), ("mix", "router")],
    [("ffn", "e1"), ("att", "q5"), ("att", "q6"), ("mix", "cwA")],
    [("ffn", "e2"), ("att", "q7"), ("att", "k"), ("att", "v")],
    [("ffn", "e3"), ("att", "S0")],
    [("ffn", "e4"), ("att", "S1"), ("att", "P0")],
    [("ffn", "e5"), ("att", "T0"), ("mix", "m0"), ("att", "V0")],
    [("ffn", "e6"), ("att", "S2"), ("att", "O0"), ("att", "P1")],
    [("ffn", "e7"), ("att", "T1"), ("att", "W0"), ("att", "V1")],
    [("ffn", "e8"), ("att", "S3"), ("att", "O1"), ("att", "P2")],
    [("ffn", "e9"), ("att", "T2"), ("att", "W1"), ("mix", "m1"), ("att", "V2")],
    [("ffn", "e10"), ("att", "P3"), ("att", "O2"), ("mix", "m2"), ("att", "W2")],
    [("ffn", "e11"), ("att", "T3"), ("mix", "m3"), ("att", "V3")],
    [("ffn", "e12"), ("att", "O3"), ("att", "W3")],
    [("ffn", "e13"), ("ffn", "e14")],
    [("ffn", "acc14"), ("mix", "m4"), ("ffn", "fin")],
    [("mix", "moe"), ("mix", "norm")],
]
assert len(SLOTS) == NS
SCHEDULE = [
    ("pre", "u0"), ("pre", "u1"), ("ffn", "keep"), ("ffn", "norm"), ("att", "op"), ("pre", "xy"), ("att", "norm"),
    ("pre", "su0"), ("pre", "su1"), ("pre", "r0"), ("pre", "r1"), ("ffn", "xfT"), ("pre", "bc"), ("att", "xn2T"),
    ("ffn", "lgD"), ("pre", "d"), ("att", "q0"), ("ffn", "router"), ("pre", "sp"), ("mix", "xT"), ("mix", "lgA"),
    ("att", "q1"), ("att", "q2"), ("ffn", "cwD"), ("ffn", "z15"), ("scan", "start"),
    *[item for s, others in enumerate(SLOTS) for item in [("scan", s), *others]],
    ("scan", "end"), ("mix", "xnT"),
]
PV_HEADS = [(0, 6), (6, 11), (11, 16)]


FFN_EXPERTS = [f"e{e}" for e in range(ED)]


def router_steps(k):
    return (["mx", "ls"] + [f"top{b}" for b in range(GB)] + ["cut"] + [f"rest{b}" for b in range(GB)]
            + ["sel", "z"] + (["d", "ds"] if k == KA else []) + ["ri", "cw", "hi", "r", "mid", "lo"])


NORM_V = [f"{w}{b}" for w in ("st", "mv", "xn") for b in range(GB)]
NORM_A = ["lnv", "rstd"]
PE_STEPS = {
    "mix": {"xT": ["xT"], "lgA": ["lgA"], "cwA": ["cwA"], **{f"m{k}": [f"gate{k}", f"up{k}", f"wide{k}"] for k in range(4)},
            "m4": ["gate4", "up4"], "moe": ["moe"], "xnT": ["xnT"]},
    "pre": {"u0": ["u0"], "u1": ["u1"], "r0": ["r0"], "r1": ["r1"], "bc": ["bc"], "d": ["d0", "d1"]},
    "scan": {"start": ["b0"], **{s: [f"c{s}"] + ([f"b{s + 1}"] if s + 1 < NS else []) + ([f"y{s - 1}"] if s else [])
                                 for s in range(NS)}, "end": [f"y{NS - 1}"]},
    "att": {"op": ["op"], "xn2T": ["xn2T"], **{f"q{k}": [f"q{k}"] for k in range(8)}, "k": ["k"], "v": ["v"],
            **{f"S{b}": [f"s{i}_{b}" for i in range(4)] for b in range(GB)},
            **{f"T{b}": [f"t{i}_{b}" for i in range(4)] for b in range(GB)},
            **{f"V{b}": [f"pv{i}_{b}" for i in range(3)] for b in range(GB)},
            **{f"O{b}": [f"o{i}_{b}" for i in range(2)] for b in range(GB)},
            **{f"W{b}": [f"wo_{b}"] for b in range(GB)}},
    "ffn": {"xfT": ["xfT"], "lgD": ["lgD"], "cwD": ["cwD"], "z15": ["z15"], "acc-1": ["acc-1"],
            **{f"e{e}": [f"z{e}", f"cw{e}"] + ([f"acc{e - 1}"] if e else []) for e in range(ED)},
            "acc14": ["acc14"], "fin": ["fin"]},
}
ACT_STEPS = {
    "mix": {"xT": ["xT"], "router": ["exp"], "cwA": ["cw3"], **{f"m{k}": [f"gate{k}"] for k in range(5)}, "moe": ["y"],
            "norm": NORM_A, "xnT": ["xnT"]},
    "pre": {"su0": ["u0"], "su1": ["u1"], "r0": ["r0"], "r1": ["r1"], "bc": ["bc_hi", "dt", "bc_mid"],
            "sp": ["e0", "sp0", "e1", "sp1"]},
    "scan": {"start": ["decay0"], **{s: [f"decay{s + 1}"] for s in range(NS - 1)}},
    "att": {"norm": NORM_A, "xn2T": ["xnT"], **{f"q{k}": [f"q{k}"] for k in range(8)}, "k": ["k"], "v": ["v", "null"],
            **{f"P{b}": [f"p_{b}", f"pn_{b}"] for b in range(GB)},
            **{f"T{b}": [f"t{i}_{b}" for i in range(4)] for b in range(GB)},
            **{f"O{b}": [f"o{i}_{b}" for i in range(2)] for b in range(GB)},
            **{f"W{b}": [f"wo_{b}"] for b in range(GB)}},
    "ffn": {"keep": ["keep"], "norm": NORM_A, "xfT": ["xfT"], "router": ["exp"], "cwD": ["cw3"], "z15": ["h15"],
            **{f"e{e}": [f"h{e}"] for e in range(ED)}, "fin": ["ff"]},
}
DVE_STEPS = {
    "mix": {"lgA": ["lg"], "router": router_steps(KA), **{f"m{k}": [f"lk{k}", f"gu{k}", f"h{k}"] for k in range(4)}, "m4": ["lk4", "h4"],
            "norm": NORM_V},
    "pre": {"bc": ["bc_r", "bc_lo"], "d": ["cl0", "cl1"], "sp": ["de0", "de1", "du"]},
    "scan": {"start": ["drive0"], **{s: [f"state{s}"] + ([f"drive{s + 1}"] if s + 1 < NS else []) + [f"read{s}"]
                                     for s in range(NS)}, "end": ["yd0", "yd1", "yg"]},
    "att": {"op": ["x2"], "norm": NORM_V, "v": ["mask"],
            **{f"S{b}": [f"s{i}_{b}" for i in range(4)] + [f"mx_{b}", f"mn_{b}"] for b in range(GB)},
            **{f"V{b}": [f"{v}{i}_{b}" for i in range(3) for v in ("den", "rden", "on")] for b in range(GB)}},
    "ffn": {"norm": NORM_V, "lgD": ["lg"], "router": router_steps(KD), **{f"e{e}": [f"c{e}"] for e in range(ED)}, "fin": ["out"]},
}
POOL_STEPS = {
    "pre": {"xy": ["xy"]},
    "att": {f"S{b}": [f"null_{b}", f"sub_{b}"] for b in range(GB)},
}
SETUP_USES = ["s_conv0", "s_conv1", "s_res", "s_out", "s_xp", "s_dt", "s_small", "s_cond", "s_crow"]


def first(g):
    return isinstance(g, int) and g == 0


def in_order(table, stage):
    return [step for st, item in SCHEDULE if st == stage for step in table[stage].get(item, [])]


def body_uses(stages):
    return [(st, u) for st, item in SCHEDULE if st in stages and st != "scan"
            for u in PE_STEPS[st].get(item, []) if not u.startswith("acc")]


def mixture_block_kernel(nc, A, out):
    x, cond_64, fside, mask = A["x"], A["cond_64"], A["fside_16xSxS_0"], A["mask_BxS_bk0"]
    NB = x.shape[0]
    NG = NB // GB
    assert x.shape[1] == P and x.shape[2] == P and NB % GB == 0

    with ExitStack() as ctx:
        def sb(name, shape, dt=F32):
            return ctx.enter_context(nc.sbuf_tensor(name, shape, dt))

        def sem(name):
            return ctx.enter_context(nc.semaphore(name))

        work = [ctx.enter_context(nc.psum_tensor(f"work{i}", [P, 512], F32)) for i in range(3)]
        b_wide = ctx.enter_context(nc.psum_tensor("b_wide", [P, 512], F32))
        c_wide = ctx.enter_context(nc.psum_tensor("c_wide", [P, 512], F32))
        y_sum = [ctx.enter_context(nc.psum_tensor(f"y_sum{i}", [P, 512], F32)) for i in range(2)]
        ffn_sum = ctx.enter_context(nc.psum_tensor("ffn_sum", [P, 512], F32))

        ident = sb("ident", [P, P])
        ident_bf = sb("ident_bf", [P, P], BF16)
        ones_row = sb("ones_row", [1, P])
        ones_bf = sb("ones_bf", [P, P], BF16)
        eps_col = sb("eps_col", [P, 1])
        sel_bc = sb("sel_bc", [96, 32], BF16)
        sel_a = sb("sel_a", [3 * EA, EA, 64], BF16)
        sel_d = sb("sel_d", [P, ED], BF16)
        w_gate = sb("w_gate", [P, EA, 64])
        w_up = sb("w_up", [P, EA, 64])
        w_down = sb("w_down", [P, 4, P])
        sw_gate = sb("sw_gate", [P, P])
        sw_up = sb("sw_up", [P, P])
        sw_down = sb("sw_down", [P, P])
        wt_n = sb("wt_n", [EA, P])
        wg_n = sb("wg_n", [EA, 64])
        cond_n = sb("cond_n", [NB, 64])
        wt_t = sb("wt_t", [P, EA])
        wg_t = sb("wg_t", [64, EA])
        cond_t = sb("cond_t", [64, NB])
        cond_logits = sb("cond_logits", [P, NB, EA])
        conv_w = sb("conv_w", [P, 2, TAPS])
        conv_t = sb("conv_t", [P, TAPS, 2, P])
        res_t = sb("res_t", [P, 2, P])
        out_t = sb("out_t", [P, 2, P])
        xp_t = sb("xp_t", [P, 2, 104])
        dtw_t = sb("dtw_t", [104, 2, P])
        a_neg = sb("a_neg", [P, 2, NS])
        cols = sb("cols", [P, 12])
        conv_b, dt_b, d_skip = cols[:, 0:2], cols[:, 2:4], cols[:, 4:6]
        ln_g, ln_b, g_in, g_out, sb1, sb2 = (cols[:, i:i + 1] for i in range(6, 12))
        w_q = sb("w_q", [P, NH * DH])
        w_k2 = sb("w_k2", [P, 2, DH])
        w_vn = sb("w_vn", [P, DH + NH])
        null_sum = sb("null_sum", [P, NH])
        null_v = sb("null_v", [P, 1])
        vn_row = sb("vn_row", [1, DH + NH])
        w_o = sb("w_o", [P, 8, P])
        o_row = sb("o_row", [1, P])
        bias = sb("bias", [P, NH, P])
        mask_u8 = sb("mask_u8", [P, T], U8)
        r_w = sb("r_w", [P, ED])
        r_b = sb("r_b", [1, ED])
        f_w1 = sb("f_w1", [P, ED, P])
        f_w2 = sb("f_w2", [P, ED, P])
        fs_w1 = sb("fs_w1", [P, P])
        fs_w2 = sb("fs_w2", [P, P])
        f_b1 = sb("f_b1", [P, ED])
        eb2_p = sb("eb2_p", [3 * ED, 3, P], BF16)

        x_n = sb("x_n", [P, GB, P])
        x_t = sb("x_t", [P, T])
        stats = {st: sb(f"stats_{st}", [P, GB, 6]) for st in ("mix", "att", "ffn")}
        mv = {st: sb(f"mv_{st}", [P, GB, 2]) for st in ("mix", "att", "ffn")}
        rstd = {st: sb(f"rstd_{st}", [P, GB]) for st in ("mix", "att", "ffn")}
        xn_n = {st: sb(f"xn_n_{st}", [P, GB, P]) for st in ("mix", "att", "ffn")}
        gap = sb("gap", [P, 7])
        both = ("mix", "ffn")
        lg = {st: sb(f"lg_{st}", [P, GB, 16]) for st in both}
        mx = {st: sb(f"mx_{st}", [P, GB]) for st in both}
        zs = {st: sb(f"zs_{st}", [P, GB]) for st in both}
        ds_ = sb("ds_", [P, GB])
        pr = {"mix": sb("pr_mix", [P, GB, 16]), "ffn": sb("pr_ffn", [P, GB, 24])}
        top8 = {st: sb(f"top8_{st}", [P, GB, 8]) for st in both}
        rest = {st: sb(f"rest_{st}", [P, GB, 24]) for st in both}
        cw = {st: sb(f"cw_{st}", [P, GB, 16]) for st in both}
        cwr = {st: sb(f"cwr_{st}", [P, GB, 16]) for st in both}
        cw3 = {st: sb(f"cw3_{st}", [P, GB, P], BF16) for st in both}
        cw3_t = {"mix": sb("cw3_t_mix", [3 * EA, T], BF16), "ffn": sb("cw3_t_ffn", [3 * ED, T], BF16)}
        gate_s = sb("gate_s", [P, 2, T])
        hid = sb("hid", [P, 5, T])
        y_n = sb("y_n", [P, GB, P])
        xy = sb("xy", [P, GB, P])
        xn_t = sb("xn_t", [P, GB, TAPS - 1 + P])
        u_c = sb("u_c", [P, 2, T])
        res_s = sb("res_s", [P, 2, T])
        bc3 = sb("bc3", [96, T], BF16)
        bc_dt = sb("bc_dt", [104, T])
        bc_r, dt_s = bc_dt[0:64, :], bc_dt[96:104, :]
        delta = sb("delta", [P, 2, T])
        du = sb("du", [P, 2, T])
        decay = sb("decay", [P, 2, 2 * T])
        chain = sb("chain", [P, 3, 2 * T])
        x2_n = sb("x2_n", [P, GB, P])
        x2_kept = sb("x2_kept", [P, GB, P])
        x2n_t = sb("x2n_t", [P, T])
        q_t = sb("q_t", [P, 8, T])
        k_t = sb("k_t", [P, T])
        v_a = sb("v_a", [P, GB, DH + 1])
        s_null = sb("s_null", [P, GB, NH])
        key_mask = sb("key_mask", [P, T], BF16)
        sc = sb("sc", [P, 2, NH, P])
        smax = sb("smax", [P, 2, NH])
        p_null = sb("p_null", [P, 2, NH])
        p_t = sb("p_t", [P, NH, P])
        den = sb("den", [P, NH])
        o_n = sb("o_n", [P, NH, DH])
        o_t = sb("o_t", [P, 8, P])
        a_n = sb("a_n", [P, GB, P])
        xf_t = sb("xf_t", [P, T])
        ff_t = sb("ff_t", [P, T])
        fh = sb("fh", [P, 4, T])
        idn = sc[:, 1, 0, :]
        eb2_r, eb_rest = sc[0:3 * ED, 1, 1, :], sc[0:3 * ED, 1, 2, :]
        null_k = sc[:, 1, 3, 0:DH]
        in_n = sc[:, 0, 0:4, :]
        out_n = sc[:, 0, 4:6, :]
        xp_n = sc[0:104, 0, 6:8, :]
        dtw_n = sc[:, 0, 8:10, 0:104]
        conv_sc = chain[:, 0, :].rearrange("p (k h m) -> p k h m", k=TAPS, h=2)
        null_prod = chain[:, 1, :].rearrange("p (h d) -> p h d", h=NH)
        y_out = sb("y_out", [P, GB, P])

        loaded = sem("loaded")
        consts = sem("consts")
        x_loaded = sem("x_loaded")
        mask_loaded = sem("mask_loaded")
        stored = sem("stored")

        act_set = Steps(sem("act_set"), ["a_exp", "ident_bf", "a_neg", "conv0", "conv1", "res", "out", "xp", "dt",
                                         "wt", "wg", "cond", "logits", "crow", "eb_hi", "eb_mid"])
        dve_set = Steps(sem("dve_set"), [f"conv{i}" for i in range(8)]
                        + ["idn0", "idn1", "sel_bc", "ida0", "ida1", "sel_a", "idd0", "idd1", "sel_d",
                           "null_p", "null_s"] + [f"wn{i}" for i in range(4)] + ["neg_v", "eb_r", "eb_lo"])
        pe_set = Steps(sem("pe_set"), list(SETUP_USES))
        pe_s, act_s, dve_s, pool_s = (
            {st: Steps(sem(f"{name}_{st}"), in_order(table, st)) for st in STAGES if st in table}
            for name, table in (("pe", PE_STEPS), ("act", ACT_STEPS), ("dve", DVE_STEPS), ("pool", POOL_STEPS)))
        pe_mix, pe_pre, pe_scan, pe_att, pe_ffn = (pe_s[st] for st in STAGES)
        act_mix, act_pre, act_scan, act_att, act_ffn = (act_s[st] for st in STAGES)
        dve_mix, dve_pre, dve_scan, dve_att, dve_ffn = (dve_s[st] for st in STAGES)
        pool_pre, pool_att = (pool_s[st] for st in ("pre", "att"))

        released = {
            **{u: (act_set, n) for u, n in zip(SETUP_USES, ["conv0", "conv1", "res", "out", "xp", "dt", "cond",
                                                            "logits", "crow"])},
            "xT": (act_mix, "xT"), "lgA": (dve_mix, "lg"), "cwA": (act_mix, "cw3"),
            **{f"gate{k}": (dve_mix, f"lk{k}") for k in range(5)},
            **{f"up{k}": (dve_mix, f"gu{k}") for k in range(4)}, "up4": (dve_mix, "h4"),
            **{f"wide{k}": (dve_mix, f"h{k}") for k in range(4)},
            "moe": (act_mix, "y"), "xnT": (act_mix, "xnT"),
            **{u: (act_pre, u) for u in ("u0", "u1", "r0", "r1")},
            "bc": (dve_pre, "bc_r"), "d0": (dve_pre, "de0"), "d1": (dve_pre, "de1"),
            "op": (dve_att, "x2"), "xn2T": (act_att, "xnT"), **{f"q{k}": (act_att, f"q{k}") for k in range(8)},
            "k": (act_att, "k"), "v": (act_att, "null"),
            **{f"{w}_{b}": (dve_att, f"{w}_{b}") for b in range(GB) for w in ("s0", "s1", "s2", "s3")},
            **{f"{w}_{b}": (act_att, f"{w}_{b}") for b in range(GB) for w in ("t0", "t1", "t2", "t3", "o0", "o1", "wo")},
            **{f"pv{i}_{b}": (dve_att, f"on{i}_{b}") for b in range(GB) for i in range(3)},
            "xfT": (act_ffn, "xfT"), "lgD": (dve_ffn, "lg"), "cwD": (act_ffn, "cw3"), "z15": (act_ffn, "h15"),
            **{f"z{e}": (act_ffn, f"h{e}") for e in range(ED)}, **{f"cw{e}": (dve_ffn, f"c{e}") for e in range(ED)},
            "fin": (dve_ffn, "out"),
        }
        set_banks = WorkBanks(SETUP_USES)

        def stages_of(i):
            return tuple(st for st in STAGES if 0 <= i + SHIFT[st] < NG)

        LOOP = (1, NG - 3)
        assert all(stages_of(i) == STAGES for i in range(*LOOP))
        banks_of = {}
        before = [("set", u) for u in set_banks.last]
        for i in [*range(-3, LOOP[0] + 1), *range(LOOP[1], NG)]:
            if i == LOOP[0]:
                assert before == body_uses(STAGES)[-3:] and len(body_uses(STAGES)) % 3 == 0
            banks_of[i] = WorkBanks(body_uses(stages_of(i)), before)
            before = banks_of[i].last

        def run_bodies(eng, body):
            for i in range(-3, LOOP[0]):
                body(i, banks_of[i], stages_of(i))
            with eng.Fori(*LOOP) as i:
                body(i, banks_of[LOOP[0]], STAGES)
            for i in range(LOOP[1], NG):
                body(i, banks_of[i], stages_of(i))

        block = ctx.enter_context(nc.Block())

        def row(ap):
            return ap.rearrange("(a n) -> a n", a=1)

        ip = A["L0_attn_in_proj_w"]
        xp = A["L0_attn_x_proj_w"]
        wkv = A["L0_cond2_Wkv"]
        wo = A["L0_cond2_Wo"]
        loads = [
            (in_n, ip.rearrange("(t p) f -> p t f", p=P)),
            (conv_w[:], A["L0_attn_conv_w"].rearrange("(h p) o k -> p h (o k)", p=P)),
            (w_gate[:], A["L0_cond_w_gate"].rearrange("e h m -> h e m")),
            (w_up[:], A["L0_cond_w_up"].rearrange("e h m -> h e m")),
            (w_down[:], A["L0_cond_w_down"].rearrange("e m h -> (e m) h").rearrange("(k p) h -> p k h", p=P)),
            (sw_gate[:], A["L0_cond_sw_gate"]),
            (sw_up[:], A["L0_cond_sw_up"]),
            (sw_down[:], A["L0_cond_sw_down"]),
            (wt_n[:], A["L0_cond_wt"]),
            (wg_n[:], A["L0_cond_wg"]),
            (cond_n[:], cond_64),
            (out_n, A["L0_attn_out_proj_w"].rearrange("e (h p) -> e h p", h=2)),
            (a_neg[:], A["L0_attn_A_log"].rearrange("(h p) s -> p h s", p=P)),
            (w_q[:], A["L0_cond2_Wq"]),
            (w_k2[:, 0, :], wkv[:, 0:DH]),
            (w_k2[:, 1, :], wkv[:, 0:DH]),
            (w_vn[:, 0:DH], wkv[:, DH:2 * DH]),
            (null_k, cond_64[0:1, :].to_broadcast([P, DH])),
            (null_v[0:DH, :], cond_64[1, :].rearrange("(p a) -> p a", a=1)),
            (null_v[DH:P, :], cond_64[1, :].rearrange("(p a) -> p a", a=1)),
            (vn_row[:, 0:DH], cond_64[1:2, :]),
            (r_w[:], A["L0_ffn_router_W"]),
            (r_b[:], row(A["L0_ffn_router_b"])),
            (f_w1[:], A["L0_ffn_eW1"].rearrange("e d h -> d e h")),
            (f_w2[:], A["L0_ffn_eW2"].rearrange("e h d -> h e d")),
            (fs_w1[:], A["L0_ffn_sW1"]),
            (fs_w2[:], A["L0_ffn_sW2"]),
            (f_b1[:], A["L0_ffn_eb1"].rearrange("e h -> h e")),
        ]
        for i in range(3):
            loads.append((xp_n[32 * i:32 * i + 2 * NS], xp[DTR:DTR + 2 * NS, :].rearrange("r (h p) -> r h p", h=2)))
            loads.append((eb2_r[ED * i:ED * i + ED, :], A["L0_ffn_eb2"]))
        loads.append((xp_n[96:104], xp[0:DTR, :].rearrange("r (h p) -> r h p", h=2)))
        loads.append((dtw_n[:, :, 96:104], A["L0_attn_dt_proj_w"].rearrange("(h p) r -> p h r", p=P)))
        for i, name in ((0, "L0_attn_conv_b"), (2, "L0_attn_dt_proj_b"), (4, "L0_attn_D")):
            loads.append((cols[:, i:i + 2], A[name].rearrange("(h p) -> p h", p=P)))
        for i, name in ((6, "L0_attn_ln_g"), (7, "L0_attn_ln_b"), (8, "L0_cond2_g_in"), (9, "L0_cond2_g_out"),
                        (10, "L0_ffn_sb1"), (11, "L0_ffn_sb2")):
            loads.append((cols[:, i:i + 1], A[name].rearrange("(p a) -> p a", a=1)))
        for quad in range(4):
            h0 = head_at(4 * quad)
            loads.append((bias[:, 4 * quad:4 * quad + 4, :], fside[h0:h0 + 7:2, :, :].rearrange("h i j -> i h j")))
            loads.append((vn_row[:, DH + 4 * quad:DH + 4 * quad + 4], row(A["L0_cond2_null_attn_bias"])[:, h0:h0 + 7:2]))
        for pos in range(NH):
            h = head_at(pos)
            loads.append((w_o[DH * (pos % 2):DH * (pos % 2) + DH, pos // 2, :], wo[h * DH:(h + 1) * DH, :]))
        ALL_LOADED = 16 * len(loads)
        CONSTS = 14

        @block.sync
        def _(sp):
            with nc.allow_non_contiguous_dma(reason="vectors of a value a partition, once"):
                for dst, src in loads:
                    sp.dma_start(dst, src).then_inc(loaded, 16)

            def body(i, banks, stages):
                if "att" in stages:
                    g = i + SHIFT["att"]
                    if not first(g):
                        sp.wait_ge(*dve_att.at("mask", g - 1))
                    sp.dma_start(mask_u8[:], mask[bass.ds(g * GB, GB), :].rearrange("(o b) s -> o (b s)", o=1)
                                 .to_broadcast([P, T])).then_inc(mask_loaded, 16)
                if "mix" in stages:
                    g = i + SHIFT["mix"]
                    if not first(g):
                        sp.wait_ge(*pool_pre.at("xy", g - 1))
                    sp.dma_start(x_n[:], x[bass.ds(g * GB, GB), :, :].rearrange("b s d -> s b d")
                                 ).then_inc(x_loaded, 16)
                if "ffn" in stages:
                    g = i + SHIFT["ffn"]
                    sp.wait_ge(*dve_ffn.at("out", g))
                    sp.dma_start(out[bass.ds(g * GB, GB), :, :].rearrange("b s d -> s b d"), y_out[:]
                                 ).then_inc(stored, 16)

            run_bodies(sp, body)
            sp.wait_ge(stored, 16 * NG)

        @block.gpsimd
        def _(pool):
            pool.memset(ident[:], 0.0).then_inc(consts, 1)
            for t, v in ((ones_row, 1.0), (ones_bf, 1.0), (eps_col, EPS), (pr["mix"], SENT), (pr["ffn"], SENT),
                         (xn_t, 0.0), (cw3["mix"], 0.0), (cw3["ffn"], 0.0), (v_a, 1.0), (decay, 0.0)):
                pool.memset(t[:], v).then_inc(consts, 1)
            pool.memset(dtw_n[:, :, 0:96], 0.0).then_inc(consts, 1)
            pool.wait_ge(consts, 1)
            pool.affine_select(out=ident[:], in_=ident[:], compare_op=ALU.not_equal, fill=1.0, base=0,
                               pattern=[[-1, P]], channel_multiplier=1).then_inc(consts, 1)
            pool.wait_ge(loaded, ALL_LOADED)
            pool.affine_select(out=bias[:], in_=bias[:], compare_op=ALU.is_ge, fill=NEG, base=0,
                               pattern=[[0, NH], [-1, P]], channel_multiplier=1).then_inc(consts, 1)

            def body(i, banks, stages):
                for stage, item in SCHEDULE:
                    if stage not in stages or item not in POOL_STEPS.get(stage, {}):
                        continue
                    g = i + SHIFT[stage]
                    if item == "xy":
                        if not first(g):
                            pool.wait_ge(*dve_att.at("x2", g - 1))
                        pool.wait_ge(*act_mix.at("y", g))
                        pool.wait_ge(x_loaded, 16 * (g + 1))
                        pool.tensor_tensor(xy[:], x_n[:], y_n[:], ALU.add).then_inc(*pool_pre.done("xy"))
                    else:
                        b = int(item[1:])
                        s = b % 2
                        pool.wait_ge(*dve_att.at(f"mn_{b}", g))
                        pool.tensor_tensor(p_null[:, s, :], s_null[:, b, :], smax[:, s, :],
                                           ALU.subtract).then_inc(*pool_att.done(f"null_{b}"))
                        pool.tensor_tensor(sc[:, s], sc[:, s], smax[:, s, :].unsqueeze(2).to_broadcast([P, NH, P]),
                                           ALU.subtract).then_inc(*pool_att.done(f"sub_{b}"))

            run_bodies(pool, body)

        @block.scalar
        def _(act):
            copy = ACT.Copy
            act.preload_act_table_set("natural_log_exp_and_others")
            act.wait_ge(loaded, ALL_LOADED)
            act.wait_ge(consts, CONSTS)
            act.activation(a_neg[:], a_neg[:], ACT.Exp).then_inc(*act_set.done("a_exp"))
            act.activation(ident_bf[:], ident[:], copy).then_inc(*act_set.done("ident_bf"))
            act.wait_ge(*act_set.at("a_exp"))
            act.activation(a_neg[:], a_neg[:], copy, scale=-1.0).then_inc(*act_set.done("a_neg"))
            flat = conv_t[:].rearrange("p k h m -> p (k h m)")
            for use, step, dst, src in (
                    ("s_conv0", "conv0", flat[:, 0:512], work[set_banks.bank["s_conv0"]][:]),
                    ("s_conv1", "conv1", flat[:, 512:1024], work[set_banks.bank["s_conv1"]][:]),
                    ("s_res", "res", res_t[:].rearrange("p h m -> p (h m)"), work[set_banks.bank["s_res"]][:, 0:256]),
                    ("s_out", "out", out_t[:].rearrange("p h m -> p (h m)"), work[set_banks.bank["s_out"]][:, 0:256]),
                    ("s_xp", "xp", xp_t[:].rearrange("p h m -> p (h m)"), work[set_banks.bank["s_xp"]][:, 0:208]),
                    ("s_dt", "dt", dtw_t[96:104].rearrange("p h m -> p (h m)"),
                     work[set_banks.bank["s_dt"]][96:104, 0:256]),
                    ("s_small", "wt", wt_t[:], work[set_banks.bank["s_small"]][:, 0:EA]),
                    ("s_small", "wg", wg_t[:], work[set_banks.bank["s_small"]][0:64, 128:128 + EA]),
                    ("s_small", "cond", cond_t[:], work[set_banks.bank["s_small"]][0:64, 256:256 + NB]),
                    ("s_cond", "logits", cond_logits[:].rearrange("p b e -> p (b e)"),
                     work[set_banks.bank["s_cond"]][:, 0:NB * EA]),
                    ("s_crow", "crow", o_row[:], work[set_banks.bank["s_crow"]][0:1, 0:P])):
                act.wait_ge(*pe_set.at(use))
                act.activation(dst, src, copy).then_inc(*act_set.done(step))
            act.activation(eb2_p[:, 0, :], eb2_r, copy).then_inc(*act_set.done("eb_hi"))
            act.wait_ge(*dve_set.at("eb_r"))
            act.activation(eb2_p[:, 1, :], eb_rest, copy).then_inc(*act_set.done("eb_mid"))

            def normalise(stage, g):
                dve, mine = dve_s[stage], act_s[stage]
                act.wait_ge(*dve.at(f"mv{GB - 1}", g))
                act.activation(rstd[stage][:], mv[stage][:, :, 1], ACT.Ln, bias=eps_col[:]).then_inc(*mine.done("lnv"))
                act.wait_ge(*mine.at("lnv", g))
                act.activation(rstd[stage][:], rstd[stage][:], ACT.Exp, scale=-0.5).then_inc(*mine.done("rstd"))

            def weights_t(stage, use, n, src, g):
                act.wait_ge(*pe_s[stage].at(use, g))
                act.activation(cw3_t[stage][:], src[:].bitcast(BF16)[0:n, 0:T], copy).then_inc(*act_s[stage].done("cw3"))

            def mix(item, g, out_of):
                if item == "xT":
                    act.wait_ge(*pe_mix.at("xT", g))
                    act.activation(x_t[:], out_of("xT")[:], copy).then_inc(*act_mix.done("xT"))
                elif item == "router":
                    act.wait_ge(*dve_mix.at("ls", g))
                    act.activation(pr["mix"][:, :, 0:EA], lg["mix"][:, :, 0:EA], ACT.Exp,
                                   scale=0.5).then_inc(*act_mix.done("exp"))
                elif item == "cwA":
                    weights_t("mix", "cwA", 3 * EA, out_of("cwA"), g)
                elif item in ("m0", "m1", "m2", "m3", "m4"):
                    k = int(item[1:])
                    act.wait_ge(*pe_mix.at(f"gate{k}", g))
                    if k >= 2:
                        act.wait_ge(*dve_mix.at(f"h{k - 2}", g))
                    act.activation(gate_s[:, k % 2, :], out_of(f"gate{k}")[:],
                                   copy).then_inc(*act_mix.done(f"gate{k}"))
                elif item == "moe":
                    act.wait_ge(*pe_mix.at("moe", g))
                    if not first(g):
                        act.wait_ge(*pool_pre.at("xy", g - 1))
                    act.activation(y_n[:].rearrange("p b d -> p (b d)"), out_of("moe")[:],
                                   copy).then_inc(*act_mix.done("y"))
                elif item == "norm":
                    normalise("mix", g)
                elif item == "xnT":
                    act.wait_ge(*pe_mix.at("xnT", g))
                    act.activation(xn_t[:, :, TAPS - 1:], out_of("xnT")[:].rearrange("p (b s) -> p b s", b=GB),
                                   ACT.Identity, scale=ln_g, bias=ln_b).then_inc(*act_mix.done("xnT"))

            def pre(item, g, out_of):
                if item in ("su0", "su1"):
                    h = int(item[2:])
                    act.wait_ge(*pe_pre.at(f"u{h}", g))
                    act.activation(u_c[:, h, :], out_of(f"u{h}")[:], ACT.Silu,
                                   bias=conv_b[:, h:h + 1]).then_inc(*act_pre.done(f"u{h}"))
                elif item in ("r0", "r1"):
                    h = int(item[1:])
                    act.wait_ge(*pe_pre.at(f"r{h}", g))
                    act.activation(res_s[:, h, :], out_of(f"r{h}")[:], ACT.Silu).then_inc(*act_pre.done(f"r{h}"))
                    if h == 1:
                        act.preload_act_table_set("natural_log_exp_and_others")
                elif item == "bc":
                    act.wait_ge(*pe_pre.at("bc", g))
                    act.activation(bc3[:], out_of("bc")[0:96, :], copy).then_inc(*act_pre.done("bc_hi"))
                    act.activation(dt_s, out_of("bc")[96:104, :], copy).then_inc(*act_pre.done("dt"))
                    act.wait_ge(*dve_pre.at("bc_r", g))
                    act.activation(bc3[0:64, :], bc_r, copy).then_inc(*act_pre.done("bc_mid"))
                elif item == "sp":
                    for h in range(2):
                        act.wait_ge(*dve_pre.at(f"cl{h}", g))
                        act.activation(delta[:, h, :], delta[:, h, :], ACT.Exp).then_inc(*act_pre.done(f"e{h}"))
                        act.wait_ge(*act_pre.at(f"e{h}", g))
                        act.activation(delta[:, h, :], delta[:, h, :], ACT.Ln, bias=1.0).then_inc(*act_pre.done(f"sp{h}"))

            def scan(item, g, out_of):
                if item == "end" or item == NS - 1:
                    return
                s = 0 if item == "start" else item + 1
                if s == 0:
                    act.wait_ge(*dve_pre.at("de1", g))
                if s >= 2:
                    act.wait_ge(*dve_scan.at(f"state{s - 2}", g))
                elif not first(g):
                    act.wait_ge(*dve_scan.at(f"state{NS - 2 + s}", g - 1))
                for h in range(2):
                    view = decay[:, s % 2, h * T:(h + 1) * T].rearrange("p (b l) -> p b l", b=GB)
                    ins = act.activation(view[:, :, 1:], delta[:, h, :].rearrange("p (b l) -> p b l", b=GB)[:, :, 1:],
                                         ACT.Exp, scale=a_neg[:, h, s:s + 1])
                ins.then_inc(*act_scan.done(f"decay{s}"))

            def att(item, g, out_of):
                if item == "norm":
                    normalise("att", g)
                elif item == "xn2T":
                    act.wait_ge(*pe_att.at("xn2T", g))
                    act.activation(x2n_t[:], out_of("xn2T")[:], copy, scale=g_in).then_inc(*act_att.done("xnT"))
                elif item[0] == "q":
                    k = int(item[1:])
                    act.wait_ge(*pe_att.at(f"q{k}", g))
                    act.activation(q_t[:, k, :], out_of(f"q{k}")[:], copy,
                                   scale=DH ** -0.5).then_inc(*act_att.done(f"q{k}"))
                elif item == "k":
                    act.wait_ge(*pe_att.at("k", g))
                    act.activation(k_t[:], out_of("k")[:], copy).then_inc(*act_att.done("k"))
                elif item == "v":
                    act.wait_ge(*pe_att.at("v", g))
                    vn = out_of("v")[:, 0:GB * (DH + NH)].rearrange("p (b n) -> p b n", b=GB)
                    act.activation(v_a[:, :, 0:DH], vn[:, :, 0:DH], copy).then_inc(*act_att.done("v"))
                    act.activation(s_null[:], vn[:, :, DH:], copy).then_inc(*act_att.done("null"))
                elif item[0] == "P":
                    b = int(item[1:])
                    s = b % 2
                    act.wait_ge(*pool_att.at(f"sub_{b}", g))
                    act.activation(sc[:, s], sc[:, s], ACT.Exp).then_inc(*act_att.done(f"p_{b}"))
                    act.activation(p_null[:, s, :], p_null[:, s, :], ACT.Exp).then_inc(*act_att.done(f"pn_{b}"))
                elif item[0] == "T":
                    b = int(item[1:])
                    for i in range(4):
                        act.wait_ge(*pe_att.at(f"t{i}_{b}", g))
                        act.activation(p_t[:, 4 * i:4 * i + 4, :].rearrange("p h i -> p (h i)"),
                                       out_of(f"t{i}_{b}")[:], copy).then_inc(*act_att.done(f"t{i}_{b}"))
                elif item[0] == "O":
                    b = int(item[1:])
                    for i in range(2):
                        act.wait_ge(*pe_att.at(f"o{i}_{b}", g))
                        act.activation(o_t[:, 4 * i:4 * i + 4, :].rearrange("p k i -> p (k i)"),
                                       out_of(f"o{i}_{b}")[:], copy).then_inc(*act_att.done(f"o{i}_{b}"))
                elif item[0] == "W":
                    b = int(item[1:])
                    act.wait_ge(*pe_att.at(f"wo_{b}", g))
                    act.activation(a_n[:, b, :], out_of(f"wo_{b}")[:, 0:P], copy).then_inc(*act_att.done(f"wo_{b}"))

            def ffn(item, g, out_of):
                if item == "keep":
                    if not first(g):
                        act.wait_ge(*dve_ffn.at("out", g - 1))
                    act.wait_ge(*dve_att.at("x2", g))
                    act.activation(x2_kept[:], x2_n[:], copy).then_inc(*act_ffn.done("keep"))
                elif item == "norm":
                    normalise("ffn", g)
                elif item == "xfT":
                    act.wait_ge(*pe_ffn.at("xfT", g))
                    act.activation(xf_t[:], out_of("xfT")[:], copy, scale=g_out).then_inc(*act_ffn.done("xfT"))
                elif item == "router":
                    act.wait_ge(*dve_ffn.at("ls", g))
                    act.activation(pr["ffn"][:, :, 0:ED], lg["ffn"][:, :, 0:ED], ACT.Exp).then_inc(*act_ffn.done("exp"))
                elif item == "cwD":
                    weights_t("ffn", "cwD", 3 * ED, out_of("cwD"), g)
                elif item == "z15":
                    act.wait_ge(*pe_ffn.at("z15", g))
                    act.activation(fh[:, 3, :], out_of("z15")[:], ACT.Relu, bias=sb1).then_inc(*act_ffn.done("h15"))
                elif item in FFN_EXPERTS:
                    e = int(item[1:])
                    act.wait_ge(*pe_ffn.at(f"z{e}", g))
                    if e >= 3:
                        act.wait_ge(*pe_ffn.at(f"acc{e - 3}", g))
                    act.activation(fh[:, e % 3, :], out_of(f"z{e}")[:], ACT.Relu,
                                   bias=f_b1[:, e:e + 1]).then_inc(*act_ffn.done(f"h{e}"))
                elif item == "fin":
                    act.wait_ge(*pe_ffn.at("acc14", g))
                    act.activation(ff_t[:], ffn_sum[:], ACT.Identity, bias=sb2).then_inc(*act_ffn.done("ff"))

            todo = {"mix": mix, "pre": pre, "scan": scan, "att": att, "ffn": ffn}

            def body(i, banks, stages):
                for stage, item in SCHEDULE:
                    if stage in stages:
                        todo[stage](item, i + SHIFT[stage], lambda use: work[banks.bank[(stage, use)]])

            run_bodies(act, body)

        @block.vector
        def _(dve):
            dve.wait_ge(loaded, ALL_LOADED)
            dve.wait_ge(consts, CONSTS)
            for i in range(8):
                k, h = divmod(i, 2)
                dve.tensor_scalar(conv_sc[:, k, h, :], in_n[:, h, :], conv_w[:, h, k:k + 1], None,
                                  ALU.mult).then_inc(*dve_set.done(f"conv{i}"))
            for tag, n, sel, width in (("n", 32, sel_bc[:], 0), ("a", EA, sel_a[:], 64), ("d", ED, sel_d[0:3 * ED, :], 0)):
                dve.tensor_tensor(idn[0:3 * n, 0:n], ident[0:3 * n, 0:n], ident[0:3 * n, n:2 * n],
                                  ALU.add).then_inc(*dve_set.done(f"id{tag}0"))
                dve.wait_ge(*dve_set.at(f"id{tag}0"))
                dve.tensor_tensor(idn[0:3 * n, 32:32 + n], idn[0:3 * n, 0:n], ident[0:3 * n, 2 * n:3 * n],
                                  ALU.add).then_inc(*dve_set.done(f"id{tag}1"))
                dve.wait_ge(*dve_set.at(f"id{tag}1"))
                src = idn[0:3 * n, 32:32 + n]
                name = {"n": "sel_bc", "a": "sel_a", "d": "sel_d"}[tag]
                dve.tensor_copy(sel, src.unsqueeze(2).to_broadcast([3 * n, n, width]) if width else src
                                ).then_inc(*dve_set.done(name))
                dve.wait_ge(*dve_set.at(name))
            dve.tensor_tensor(null_prod, w_q[:].rearrange("p (h d) -> p h d", h=NH),
                              null_k.unsqueeze(1).to_broadcast([P, NH, DH]), ALU.mult).then_inc(*dve_set.done("null_p"))
            dve.wait_ge(*dve_set.at("null_p"))
            dve.tensor_reduce(null_sum[:], null_prod, AX.X, ALU.add).then_inc(*dve_set.done("null_s"))
            dve.wait_ge(*dve_set.at("null_s"))
            for quad in range(4):
                h0 = head_at(4 * quad)
                dve.tensor_scalar(w_vn[:, DH + 4 * quad:DH + 4 * quad + 4], null_sum[:, h0:h0 + 7:2], DH ** -0.5, None,
                                  ALU.mult).then_inc(*dve_set.done(f"wn{quad}"))
            dve.tensor_scalar(vn_row[:, 0:DH], vn_row[:, 0:DH], -1.0, None, ALU.mult).then_inc(*dve_set.done("neg_v"))
            dve.wait_ge(*act_set.at("eb_hi"))
            dve.tensor_tensor(eb_rest, eb2_r, eb2_p[:, 0, :], ALU.subtract).then_inc(*dve_set.done("eb_r"))
            dve.wait_ge(*act_set.at("eb_mid"))
            dve.tensor_tensor(eb2_p[:, 2, :], eb_rest, eb2_p[:, 1, :], ALU.subtract).then_inc(*dve_set.done("eb_lo"))

            def normalise(stage, src, g, gaps):
                mine, others = dve_s[stage], act_s[stage]
                for b in range(GB):
                    dve.bn_stats(stats[stage][:, b, :], src[:, b, :]).then_inc(*mine.done(f"st{b}"))
                dve.wait_ge(*mine.at(f"st{GB - 1}", g))
                dve.memset(gap[:, gaps:gaps + 1], 0.0)
                for b in range(GB):
                    dve.bn_aggr(mv[stage][:, b, :], stats[stage][:, b, :]).then_inc(*mine.done(f"mv{b}"))
                dve.wait_ge(*others.at("rstd", g))
                for b in range(GB):
                    dve.tensor_scalar(xn_n[stage][:, b, :], src[:, b, :], mv[stage][:, b, 0:1], rstd[stage][:, b:b + 1],
                                      ALU.subtract, ALU.mult).then_inc(*mine.done(f"xn{b}"))

            def router(stage, g, E, K, gaps):
                mine, others = dve_s[stage], act_s[stage]
                lg_, mx_, pr_, top_, rest_, zs_, cw_, cwr_, cw3_ = (
                    t[stage] for t in (lg, mx, pr, top8, rest, zs, cw, cwr, cw3))
                w = pr_.shape[2]
                dve.wait_ge(*mine.at("lg", g))
                dve.tensor_reduce(mx_[:], lg_[:, :, 0:E], AX.X, ALU.max).then_inc(*mine.done("mx"))
                dve.wait_ge(*mine.at("mx", g))
                dve.tensor_tensor(lg_[:, :, 0:E], lg_[:, :, 0:E], mx_[:].unsqueeze(2).to_broadcast([P, GB, E]),
                                  ALU.subtract).then_inc(*mine.done("ls"))
                dve.wait_ge(*others.at("exp", g))
                dve.memset(gap[:, gaps:gaps + 1], 0.0)
                for b in range(GB):
                    dve.max(top_[:, b, :], pr_[:, b, :]).then_inc(*mine.done(f"top{b}"))
                dve.wait_ge(*mine.at(f"top{GB - 1}", g))
                dve.memset(top_[:, :, K:8], SENT).then_inc(*mine.done("cut"))
                dve.wait_ge(*mine.at("cut", g))
                dve.memset(gap[:, gaps + 1:gaps + 2], 0.0)
                for b in range(GB):
                    dve.match_replace(rest_[:, b, 0:w], top_[:, b, :], pr_[:, b, :], 0.0).then_inc(*mine.done(f"rest{b}"))
                dve.wait_ge(*mine.at(f"rest{GB - 1}", g))
                dve.tensor_tensor(cw_[:, :, 0:E], pr_[:, :, 0:E], rest_[:, :, 0:E], ALU.subtract).then_inc(*mine.done("sel"))
                dve.tensor_reduce(zs_[:], pr_[:, :, 0:E], AX.X, ALU.add).then_inc(*mine.done("z"))
                if K == KA:
                    dve.wait_ge(*mine.at("z", g))
                    dve.tensor_reduce(ds_[:], cw_[:, :, 0:E], AX.X, ALU.add).then_inc(*mine.done("d"))
                    dve.wait_ge(*mine.at("d", g))
                    dve.scalar_tensor_tensor(out=zs_[:], in0=zs_[:], scalar=1e-20, in1=ds_[:], op0=ALU.mult,
                                             op1=ALU.add).then_inc(*mine.done("ds"))
                dve.wait_ge(*mine.at("ds" if K == KA else "z", g))
                dve.reciprocal(zs_[:], zs_[:]).then_inc(*mine.done("ri"))
                dve.wait_ge(*mine.at("ri", g))
                dve.tensor_tensor(cw_[:, :, 0:E], cw_[:, :, 0:E], zs_[:].unsqueeze(2).to_broadcast([P, GB, E]),
                                  ALU.mult).then_inc(*mine.done("cw"))
                dve.wait_ge(*mine.at("cw", g))
                dve.tensor_copy(cw3_[:, :, 0:E], cw_[:, :, 0:E]).then_inc(*mine.done("hi"))
                dve.wait_ge(*mine.at("hi", g))
                dve.tensor_tensor(cwr_[:, :, 0:E], cw_[:, :, 0:E], cw3_[:, :, 0:E], ALU.subtract).then_inc(*mine.done("r"))
                dve.wait_ge(*mine.at("r", g))
                dve.tensor_copy(cw3_[:, :, E:2 * E], cwr_[:, :, 0:E]).then_inc(*mine.done("mid"))
                dve.wait_ge(*mine.at("mid", g))
                dve.tensor_tensor(cw3_[:, :, 2 * E:3 * E], cwr_[:, :, 0:E], cw3_[:, :, E:2 * E],
                                  ALU.subtract).then_inc(*mine.done("lo"))

            def mix(item, g, out_of):
                if item == "lgA":
                    dve.wait_ge(*pe_mix.at("lgA", g))
                    dve.tensor_tensor(lg["mix"][:, :, 0:EA], out_of("lgA")[:, 0:GB * EA].rearrange("p (b e) -> p b e", b=GB),
                                      cond_logits[:, bass.ds(g * GB, GB), :], ALU.add).then_inc(*dve_mix.done("lg"))
                elif item == "router":
                    router("mix", g, EA, KA, 3)
                elif item in ("m0", "m1", "m2", "m3", "m4"):
                    k = int(item[1:])
                    dve.wait_ge(*act_mix.at(f"gate{k}", g))
                    dve.scalar_tensor_tensor(out=gate_s[:, k % 2, :], in0=out_of(f"gate{k}")[:], scalar=LEAK,
                                             in1=gate_s[:, k % 2, :], op0=ALU.mult,
                                             op1=ALU.max).then_inc(*dve_mix.done(f"lk{k}"))
                    dve.wait_ge(*dve_mix.at(f"lk{k}", g))
                    dve.wait_ge(*pe_mix.at(f"up{k}", g))
                    dst = gate_s[:, k % 2, :] if k < 4 else hid[:, 4, :]
                    dve.tensor_tensor(dst, gate_s[:, k % 2, :], out_of(f"up{k}")[:],
                                      ALU.mult).then_inc(*dve_mix.done(f"gu{k}" if k < 4 else "h4"))
                    if k < 4:
                        dve.wait_ge(*dve_mix.at(f"gu{k}", g))
                        dve.wait_ge(*pe_mix.at(f"wide{k}", g))
                        dve.tensor_tensor(hid[:, k, :], gate_s[:, k % 2, :], out_of(f"wide{k}")[:],
                                          ALU.mult).then_inc(*dve_mix.done(f"h{k}"))
                elif item == "norm":
                    dve.wait_ge(*act_mix.at("y", g))
                    normalise("mix", y_n, g, 0)

            def pre(item, g, out_of):
                if item == "bc":
                    dve.wait_ge(*act_pre.at("dt", g))
                    dve.tensor_tensor(bc_r, out_of("bc")[0:64, :], bc3[0:64, :],
                                      ALU.subtract).then_inc(*dve_pre.done("bc_r"))
                    dve.wait_ge(*act_pre.at("bc_mid", g))
                    dve.tensor_tensor(bc3[0:32, :], bc_dt[0:32, :], bc3[0:32, :],
                                      ALU.subtract).then_inc(*dve_pre.done("bc_lo"))
                elif item == "d":
                    for h in range(2):
                        dve.wait_ge(*pe_pre.at(f"d{h}", g))
                        dve.tensor_scalar(delta[:, h, :], out_of(f"d{h}")[:], dt_b[:, h:h + 1], CLAMP, ALU.add,
                                          ALU.min).then_inc(*dve_pre.done(f"cl{h}"))
                elif item == "sp":
                    for h in range(2):
                        dve.wait_ge(*act_pre.at(f"sp{h}", g))
                        dve.scalar_tensor_tensor(out=delta[:, h, :], in0=out_of(f"d{h}")[:], scalar=dt_b[:, h:h + 1],
                                                 in1=delta[:, h, :], op0=ALU.add,
                                                 op1=ALU.max).then_inc(*dve_pre.done(f"de{h}"))
                    dve.wait_ge(*dve_pre.at("de1", g))
                    dve.tensor_tensor(du[:], delta[:], u_c[:], ALU.mult).then_inc(*dve_pre.done("du"))

            def scan(item, g, out_of):
                def drive_of(s):
                    dve.wait_ge(*pe_scan.at(f"b{s}", g))
                    if s >= 3:
                        dve.wait_ge(*pe_scan.at(f"y{s - 3}", g))
                    dve.tensor_tensor(chain[:, s % 3, :].rearrange("p (h t) -> p h t", h=2), du[:],
                                      b_wide[:].unsqueeze(1).to_broadcast([P, 2, T]),
                                      ALU.mult).then_inc(*dve_scan.done(f"drive{s}"))

                if item == "start":
                    dve.wait_ge(*dve_pre.at("du", g))
                    drive_of(0)
                elif item == "end":
                    dve.wait_ge(*pe_scan.at(f"y{NS - 1}", g))
                    for h in range(2):
                        dve.scalar_tensor_tensor(out=u_c[:, h, :], in0=u_c[:, h, :], scalar=d_skip[:, h:h + 1],
                                                 in1=y_sum[h][:], op0=ALU.mult,
                                                 op1=ALU.add).then_inc(*dve_scan.done(f"yd{h}"))
                    dve.wait_ge(*dve_scan.at("yd1", g))
                    dve.tensor_tensor(u_c[:], u_c[:], res_s[:], ALU.mult).then_inc(*dve_scan.done("yg"))
                else:
                    s = item
                    dve.wait_ge(*dve_scan.at(f"drive{s}", g))
                    dve.wait_ge(*act_scan.at(f"decay{s}", g))
                    dve.tensor_tensor_scan(chain[:, s % 3, :], decay[:, s % 2, :], chain[:, s % 3, :], 0.0,
                                           ALU.mult, ALU.add).then_inc(*dve_scan.done(f"state{s}"))
                    if s + 1 < NS:
                        drive_of(s + 1)
                    dve.wait_ge(*dve_scan.at(f"state{s}", g))
                    dve.wait_ge(*pe_scan.at(f"c{s}", g))
                    dve.tensor_tensor(chain[:, s % 3, :].rearrange("p (h t) -> p h t", h=2),
                                      chain[:, s % 3, :].rearrange("p (h t) -> p h t", h=2),
                                      c_wide[:].unsqueeze(1).to_broadcast([P, 2, T]),
                                      ALU.mult).then_inc(*dve_scan.done(f"read{s}"))

            def att(item, g, out_of):
                if item == "op":
                    dve.wait_ge(*pe_att.at("op", g))
                    dve.wait_ge(*pool_pre.at("xy", g))
                    if not first(g):
                        dve.wait_ge(*act_ffn.at("keep", g - 1))
                    dve.tensor_tensor(x2_n[:], out_of("op")[:].rearrange("p (b d) -> p b d", b=GB), xy[:],
                                      ALU.add).then_inc(*dve_att.done("x2"))
                elif item == "norm":
                    dve.wait_ge(*dve_att.at("x2", g))
                    normalise("att", x2_n, g, 1)
                elif item == "v":
                    dve.wait_ge(mask_loaded, 16 * (g + 1))
                    dve.tensor_scalar(key_mask[:], mask_u8[:], -1.0, -NEG, ALU.add,
                                      ALU.mult).then_inc(*dve_att.done("mask"))
                elif item[0] == "S":
                    b = int(item[1:])
                    s = b % 2
                    for i in range(4):
                        dve.wait_ge(*pe_att.at(f"s{i}_{b}", g))
                        dve.tensor_tensor(sc[:, s, 4 * i:4 * i + 4, :],
                                          out_of(f"s{i}_{b}")[:].rearrange("p (h j) -> p h j", h=4),
                                          bias[:, 4 * i:4 * i + 4, :], ALU.add).then_inc(*dve_att.done(f"s{i}_{b}"))
                    dve.wait_ge(*dve_att.at(f"s3_{b}", g))
                    dve.tensor_reduce(smax[:, s, :], sc[:, s], AX.X, ALU.max).then_inc(*dve_att.done(f"mx_{b}"))
                    dve.wait_ge(*dve_att.at(f"mx_{b}", g))
                    dve.wait_ge(*act_att.at("null", g))
                    dve.tensor_tensor(smax[:, s, :], smax[:, s, :], s_null[:, b, :],
                                      ALU.max).then_inc(*dve_att.done(f"mn_{b}"))
                elif item[0] == "V":
                    b = int(item[1:])
                    s = b % 2
                    dve.wait_ge(*act_att.at(f"pn_{b}", g))
                    for i, (h0, h1) in enumerate(PV_HEADS):
                        n = h1 - h0
                        dve.wait_ge(*pe_att.at(f"pv{i}_{b}", g))
                        pv = out_of(f"pv{i}_{b}")[:, 0:n * (DH + 1)].rearrange("p (h d) -> p h d", h=n)
                        dve.tensor_tensor(den[:, h0:h1], pv[:, :, DH], p_null[:, s, h0:h1],
                                          ALU.add).then_inc(*dve_att.done(f"den{i}_{b}"))
                        dve.wait_ge(*dve_att.at(f"den{i}_{b}", g))
                        dve.reciprocal(den[:, h0:h1], den[:, h0:h1]).then_inc(*dve_att.done(f"rden{i}_{b}"))
                        dve.wait_ge(*dve_att.at(f"rden{i}_{b}", g))
                        dve.tensor_tensor(o_n[:, h0:h1, :], pv[:, :, 0:DH],
                                          den[:, h0:h1].unsqueeze(2).to_broadcast([P, n, DH]),
                                          ALU.mult).then_inc(*dve_att.done(f"on{i}_{b}"))

            def ffn(item, g, out_of):
                if item == "norm":
                    dve.wait_ge(*act_att.at(f"wo_{GB - 1}", g))
                    normalise("ffn", a_n, g, 2)
                elif item == "lgD":
                    dve.wait_ge(*pe_ffn.at("lgD", g))
                    dve.tensor_copy(lg["ffn"][:, :, 0:ED],
                                    out_of("lgD")[:, 0:GB * ED].rearrange("p (b e) -> p b e", b=GB)
                                    ).then_inc(*dve_ffn.done("lg"))
                elif item == "router":
                    router("ffn", g, ED, KD, 5)
                elif item in FFN_EXPERTS:
                    e = int(item[1:])
                    dve.wait_ge(*act_ffn.at(f"h{e}", g))
                    dve.wait_ge(*pe_ffn.at(f"cw{e}", g))
                    dve.tensor_tensor(fh[:, e % 3, :], fh[:, e % 3, :], out_of(f"cw{e}")[:],
                                      ALU.mult).then_inc(*dve_ffn.done(f"c{e}"))
                elif item == "fin":
                    dve.wait_ge(*pe_ffn.at("fin", g))
                    if not first(g):
                        dve.wait_ge(stored, 16 * g)
                    dve.wait_ge(*act_ffn.at("keep", g))
                    dve.tensor_tensor(y_out[:], out_of("fin")[:].rearrange("p (b d) -> p b d", b=GB), x2_kept[:],
                                      ALU.add).then_inc(*dve_ffn.done("out"))

            todo = {"mix": mix, "pre": pre, "scan": scan, "att": att, "ffn": ffn}

            def body(i, banks, stages):
                for stage, item in SCHEDULE:
                    if stage in stages:
                        todo[stage](item, i + SHIFT[stage], lambda use: work[banks.bank[(stage, use)]])

            run_bodies(dve, body)

        @block.tensor
        def _(pe):
            pe.wait_ge(loaded, ALL_LOADED)
            pe.wait_ge(consts, CONSTS)

            def set_claim(use):
                if set_banks.prev[use]:
                    steps, name = released[set_banks.prev[use][0]]
                    pe.wait_ge(*steps.at(name))
                return work[set_banks.bank[use]]

            for i in range(2):
                o = set_claim(f"s_conv{i}")
                pe.wait_ge(*dve_set.at(f"conv{4 * i + 3}"))
                for j in range(4):
                    k, h = divmod(4 * i + j, 2)
                    ins = pe.transpose(o[:, j * P:(j + 1) * P], conv_sc[:, k, h, :], ident[:])
                ins.then_inc(*pe_set.done(f"s_conv{i}"))
            o = set_claim("s_res")
            for h in range(2):
                ins = pe.transpose(o[:, h * P:(h + 1) * P], in_n[:, 2 + h, :], ident[:])
            ins.then_inc(*pe_set.done("s_res"))
            o = set_claim("s_out")
            for h in range(2):
                ins = pe.transpose(o[:, h * P:(h + 1) * P], out_n[:, h, :], ident[:])
            ins.then_inc(*pe_set.done("s_out"))
            o = set_claim("s_xp")
            for h in range(2):
                ins = pe.transpose(o[:, h * 104:(h + 1) * 104], xp_n[:, h, :], ident[0:104, 0:104])
            ins.then_inc(*pe_set.done("s_xp"))
            o = set_claim("s_dt")
            for h in range(2):
                ins = pe.transpose(o[0:104, h * P:(h + 1) * P], dtw_n[:, h, :], ident[:])
            ins.then_inc(*pe_set.done("s_dt"))
            o = set_claim("s_small")
            pe.transpose(o[:, 0:EA], wt_n[:], ident[0:EA, 0:EA])
            pe.transpose(o[0:64, 128:128 + EA], wg_n[:], ident[0:EA, 0:EA])
            pe.transpose(o[0:64, 256:256 + NB], cond_n[:], ident[0:NB, 0:NB]).then_inc(*pe_set.done("s_small"))
            o = set_claim("s_cond")
            pe.wait_ge(*act_set.at("cond"))
            for b in range(NB):
                ins = pe.matmul(o[:, b * EA:(b + 1) * EA], cond_t[:, b:b + 1].to_broadcast([64, P]), wg_t[:],
                                start=True, stop=True)
            ins.then_inc(*pe_set.done("s_cond"))
            o = set_claim("s_crow")
            for k in range(8):
                ins = pe.matmul(o[0:1, 0:P], null_v[:], w_o[:, k, :], start=(k == 0), stop=(k == 7))
            ins.then_inc(*pe_set.done("s_crow"))
            pe.wait_ge(*act_set.at("eb_mid"))
            pe.wait_ge(*dve_set.at("eb_lo"))

            def seq(t, b):
                return t[:, b * P:(b + 1) * P]

            def to_features(o, src):
                for b in range(GB):
                    ins = pe.transpose(seq(o, b), src[:, b, :], ident[:])
                return ins

            def parts_to_rows(o, parts):
                for b in range(GB):
                    ins = pe.transpose(o[:].bitcast(BF16)[:, b * P:(b + 1) * P], parts[:, b, :], ident_bf[:])
                return ins

            def product(o, lhsT, rhs):
                return pe.matmul(o[:], lhsT, rhs, start=True, stop=True)

            def mix(item, g, claim):
                if item == "xT":
                    pe.wait_ge(x_loaded, 16 * (g + 1))
                    to_features(claim("xT"), x_n).then_inc(*pe_mix.done("xT"))
                elif item == "lgA":
                    o = claim("lgA")
                    pe.wait_ge(*act_mix.at("xT", g))
                    for b in range(GB):
                        ins = pe.matmul(o[:, b * EA:(b + 1) * EA], seq(x_t, b), wt_t[:], start=True, stop=True)
                    ins.then_inc(*pe_mix.done("lgA"))
                elif item == "cwA":
                    o = claim("cwA")
                    pe.wait_ge(*dve_mix.at("lo", g))
                    parts_to_rows(o, cw3["mix"]).then_inc(*pe_mix.done("cwA"))
                elif item in ("m0", "m1", "m2", "m3"):
                    k = int(item[1:])
                    pair = slice(2 * k, 2 * k + 2)
                    product(claim(f"gate{k}"), w_gate[:, pair, :].rearrange("p e m -> p (e m)"),
                            x_t[:]).then_inc(*pe_mix.done(f"gate{k}"))
                    product(claim(f"up{k}"), w_up[:, pair, :].rearrange("p e m -> p (e m)"),
                            x_t[:]).then_inc(*pe_mix.done(f"up{k}"))
                    o = claim(f"wide{k}")
                    pe.wait_ge(*act_mix.at("cw3", g))
                    product(o, sel_a[:, pair, :].rearrange("p e m -> p (e m)"),
                            cw3_t["mix"][:]).then_inc(*pe_mix.done(f"wide{k}"))
                elif item == "m4":
                    product(claim("gate4"), sw_gate[:], x_t[:]).then_inc(*pe_mix.done("gate4"))
                    product(claim("up4"), sw_up[:], x_t[:]).then_inc(*pe_mix.done("up4"))
                elif item == "moe":
                    o = claim("moe")
                    pe.wait_ge(*dve_mix.at("h4", g))
                    for b in range(GB):
                        for k in range(5):
                            ins = pe.matmul(seq(o, b), hid[:, k, b * P:(b + 1) * P],
                                            w_down[:, k, :] if k < 4 else sw_down[:], start=(k == 0), stop=(k == 4))
                    ins.then_inc(*pe_mix.done("moe"))
                elif item == "xnT":
                    o = claim("xnT")
                    pe.wait_ge(*dve_mix.at(f"xn{GB - 1}", g))
                    to_features(o, xn_n["mix"]).then_inc(*pe_mix.done("xnT"))

            def pre(item, g, claim):
                if item in ("u0", "u1"):
                    h = int(item[1:])
                    o = claim(item)
                    pe.wait_ge(*act_mix.at("xnT", g))
                    for k in range(TAPS):
                        ins = pe.matmul(o[:].rearrange("p (b s) -> p b s", b=GB), conv_t[:, k, h, :],
                                        xn_t[:, :, k:k + P], start=(k == 0), stop=(k == TAPS - 1))
                    ins.then_inc(*pe_pre.done(item))
                elif item in ("r0", "r1"):
                    o = claim(item)
                    pe.matmul(o[:].rearrange("p (b s) -> p b s", b=GB), res_t[:, int(item[1:]), :],
                              xn_t[:, :, TAPS - 1:], start=True, stop=True).then_inc(*pe_pre.done(item))
                elif item == "bc":
                    o = claim("bc")
                    pe.wait_ge(*act_pre.at("u1", g))
                    for h in range(2):
                        ins = pe.matmul(o[0:104, :], xp_t[:, h, :], u_c[:, h, :], start=(h == 0), stop=(h == 1))
                    ins.then_inc(*pe_pre.done("bc"))
                elif item == "d":
                    for h in range(2):
                        o = claim(f"d{h}")
                        pe.wait_ge(*act_pre.at("dt", g))
                        pe.matmul(o[:], dtw_t[96:104, h, :], dt_s, start=True, stop=True,
                                  tile_position=(96, 0)).then_inc(*pe_pre.done(f"d{h}"))

            def scan(item, g, claim):
                def widen(psum, name, row, read_by):
                    if read_by is not None:
                        pe.wait_ge(*read_by)
                    pe.matmul(psum[:], sel_bc[:, row:row + 1].to_broadcast([96, P]), bc3[:], start=True,
                              stop=True).then_inc(*pe_scan.done(name))

                def sum_state(s):
                    if s == 0 and not first(g):
                        pe.wait_ge(*dve_scan.at("yd1", g - 1))
                    pe.wait_ge(*dve_scan.at(f"read{s}", g))
                    for h in range(2):
                        ins = pe.matmul(y_sum[h][:], ident[:], chain[:, s % 3, h * T:(h + 1) * T],
                                        start=(s == 0), stop=(s == NS - 1))
                    ins.then_inc(*pe_scan.done(f"y{s}"))

                if item == "start":
                    pe.wait_ge(*dve_pre.at("bc_lo", g))
                    widen(b_wide, "b0", 0, None if first(g) else dve_scan.at(f"drive{NS - 1}", g - 1))
                elif item == "end":
                    sum_state(NS - 1)
                else:
                    s = item
                    widen(c_wide, f"c{s}", NS + s, dve_scan.at(f"read{s - 1}", g) if s else
                          None if first(g) else dve_scan.at(f"read{NS - 1}", g - 1))
                    if s + 1 < NS:
                        widen(b_wide, f"b{s + 1}", s + 1, dve_scan.at(f"drive{s}", g))
                    if s:
                        sum_state(s - 1)

            def att(item, g, claim):
                if item == "op":
                    o = claim("op")
                    pe.wait_ge(*dve_scan.at("yg", g))
                    for b in range(GB):
                        for h in range(2):
                            ins = pe.matmul(seq(o, b), u_c[:, h, b * P:(b + 1) * P], out_t[:, h, :],
                                            start=(h == 0), stop=(h == 1))
                    ins.then_inc(*pe_att.done("op"))
                elif item == "xn2T":
                    o = claim("xn2T")
                    pe.wait_ge(*dve_att.at(f"xn{GB - 1}", g))
                    to_features(o, xn_n["att"]).then_inc(*pe_att.done("xn2T"))
                elif item[0] == "q":
                    o = claim(item)
                    k = int(item[1:])
                    pe.wait_ge(*act_att.at("xnT", g))
                    product(o, w_q[:, k * P:(k + 1) * P], x2n_t[:]).then_inc(*pe_att.done(item))
                elif item == "k":
                    product(claim("k"), w_k2[:].rearrange("p a d -> p (a d)"), x2n_t[:]).then_inc(*pe_att.done("k"))
                elif item == "v":
                    o = claim("v")
                    n = DH + NH
                    for b in range(GB):
                        pe.matmul(o[:, b * n:(b + 1) * n], seq(x2n_t, b), w_vn[:], start=True, stop=False)
                        ins = pe.matmul(o[:, b * n:(b + 1) * n], ones_row[:], vn_row[:], start=False, stop=True)
                    ins.then_inc(*pe_att.done("v"))
                elif item[0] == "S":
                    b = int(item[1:])
                    tok = slice(b * P, (b + 1) * P)
                    for i in range(4):
                        o = claim(f"s{i}_{b}")
                        if b == 0 and i == 0:
                            pe.wait_ge(*act_att.at("k", g))
                            pe.wait_ge(*dve_att.at("mask", g))
                        r = 64 * (i % 2)
                        pe.matmul(o[:].rearrange("p (h j) -> p h j", h=4), ones_bf[r:r + 1, :],
                                  key_mask[r:r + 1, tok].unsqueeze(1).to_broadcast([1, 4, P]), start=True, stop=False)
                        for j in range(4):
                            ins = pe.matmul(o[:, j * P:(j + 1) * P], q_t[r:r + 64, head_at(4 * i + j) // 2, tok],
                                            k_t[r:r + 64, tok], start=False, stop=(j == 3))
                        ins.then_inc(*pe_att.done(f"s{i}_{b}"))
                elif item[0] == "T":
                    b = int(item[1:])
                    pe.wait_ge(*act_att.at(f"p_{b}", g))
                    for i in range(4):
                        o = claim(f"t{i}_{b}")
                        for j in range(4):
                            ins = pe.transpose(seq(o, j), sc[:, b % 2, 4 * i + j, :], ident[:])
                        ins.then_inc(*pe_att.done(f"t{i}_{b}"))
                elif item[0] == "V":
                    b = int(item[1:])
                    for i, (h0, h1) in enumerate(PV_HEADS):
                        o = claim(f"pv{i}_{b}")
                        pe.wait_ge(*act_att.at(f"t{(h1 - 1) // 4}_{b}", g))
                        for h in range(h0, h1):
                            ins = pe.matmul(o[:, (h - h0) * (DH + 1):(h - h0 + 1) * (DH + 1)], p_t[:, h, :],
                                            v_a[:, b, :], start=True, stop=True)
                        ins.then_inc(*pe_att.done(f"pv{i}_{b}"))
                elif item[0] == "O":
                    b = int(item[1:])
                    for i in range(2):
                        o = claim(f"o{i}_{b}")
                        pe.wait_ge(*dve_att.at(f"on{i + 1}_{b}", g))
                        for j in range(4):
                            k = 4 * i + j
                            ins = pe.transpose(seq(o, j), o_n[:, 2 * k:2 * k + 2, :].rearrange("p h d -> p (h d)"),
                                               ident[:])
                        ins.then_inc(*pe_att.done(f"o{i}_{b}"))
                elif item[0] == "W":
                    b = int(item[1:])
                    o = claim(f"wo_{b}")
                    pe.wait_ge(*act_att.at(f"o1_{b}", g))
                    for k in range(8):
                        pe.matmul(o[:, 0:P], o_t[:, k, :], w_o[:, k, :], start=(k == 0), stop=False)
                    pe.matmul(o[:, 0:P], ones_row[:], o_row[:], start=False, stop=True).then_inc(*pe_att.done(f"wo_{b}"))

            def ffn(item, g, claim):
                def accumulate(e):
                    pe.wait_ge(*dve_ffn.at(f"c{e}", g))
                    pe.matmul(ffn_sum[:], f_w2[:, e, :], fh[:, e % 3, :], start=False,
                              stop=(e == ED - 1)).then_inc(*pe_ffn.done(f"acc{e}"))

                if item == "xfT":
                    o = claim("xfT")
                    pe.wait_ge(*dve_ffn.at(f"xn{GB - 1}", g))
                    to_features(o, xn_n["ffn"]).then_inc(*pe_ffn.done("xfT"))
                elif item == "lgD":
                    o = claim("lgD")
                    pe.wait_ge(*act_ffn.at("xfT", g))
                    for b in range(GB):
                        pe.matmul(o[:, b * ED:(b + 1) * ED], seq(xf_t, b), r_w[:], start=True, stop=False)
                        ins = pe.matmul(o[:, b * ED:(b + 1) * ED], ones_row[:], r_b[:], start=False, stop=True)
                    ins.then_inc(*pe_ffn.done("lgD"))
                elif item == "cwD":
                    o = claim("cwD")
                    pe.wait_ge(*dve_ffn.at("lo", g))
                    parts_to_rows(o, cw3["ffn"]).then_inc(*pe_ffn.done("cwD"))
                elif item == "z15":
                    product(claim("z15"), fs_w1[:], xf_t[:]).then_inc(*pe_ffn.done("z15"))
                elif item == "acc-1":
                    if not first(g):
                        pe.wait_ge(*act_ffn.at("ff", g - 1))
                    pe.wait_ge(*act_ffn.at("cw3", g))
                    for part in range(3):
                        pe.matmul(ffn_sum[:], eb2_p[:, part, :], cw3_t["ffn"][:], start=(part == 0), stop=False)
                    pe.wait_ge(*act_ffn.at("h15", g))
                    pe.matmul(ffn_sum[:], fs_w2[:], fh[:, 3, :], start=False, stop=False).then_inc(*pe_ffn.done("acc-1"))
                elif item in FFN_EXPERTS:
                    e = int(item[1:])
                    product(claim(f"z{e}"), f_w1[:, e, :], xf_t[:]).then_inc(*pe_ffn.done(f"z{e}"))
                    product(claim(f"cw{e}"), sel_d[0:3 * ED, e:e + 1].to_broadcast([3 * ED, P]),
                            cw3_t["ffn"][:]).then_inc(*pe_ffn.done(f"cw{e}"))
                    if e:
                        accumulate(e - 1)
                elif item == "acc14":
                    accumulate(ED - 1)
                elif item == "fin":
                    o = claim("fin")
                    pe.wait_ge(*act_ffn.at("ff", g))
                    for b in range(GB):
                        ins = pe.transpose(seq(o, b), seq(ff_t, b), ident[:])
                    ins.then_inc(*pe_ffn.done("fin"))

            todo = {"mix": mix, "pre": pre, "scan": scan, "att": att, "ffn": ffn}

            def body(i, banks, stages):
                def claim(stage, use):
                    (before, name), between = banks.prev[(stage, use)]
                    steps, step = released[name]
                    pe.wait_ge(*steps.at(step, 0 if before == "set" else i + SHIFT[before] - between))
                    return work[banks.bank[(stage, use)]]

                for stage, item in SCHEDULE:
                    if stage in stages:
                        todo[stage](item, i + SHIFT[stage], lambda use: claim(stage, use))

            run_bodies(pe, body)


def kernel(**inputs):
    import numpy as _np
    import concourse.bacc as _bacc
    from concourse import mybir as _mybir
    from concourse.bass_utils import run_bass_kernel_spmd as _run

    nc = _bacc.Bacc("TRN2", target_bir_lowering=False, num_devices=1)
    arrays, args = {}, {}
    for name, value in inputs.items():
        a = _np.ascontiguousarray(value)
        arrays[f"in_{name}_dram"] = a
        args[name] = nc.dram_tensor(f"in_{name}_dram", a.shape, _mybir.dt.from_np(a.dtype), kind="ExternalInput").ap()
    shape = inputs["x"].shape
    out = nc.dram_tensor("out_0_dram", shape, _mybir.dt.from_np(_np.dtype("float32")), kind="ExternalOutput").ap()
    mixture_block_kernel(nc, args, out)
    r = _run(nc, [arrays], core_ids=[0])
    return r.results[0]["out_0_dram"]
```

```python
from contextlib import ExitStack

import concourse.bass as bass
from concourse import mybir

ALU = mybir.AluOpType
ACT = mybir.ActivationFunctionType
AX = mybir.AxisListType
F32 = mybir.dt.float32
BF16 = mybir.dt.bfloat16
U8 = mybir.dt.uint8


P = 128
GB = 4
T = GB * P
EPS = 1e-5
NEG = -1.0e30
TAPS = 4
NS = 16
NH, DH = 16, 64
EA, KA = 8, 2
ED, KD = 15, 3
DTR = 8
LEAK = 0.01
CLAMP = 30.0
WORK = 5
SENT = -1.0


def head_at(pos):
    quad, j = divmod(pos, 4)
    return 8 * (quad // 2) + 2 * j + quad % 2


class Steps:

    def __init__(self, sem, names):
        self.sem, self.names, self.no, self.next = sem, names, {n: i for i, n in enumerate(names)}, 0
        assert len(self.no) == len(names)

    def done(self, name):
        assert self.names[self.next] == name, (self.names[self.next], name)
        self.next = (self.next + 1) % len(self.names)
        return self.sem, 1

    def at(self, name, g=0):
        return self.sem, g * len(self.names) + self.no[name] + 1


class WorkBanks:

    def __init__(self, uses, before=()):
        n = len(uses)
        assert len(set(uses)) == n and n >= WORK
        self.last = uses[-WORK:]
        self.bank = {u: (i - n) % WORK for i, u in enumerate(uses)}
        self.prev = {}
        holder = {i: (u, True) for i, u in enumerate(before)}
        for u in uses:
            self.prev[u] = holder.get(self.bank[u])
            holder[self.bank[u]] = (u, False)


SHIFT = {"mix": 3, "pre": 2, "scan": 2, "att": 1, "ffn": 0}
STAGES = ("mix", "pre", "scan", "att", "ffn")

ORDER = """
    att.end ffn.norm ffn.keep pre.u0 pre.u1 ffn.xfT att.op pre.su0 pre.r0 pre.su1 pre.xy pre.r1 att.norm pre.bc
          mix.xT ffn.lgD pre.d att.xn2T ffn.router pre.sp att.q0 att.q1 ffn.cwD att.q2 mix.lgA scan.start ffn.z15
    scan.h0 ffn.acc-1 ffn.e0 scan.d0 att.q3 att.q4 scan.r0 mix.router att.q5
    scan.h1 ffn.e1 scan.d1 att.q6 att.q7 scan.r1 mix.cwA att.k
    scan.h2 ffn.e2 scan.d2 scan.r2 mix.m0 att.v
    scan.h3 ffn.e3 scan.d3 scan.r3 att.S0
    scan.h4 ffn.e4 mix.m1 scan.d4 scan.r4 att.S1
    scan.h5 scan.d5 att.P0 scan.r5 att.T0 ffn.e5 att.V0
    scan.h6 ffn.e6 scan.d6 scan.r6 mix.m2
    scan.h7 ffn.e7 att.P1 scan.d7 scan.r7 att.S2 att.O0 ffn.e8
    scan.h8 scan.d8 att.T1 scan.r8 att.W0
    scan.h9 ffn.e9 scan.d9 scan.r9 att.V1 mix.m3 att.P2
    scan.h10 scan.d10 ffn.e10 scan.r10 att.S3 att.O1
    scan.h11 scan.d11 att.T2 ffn.e11 scan.r11 att.W1 att.P3
    scan.h12 ffn.e12 scan.d12 att.V2 scan.r12 mix.m4
    scan.h13 ffn.e13 scan.d13 mix.moe scan.r13 att.O2 att.T3 mix.norm
    scan.h14 ffn.e14 scan.d14 att.V3 scan.r14 att.W2
    scan.h15 ffn.acc14 mix.xnT scan.d15 att.O3 scan.r15 ffn.fin att.W3
"""
SCHEDULE = [tuple(item.split(".")) for item in ORDER.split()]
PV_HEADS = [(0, 6), (6, 11), (11, 16)]


FFN_EXPERTS = [f"e{e}" for e in range(ED)]


def router_steps(k):
    return (["mx", "ls"] + [f"top{b}" for b in range(GB)] + ["cut"] + [f"rest{b}" for b in range(GB)]
            + ["sel", "z"] + (["d", "ds"] if k == KA else []) + ["ri", "cw", "hi", "r", "mid", "lo"])


NORM_V = [f"{w}{b}" for w in ("st", "mv", "xn") for b in range(GB)]
NORM_A = ["lnv", "rstd"]
PE_STEPS = {
    "mix": {"xT": ["xT"], "lgA": ["lgA"], "cwA": ["cwA"], **{f"m{k}": [f"gate{k}", f"up{k}", f"wide{k}"] for k in range(4)},
            "m4": ["gate4", "up4"], "moe": ["moe"], "xnT": ["xnT"]},
    "pre": {"u0": ["u0"], "u1": ["u1"], "r0": ["r0"], "r1": ["r1"], "bc": ["bc"], "d": ["d0", "d1"]},
    "scan": {"start": ["b0"], **{f"h{s}": [f"b{s + 1}"] for s in range(NS - 1)}, **{f"d{s}": [f"c{s}"] for s in range(NS)}},
    "att": {"op": ["op"], "xn2T": ["xn2T"], **{f"q{k}": [f"q{k}"] for k in range(8)}, "k": ["k"], "v": ["v"],
            **{f"S{b}": [f"s{i}_{b}" for i in range(4)] for b in range(GB)},
            **{f"T{b}": [f"t{i}_{b}" for i in range(4)] for b in range(GB)},
            **{f"V{b}": [f"pv{i}_{b}" for i in range(3)] for b in range(GB)},
            **{f"O{b}": [f"o{i}_{b}" for i in range(2)] for b in range(GB)},
            **{f"W{b}": [f"wo_{b}"] for b in range(GB)}},
    "ffn": {"xfT": ["xfT"], "lgD": ["lgD"], "cwD": ["cwD"], "z15": ["z15"], "acc-1": ["acc-1"],
            **{f"e{e}": [f"z{e}", f"cw{e}"] + ([f"acc{e - 1}"] if e else []) for e in range(ED)},
            "acc14": ["acc14"], "fin": ["fin"]},
}
ACT_STEPS = {
    "mix": {"xT": ["xT"], "router": ["exp"], "cwA": ["cw3"], **{f"m{k}": [f"gate{k}"] for k in range(5)}, "moe": ["y"],
            "norm": NORM_A, "xnT": ["xnT"]},
    "pre": {"su0": ["u0"], "su1": ["u1"], "r0": ["r0"], "r1": ["r1"], "bc": ["bc_hi", "dt", "bc_mid"],
            "sp": ["e0", "sp0", "e1", "sp1"]},
    "scan": {"start": ["decay0"], **{f"h{s}": [f"decay{s + 1}"] for s in range(NS - 1)}},
    "att": {"norm": NORM_A, "xn2T": ["xnT"], **{f"q{k}": [f"q{k}"] for k in range(8)}, "k": ["k"], "v": ["v", "null"],
            **{f"P{b}": [f"p_{b}", f"pn_{b}"] for b in range(GB)},
            **{f"T{b}": [f"t{i}_{b}" for i in range(4)] for b in range(GB)},
            **{f"V{b}": [f"{v}{i}_{b}" for i in range(3) for v in ("pv", "sum")] for b in range(GB)},
            **{f"O{b}": [f"o{i}_{b}" for i in range(2)] for b in range(GB)},
            **{f"W{b}": [f"wo_{b}"] for b in range(GB)}},
    "ffn": {"keep": ["keep"], "norm": NORM_A, "xfT": ["xfT"], "router": ["exp"], "cwD": ["cw3"], "z15": ["h15"],
            **{f"e{e}": [f"h{e}"] for e in range(ED)}, "fin": ["ff"]},
}
DVE_STEPS = {
    "mix": {"lgA": ["lg"], "router": router_steps(KA), **{f"m{k}": [f"lk{k}", f"gu{k}", f"h{k}"] for k in range(4)}, "m4": ["lk4", "h4"],
            "norm": NORM_V},
    "pre": {"bc": ["bc_r", "bc_lo"], "d": ["cl0", "cl1"], "sp": ["de0", "de1", "du"]},
    "scan": {"start": ["drive0"], **{f"h{s}": [f"state{s}"] for s in range(NS)},
             **{f"d{s}": [f"drive{s + 1}"] for s in range(NS - 1)}, **{f"r{s}": [f"read{s}"] for s in range(NS)}},
    "att": {"end": ["yd0", "yd1", "yg"], "op": ["x2"], "norm": NORM_V, "v": ["mask"],
            **{f"S{b}": [f"s0_{b}"] + [f"{w}_{b}" for i in (1, 2, 3) for w in (f"s{i}", f"mx{i - 1}")] + [f"mx3_{b}", f"mn_{b}"] for b in range(GB)},
            **{f"V{b}": [f"den_{b}", f"rden_{b}"] for b in range(GB)}},
    "ffn": {"norm": NORM_V, "lgD": ["lg"], "router": router_steps(KD), **{f"e{e}": [f"c{e}"] for e in range(ED)}, "fin": ["out"]},
}
POOL_STEPS = {
    "pre": {"xy": ["xy"]},
    "scan": {f"r{s}": [f"y{s}"] for s in range(1, NS)},
    "att": {**{f"S{b}": [f"null_{b}", f"sub_{b}"] for b in range(GB)}, **{f"V{b}": [f"on_{b}"] for b in range(GB)}},
}
SETUP_USES = {-3: ["s_small", "s_cond"], -2: ["s_conv0", "s_conv1", "s_res", "s_xp", "s_dt"], -1: ["s_out", "s_crow"]}


def first(g):
    return isinstance(g, int) and g == 0


def in_order(table, stage):
    return [step for st, item in SCHEDULE if st == stage for step in table[stage].get(item, [])]


def body_uses(stages):
    return [(st, u) for st, item in SCHEDULE if st in stages and st != "scan"
            for u in PE_STEPS[st].get(item, []) if not u.startswith("acc")]


def mixture_block_kernel(nc, A, out):
    x, cond_64, fside, mask = A["x"], A["cond_64"], A["fside_16xSxS_0"], A["mask_BxS_bk0"]
    NB = x.shape[0]
    NG = NB // GB
    assert x.shape[1] == P and x.shape[2] == P and NB % GB == 0

    with ExitStack() as ctx:
        def sb(name, shape, dt=F32):
            return ctx.enter_context(nc.sbuf_tensor(name, shape, dt))

        def sem(name):
            return ctx.enter_context(nc.semaphore(name))

        work = [ctx.enter_context(nc.psum_tensor(f"work{i}", [P, 512], F32)) for i in range(WORK)]
        b_wide = ctx.enter_context(nc.psum_tensor("b_wide", [P, 512], F32))
        c_wide = ctx.enter_context(nc.psum_tensor("c_wide", [P, 512], F32))
        ffn_sum = ctx.enter_context(nc.psum_tensor("ffn_sum", [P, 512], F32))

        ident = sb("ident", [P, P])
        ident_bf = sb("ident_bf", [P, P], BF16)
        ones_row = sb("ones_row", [1, P])
        ones_bf = sb("ones_bf", [P, P], BF16)
        eps_col = sb("eps_col", [P, 1])
        sel_bc = sb("sel_bc", [96, 32], BF16)
        sel_a = sb("sel_a", [3 * EA, EA, 64], BF16)
        sel_d = sb("sel_d", [P, ED], BF16)
        w_gate = sb("w_gate", [P, EA, 64])
        w_up = sb("w_up", [P, EA, 64])
        w_down = sb("w_down", [P, 4, P])
        sw_gate = sb("sw_gate", [P, P])
        sw_up = sb("sw_up", [P, P])
        sw_down = sb("sw_down", [P, P])
        wt_n = sb("wt_n", [EA, P])
        wg_n = sb("wg_n", [EA, 64])
        cond_n = sb("cond_n", [NB, 64])
        wt_t = sb("wt_t", [P, EA])
        wg_t = sb("wg_t", [64, EA])
        cond_t = sb("cond_t", [64, NB])
        cond_logits = sb("cond_logits", [P, NB, EA])
        conv_w = sb("conv_w", [P, 2, TAPS])
        conv_t = sb("conv_t", [P, TAPS, 2, P])
        res_t = sb("res_t", [P, 2, P])
        out_t = sb("out_t", [P, 2, P])
        xp_t = sb("xp_t", [P, 2, 104])
        dtw_t = sb("dtw_t", [104, 2, P])
        a_neg = sb("a_neg", [P, 2, NS])
        cols = sb("cols", [P, 12])
        conv_b, dt_b, d_skip = cols[:, 0:2], cols[:, 2:4], cols[:, 4:6]
        ln_g, ln_b, g_in, g_out, sb1, sb2 = (cols[:, i:i + 1] for i in range(6, 12))
        w_q = sb("w_q", [P, NH * DH])
        w_k2 = sb("w_k2", [P, 2, DH])
        w_vn = sb("w_vn", [P, DH + NH])
        null_sum = sb("null_sum", [P, NH])
        null_v = sb("null_v", [P, 1])
        vn_row = sb("vn_row", [1, DH + NH])
        w_o = sb("w_o", [P, 8, P])
        o_row = sb("o_row", [1, P])
        bias = sb("bias", [P, NH, P])
        mask_u8 = sb("mask_u8", [P, T], U8)
        r_w = sb("r_w", [P, ED])
        r_b = sb("r_b", [1, ED])
        f_w1 = sb("f_w1", [P, ED, P])
        f_w2 = sb("f_w2", [P, ED, P])
        fs_w1 = sb("fs_w1", [P, P])
        fs_w2 = sb("fs_w2", [P, P])
        f_b1 = sb("f_b1", [P, ED])
        eb2_p = sb("eb2_p", [3 * ED, 3, P], BF16)

        x_n = sb("x_n", [P, GB, P])
        x_t = sb("x_t", [P, T])
        stats = {st: sb(f"stats_{st}", [P, GB, 6]) for st in ("mix", "att", "ffn")}
        mv = {st: sb(f"mv_{st}", [P, GB, 2]) for st in ("mix", "att", "ffn")}
        rstd = {st: sb(f"rstd_{st}", [P, GB]) for st in ("mix", "att", "ffn")}
        xn_n = {st: sb(f"xn_n_{st}", [P, GB, P]) for st in ("mix", "att", "ffn")}
        gap = sb("gap", [P, 7])
        both = ("mix", "ffn")
        lg = {st: sb(f"lg_{st}", [P, GB, 16]) for st in both}
        mx = {st: sb(f"mx_{st}", [P, GB]) for st in both}
        zs = {st: sb(f"zs_{st}", [P, GB]) for st in both}
        ds_ = sb("ds_", [P, GB])
        pr = {"mix": sb("pr_mix", [P, GB, 16]), "ffn": sb("pr_ffn", [P, GB, 24])}
        top8 = {st: sb(f"top8_{st}", [P, GB, 8]) for st in both}
        rest = {st: sb(f"rest_{st}", [P, GB, 24]) for st in both}
        cw = {st: sb(f"cw_{st}", [P, GB, 16]) for st in both}
        cwr = {st: sb(f"cwr_{st}", [P, GB, 16]) for st in both}
        cw3 = {st: sb(f"cw3_{st}", [P, GB, P], BF16) for st in both}
        cw3_t = {"mix": sb("cw3_t_mix", [3 * EA, T], BF16), "ffn": sb("cw3_t_ffn", [3 * ED, T], BF16)}
        gate_s = sb("gate_s", [P, 2, T])
        hid = sb("hid", [P, 5, T])
        y_n = sb("y_n", [P, GB, P])
        xy = sb("xy", [P, GB, P])
        xn_t = sb("xn_t", [P, GB, TAPS - 1 + P])
        u_c = sb("u_c", [P, 2, T])
        res_s = sb("res_s", [P, 2, T])
        bc3 = sb("bc3", [96, T], BF16)
        bc_dt = sb("bc_dt", [104, T])
        bc_r, dt_s = bc_dt[0:64, :], bc_dt[96:104, :]
        delta = sb("delta", [P, 2, T])
        du = sb("du", [P, 2, T])
        decay = sb("decay", [P, 2, 2 * T])
        chain = sb("chain", [P, 3, 2 * T])
        y_sum = sb("y_sum", [P, 2 * T])
        x2_n = sb("x2_n", [P, GB, P])
        x2_kept = sb("x2_kept", [P, GB, P])
        x2n_t = sb("x2n_t", [P, T])
        q_t = sb("q_t", [P, 8, T])
        k_t = sb("k_t", [P, T])
        v_a = sb("v_a", [P, GB, DH + 1])
        s_null = sb("s_null", [P, GB, NH])
        key_mask = sb("key_mask", [P, T], BF16)
        sc = sb("sc", [P, 2, NH, P])
        smax = sb("smax", [P, 2, NH])
        p_null = sb("p_null", [P, 2, NH])
        p_t = sb("p_t", [P, NH, P])
        den = sb("den", [P, NH])
        o_n = sb("o_n", [P, NH, DH])
        o_t = sb("o_t", [P, 8, P])
        a_n = sb("a_n", [P, GB, P])
        xf_t = sb("xf_t", [P, T])
        fh = sb("fh", [P, 4, T])
        ff_t = fh[:, 0, :]
        idn = sc[:, 1, 0, :]
        eb2_r, eb_rest = sc[0:3 * ED, 1, 1, :], sc[0:3 * ED, 1, 2, :]
        null_k = sc[:, 1, 3, 0:DH]
        cond_prod = sc[0:64, 1, 4:6, :].rearrange("p a n -> p (a n)")[:, 0:NB * EA].rearrange("p (b e) -> p b e", b=NB)
        ones_64 = sc[0:64, 1, 6, :]
        null_prod = sc[:, 1, 8:16, :].rearrange("p a n -> p (a n)").rearrange("p (h d) -> p h d", h=NH)
        in_n = sc[:, 0, 0:4, :]
        out_n = sc[:, 0, 4:6, :]
        xp_n = sc[0:104, 0, 6:8, :]
        dtw_n = sc[:, 0, 8:10, 0:104]
        conv_sc = chain[:, 0, :].rearrange("p (k h m) -> p k h m", k=TAPS, h=2)

        loaded = [sem(f"loaded{i}") for i in range(3)]
        consts = sem("consts")
        x_loaded = sem("x_loaded")
        mask_loaded = sem("mask_loaded")
        stored = sem("stored")

        act_set = Steps(sem("act_set"), ["ident_bf", "wt", "wg", "cond", "logits", "a_exp", "a_neg", "conv0", "conv1",
                                         "res", "xp", "dt", "out", "crow", "eb_hi", "eb_mid"])
        dve_set = Steps(sem("dve_set"), ["idn0", "idn1", "sel_bc", "ida0", "ida1", "sel_a", "idd0", "idd1", "sel_d", "prod"]
                        + [f"conv{i}" for i in range(8)] + ["null_p", "null_s"] + [f"wn{i}" for i in range(4)]
                        + ["neg_v", "eb_r", "eb_lo"])
        pe_set = Steps(sem("pe_set"), [use for part in SETUP_USES.values() for use in part])
        pe_s, act_s, dve_s, pool_s = (
            {st: Steps(sem(f"{name}_{st}"), in_order(table, st)) for st in STAGES if st in table}
            for name, table in (("pe", PE_STEPS), ("act", ACT_STEPS), ("dve", DVE_STEPS), ("pool", POOL_STEPS)))
        pe_mix, pe_pre, pe_scan, pe_att, pe_ffn = (pe_s[st] for st in STAGES)
        act_mix, act_pre, act_scan, act_att, act_ffn = (act_s[st] for st in STAGES)
        dve_mix, dve_pre, dve_scan, dve_att, dve_ffn = (dve_s[st] for st in STAGES)
        pool_pre, pool_scan, pool_att = (pool_s[st] for st in ("pre", "scan", "att"))

        released = {
            **{f"s_{n}": (act_set, n) for n in ("conv0", "conv1", "res", "out", "xp", "dt", "crow")},
            "s_small": (act_set, "cond"), "s_cond": (act_set, "logits"),
            "xT": (act_mix, "xT"), "lgA": (dve_mix, "lg"), "cwA": (act_mix, "cw3"),
            **{f"gate{k}": (dve_mix, f"lk{k}") for k in range(5)},
            **{f"up{k}": (dve_mix, f"gu{k}") for k in range(4)}, "up4": (dve_mix, "h4"),
            **{f"wide{k}": (dve_mix, f"h{k}") for k in range(4)},
            "moe": (act_mix, "y"), "xnT": (act_mix, "xnT"),
            **{u: (act_pre, u) for u in ("u0", "u1", "r0", "r1")},
            "bc": (dve_pre, "bc_r"), "d0": (dve_pre, "de0"), "d1": (dve_pre, "de1"),
            "op": (dve_att, "x2"), "xn2T": (act_att, "xnT"), **{f"q{k}": (act_att, f"q{k}") for k in range(8)},
            "k": (act_att, "k"), "v": (act_att, "null"),
            **{f"{w}_{b}": (dve_att, f"{w}_{b}") for b in range(GB) for w in ("s0", "s1", "s2", "s3")},
            **{f"{w}_{b}": (act_att, f"{w}_{b}") for b in range(GB) for w in ("t0", "t1", "t2", "t3", "o0", "o1", "wo")},
            **{f"pv{i}_{b}": (act_att, f"sum{i}_{b}") for b in range(GB) for i in range(3)},
            "xfT": (act_ffn, "xfT"), "lgD": (dve_ffn, "lg"), "cwD": (act_ffn, "cw3"), "z15": (act_ffn, "h15"),
            **{f"z{e}": (act_ffn, f"h{e}") for e in range(ED)}, **{f"cw{e}": (dve_ffn, f"c{e}") for e in range(ED)},
            "fin": (dve_ffn, "out"),
        }

        def stages_of(i):
            return tuple(st for st in STAGES if 0 <= i + SHIFT[st] < NG)

        LOOP = (1, NG - 3)
        assert all(stages_of(i) == STAGES for i in range(*LOOP))
        banks_of = {}
        before = ()
        for i in [*range(-3, LOOP[0] + 1), *range(LOOP[1], NG)]:
            if i == LOOP[0]:
                assert before == body_uses(STAGES)[-WORK:]
            banks_of[i] = WorkBanks([("set", u) for u in SETUP_USES.get(i, [])] + body_uses(stages_of(i)), before)
            before = banks_of[i].last

        def run_bodies(eng, setup, body):
            for i in range(-3, LOOP[0]):
                if setup and i in SETUP_USES:
                    setup(i)
                body(i, banks_of[i], stages_of(i))
            with eng.Fori(*LOOP) as i:
                body(i, banks_of[LOOP[0]], STAGES)
            for i in range(LOOP[1], NG):
                body(i, banks_of[i], stages_of(i))

        block = ctx.enter_context(nc.Block())

        def row(ap):
            return ap.rearrange("(a n) -> a n", a=1)

        ip = A["L0_attn_in_proj_w"]
        xp = A["L0_attn_x_proj_w"]
        wkv = A["L0_cond2_Wkv"]
        wo = A["L0_cond2_Wo"]
        loads = {
            -3: [
                (wt_n[:], A["L0_cond_wt"]),
                (wg_n[:], A["L0_cond_wg"]),
                (cond_n[:], cond_64),
                (w_gate[:], A["L0_cond_w_gate"].rearrange("e h m -> h e m")),
                (w_up[:], A["L0_cond_w_up"].rearrange("e h m -> h e m")),
                (sw_gate[:], A["L0_cond_sw_gate"]),
                (sw_up[:], A["L0_cond_sw_up"]),
                (w_down[:], A["L0_cond_w_down"].rearrange("e m h -> (e m) h").rearrange("(k p) h -> p k h", p=P)),
                (sw_down[:], A["L0_cond_sw_down"]),
                *[(cols[:, i:i + 1], A[name].rearrange("(p a) -> p a", a=1))
                  for i, name in ((6, "L0_attn_ln_g"), (7, "L0_attn_ln_b"))],
            ],
            -2: [
                (in_n, ip.rearrange("(t p) f -> p t f", p=P)),
                (conv_w[:], A["L0_attn_conv_w"].rearrange("(h p) o k -> p h (o k)", p=P)),
                (a_neg[:], A["L0_attn_A_log"].rearrange("(h p) s -> p h s", p=P)),
                *[(xp_n[32 * i:32 * i + 2 * NS], xp[DTR:DTR + 2 * NS, :].rearrange("r (h p) -> r h p", h=2))
                  for i in range(3)],
                (xp_n[96:104], xp[0:DTR, :].rearrange("r (h p) -> r h p", h=2)),
                (dtw_n[:, :, 96:104], A["L0_attn_dt_proj_w"].rearrange("(h p) r -> p h r", p=P)),
                *[(cols[:, i:i + 2], A[name].rearrange("(h p) -> p h", p=P))
                  for i, name in ((0, "L0_attn_conv_b"), (2, "L0_attn_dt_proj_b"), (4, "L0_attn_D"))],
                *[(cols[:, i:i + 1], A[name].rearrange("(p a) -> p a", a=1))
                  for i, name in ((8, "L0_cond2_g_in"), (9, "L0_cond2_g_out"), (10, "L0_ffn_sb1"),
                                  (11, "L0_ffn_sb2"))],
            ],
            -1: [
                (out_n, A["L0_attn_out_proj_w"].rearrange("e (h p) -> e h p", h=2)),
                (w_q[:], A["L0_cond2_Wq"]),
                (w_k2[:, 0, :], wkv[:, 0:DH]),
                (w_k2[:, 1, :], wkv[:, 0:DH]),
                (w_vn[:, 0:DH], wkv[:, DH:2 * DH]),
                (null_k, cond_64[0:1, :].to_broadcast([P, DH])),
                (null_v[0:DH, :], cond_64[1, :].rearrange("(p a) -> p a", a=1)),
                (null_v[DH:P, :], cond_64[1, :].rearrange("(p a) -> p a", a=1)),
                (vn_row[:, 0:DH], cond_64[1:2, :]),
                (r_w[:], A["L0_ffn_router_W"]),
                (r_b[:], row(A["L0_ffn_router_b"])),
                (f_w1[:], A["L0_ffn_eW1"].rearrange("e d h -> d e h")),
                (f_w2[:], A["L0_ffn_eW2"].rearrange("e h d -> h e d")),
                (fs_w1[:], A["L0_ffn_sW1"]),
                (fs_w2[:], A["L0_ffn_sW2"]),
                (f_b1[:], A["L0_ffn_eb1"].rearrange("e h -> h e")),
                *[(eb2_r[ED * i:ED * i + ED, :], A["L0_ffn_eb2"]) for i in range(3)],
            ],
        }
        for quad in range(4):
            h0 = head_at(4 * quad)
            loads[-1].append((bias[:, 4 * quad:4 * quad + 4, :], fside[h0:h0 + 7:2, :, :].rearrange("h i j -> i h j")))
            loads[-1].append((vn_row[:, DH + 4 * quad:DH + 4 * quad + 4],
                              row(A["L0_cond2_null_attn_bias"])[:, h0:h0 + 7:2]))
        for pos in range(NH):
            h = head_at(pos)
            loads[-1].append((w_o[DH * (pos % 2):DH * (pos % 2) + DH, pos // 2, :], wo[h * DH:(h + 1) * DH, :]))

        def all_loaded(part):
            return loaded[part + 3], 16 * len(loads[part])

        CONSTS = 14
        BIAS = CONSTS + 1

        @block.sync
        def _(sp):
            def setup(part):
                with nc.allow_non_contiguous_dma(reason="vectors of a value a partition, once"):
                    for p in {-3: [-3], -2: [-2, -1], -1: []}[part]:
                        for dst, src in loads[p]:
                            sp.dma_start(dst, src).then_inc(loaded[p + 3], 16)

            def body(i, banks, stages):
                if "att" in stages:
                    g = i + SHIFT["att"]
                    if not first(g):
                        sp.wait_ge(*dve_att.at("mask", g - 1))
                    sp.dma_start(mask_u8[:], mask[bass.ds(g * GB, GB), :].rearrange("(o b) s -> o (b s)", o=1)
                                 .to_broadcast([P, T])).then_inc(mask_loaded, 16)
                if "mix" in stages:
                    g = i + SHIFT["mix"]
                    if not first(g):
                        sp.wait_ge(*pool_pre.at("xy", g - 1))
                    sp.dma_start(x_n[:], x[bass.ds(g * GB, GB), :, :].rearrange("b s d -> s b d")
                                 ).then_inc(x_loaded, 16)
                if "ffn" in stages:
                    g = i + SHIFT["ffn"]
                    sp.wait_ge(*dve_ffn.at("out", g))
                    sp.dma_start(out[bass.ds(g * GB, GB), :, :].rearrange("b s d -> s b d"), x2_kept[:]
                                 ).then_inc(stored, 16)

            run_bodies(sp, setup, body)
            sp.wait_ge(stored, 16 * NG)

        @block.gpsimd
        def _(pool):
            pool.memset(ident[:], 0.0).then_inc(consts, 1)
            pool.wait_ge(consts, 1)
            pool.affine_select(out=ident[:], in_=ident[:], compare_op=ALU.not_equal, fill=1.0, base=0,
                               pattern=[[-1, P]], channel_multiplier=1).then_inc(consts, 1)
            for t, v in ((ones_row[:], 1.0), (ones_64, 1.0), (ones_bf[:], 1.0), (eps_col[:], EPS), (pr["mix"][:], SENT),
                         (pr["ffn"][:], SENT), (xn_t[:], 0.0), (cw3["mix"][:], 0.0), (cw3["ffn"][:], 0.0), (v_a[:], 1.0),
                         (decay[:], 0.0), (dtw_n[:, :, 0:96], 0.0)):
                pool.memset(t, v).then_inc(consts, 1)
            pool.wait_ge(*all_loaded(-1))
            pool.affine_select(out=bias[:], in_=bias[:], compare_op=ALU.is_ge, fill=NEG, base=0,
                               pattern=[[0, NH], [-1, P]], channel_multiplier=1).then_inc(consts, 1)

            def body(i, banks, stages):
                for stage, item in SCHEDULE:
                    if stage not in stages or item not in POOL_STEPS.get(stage, {}):
                        continue
                    g = i + SHIFT[stage]
                    if item == "xy":
                        if not first(g):
                            pool.wait_ge(*dve_att.at("x2", g - 1))
                        pool.wait_ge(*act_mix.at("y", g))
                        pool.wait_ge(x_loaded, 16 * (g + 1))
                        pool.tensor_tensor(xy[:], x_n[:], y_n[:], ALU.add).then_inc(*pool_pre.done("xy"))
                    elif stage == "scan":
                        s = int(item[1:])
                        if s == 1:
                            if not first(g):
                                pool.wait_ge(*dve_att.at("yd1", g - 1))
                            pool.wait_ge(*dve_scan.at("read1", g))
                            pool.tensor_tensor(y_sum[:], chain[:, 0, :], chain[:, 1, :],
                                               ALU.add).then_inc(*pool_scan.done("y1"))
                        else:
                            pool.wait_ge(*pool_scan.at(f"y{s - 1}", g))
                            pool.wait_ge(*dve_scan.at(f"read{s}", g))
                            pool.tensor_tensor(y_sum[:], y_sum[:], chain[:, s % 3, :],
                                               ALU.add).then_inc(*pool_scan.done(f"y{s}"))
                    elif item[0] == "V":
                        b = int(item[1:])
                        pool.wait_ge(*dve_att.at(f"rden_{b}", g))
                        pool.tensor_tensor(o_n[:], o_n[:], den[:].unsqueeze(2).to_broadcast([P, NH, DH]),
                                           ALU.mult).then_inc(*pool_att.done(f"on_{b}"))
                    else:
                        b = int(item[1:])
                        s = b % 2
                        pool.wait_ge(*dve_att.at(f"mn_{b}", g))
                        pool.tensor_tensor(p_null[:, s, :], s_null[:, b, :], smax[:, s, :],
                                           ALU.subtract).then_inc(*pool_att.done(f"null_{b}"))
                        pool.tensor_tensor(sc[:, s], sc[:, s], smax[:, s, :].unsqueeze(2).to_broadcast([P, NH, P]),
                                           ALU.subtract).then_inc(*pool_att.done(f"sub_{b}"))

            run_bodies(pool, None, body)

        @block.scalar
        def _(act):
            copy = ACT.Copy
            act.preload_act_table_set("natural_log_exp_and_others")
            flat = conv_t[:].rearrange("p k h m -> p (k h m)")
            copies = {
                -3: [("s_small", "wt", wt_t[:], (slice(0, P), slice(0, EA))),
                     ("s_small", "wg", wg_t[:], (slice(0, 64), slice(128, 128 + EA))),
                     ("s_small", "cond", cond_t[:], (slice(0, 64), slice(256, 256 + NB))),
                     ("s_cond", "logits", cond_logits[:].rearrange("p b e -> p (b e)"), (slice(0, P), slice(0, NB * EA)))],
                -2: [("s_conv0", "conv0", flat[:, 0:512], (slice(0, P), slice(0, 512))),
                     ("s_conv1", "conv1", flat[:, 512:1024], (slice(0, P), slice(0, 512))),
                     ("s_res", "res", res_t[:].rearrange("p h m -> p (h m)"), (slice(0, P), slice(0, 256))),
                     ("s_xp", "xp", xp_t[:].rearrange("p h m -> p (h m)"), (slice(0, P), slice(0, 208))),
                     ("s_dt", "dt", dtw_t[96:104].rearrange("p h m -> p (h m)"), (slice(96, 104), slice(0, 256)))],
                -1: [("s_out", "out", out_t[:].rearrange("p h m -> p (h m)"), (slice(0, P), slice(0, 256))),
                     ("s_crow", "crow", o_row[:], (slice(0, 1), slice(0, P)))],
            }

            def setup(part):
                act.wait_ge(*all_loaded(part))
                if part == -3:
                    act.wait_ge(consts, CONSTS)
                    act.activation(ident_bf[:], ident[:], copy).then_inc(*act_set.done("ident_bf"))
                elif part == -2:
                    act.activation(a_neg[:], a_neg[:], ACT.Exp).then_inc(*act_set.done("a_exp"))
                    act.wait_ge(*act_set.at("a_exp"))
                    act.activation(a_neg[:], a_neg[:], copy, scale=-1.0).then_inc(*act_set.done("a_neg"))
                for use, step, dst, (rows, columns) in copies[part]:
                    act.wait_ge(*pe_set.at(use))
                    act.activation(dst, work[banks_of[part].bank[("set", use)]][rows, columns],
                                   copy).then_inc(*act_set.done(step))
                if part == -1:
                    act.activation(eb2_p[:, 0, :], eb2_r, copy).then_inc(*act_set.done("eb_hi"))
                    act.wait_ge(*dve_set.at("eb_r"))
                    act.activation(eb2_p[:, 1, :], eb_rest, copy).then_inc(*act_set.done("eb_mid"))

            def normalise(stage, g):
                dve, mine = dve_s[stage], act_s[stage]
                act.wait_ge(*dve.at(f"mv{GB - 1}", g))
                act.activation(rstd[stage][:], mv[stage][:, :, 1], ACT.Ln, bias=eps_col[:]).then_inc(*mine.done("lnv"))
                act.wait_ge(*mine.at("lnv", g))
                act.activation(rstd[stage][:], rstd[stage][:], ACT.Exp, scale=-0.5).then_inc(*mine.done("rstd"))

            def weights_t(stage, use, n, src, g):
                act.wait_ge(*pe_s[stage].at(use, g))
                act.activation(cw3_t[stage][:], src[:].bitcast(BF16)[0:n, 0:T], copy).then_inc(*act_s[stage].done("cw3"))

            def mix(item, g, out_of):
                if item == "xT":
                    act.wait_ge(*pe_mix.at("xT", g))
                    act.activation(x_t[:], out_of("xT")[:], copy).then_inc(*act_mix.done("xT"))
                elif item == "router":
                    act.wait_ge(*dve_mix.at("ls", g))
                    act.activation(pr["mix"][:, :, 0:EA], lg["mix"][:, :, 0:EA], ACT.Exp,
                                   scale=0.5).then_inc(*act_mix.done("exp"))
                elif item == "cwA":
                    weights_t("mix", "cwA", 3 * EA, out_of("cwA"), g)
                elif item in ("m0", "m1", "m2", "m3", "m4"):
                    k = int(item[1:])
                    act.wait_ge(*pe_mix.at(f"gate{k}", g))
                    if k >= 2:
                        act.wait_ge(*dve_mix.at(f"h{k - 2}", g))
                    act.activation(gate_s[:, k % 2, :], out_of(f"gate{k}")[:],
                                   copy).then_inc(*act_mix.done(f"gate{k}"))
                elif item == "moe":
                    act.wait_ge(*pe_mix.at("moe", g))
                    if not first(g):
                        act.wait_ge(*pool_pre.at("xy", g - 1))
                    act.activation(y_n[:].rearrange("p b d -> p (b d)"), out_of("moe")[:],
                                   copy).then_inc(*act_mix.done("y"))
                elif item == "norm":
                    normalise("mix", g)
                elif item == "xnT":
                    act.wait_ge(*pe_mix.at("xnT", g))
                    act.activation(xn_t[:, :, TAPS - 1:], out_of("xnT")[:].rearrange("p (b s) -> p b s", b=GB),
                                   ACT.Identity, scale=ln_g, bias=ln_b).then_inc(*act_mix.done("xnT"))

            def pre(item, g, out_of):
                if item in ("su0", "su1"):
                    h = int(item[2:])
                    if h == 0 and not first(g):
                        act.wait_ge(*pe_att.at("op", g - 1))
                    act.wait_ge(*pe_pre.at(f"u{h}", g))
                    act.activation(u_c[:, h, :], out_of(f"u{h}")[:], ACT.Silu,
                                   bias=conv_b[:, h:h + 1]).then_inc(*act_pre.done(f"u{h}"))
                elif item in ("r0", "r1"):
                    h = int(item[1:])
                    act.wait_ge(*pe_pre.at(f"r{h}", g))
                    act.activation(res_s[:, h, :], out_of(f"r{h}")[:], ACT.Silu).then_inc(*act_pre.done(f"r{h}"))
                    if h == 1:
                        act.preload_act_table_set("natural_log_exp_and_others")
                elif item == "bc":
                    act.wait_ge(*pe_pre.at("bc", g))
                    act.activation(bc3[:], out_of("bc")[0:96, :], copy).then_inc(*act_pre.done("bc_hi"))
                    act.activation(dt_s, out_of("bc")[96:104, :], copy).then_inc(*act_pre.done("dt"))
                    act.wait_ge(*dve_pre.at("bc_r", g))
                    act.activation(bc3[0:64, :], bc_r, copy).then_inc(*act_pre.done("bc_mid"))
                elif item == "sp":
                    for h in range(2):
                        act.wait_ge(*dve_pre.at(f"cl{h}", g))
                        act.activation(delta[:, h, :], delta[:, h, :], ACT.Exp).then_inc(*act_pre.done(f"e{h}"))
                        act.wait_ge(*act_pre.at(f"e{h}", g))
                        act.activation(delta[:, h, :], delta[:, h, :], ACT.Ln, bias=1.0).then_inc(*act_pre.done(f"sp{h}"))

            def scan(item, g, out_of):
                if item not in ACT_STEPS["scan"]:
                    return
                s = 0 if item == "start" else int(item[1:]) + 1
                if s == 0:
                    act.wait_ge(*dve_pre.at("de1", g))
                if s >= 2:
                    act.wait_ge(*dve_scan.at(f"state{s - 2}", g))
                elif not first(g):
                    act.wait_ge(*dve_scan.at(f"state{NS - 2 + s}", g - 1))
                for h in range(2):
                    view = decay[:, s % 2, h * T:(h + 1) * T].rearrange("p (b l) -> p b l", b=GB)
                    ins = act.activation(view[:, :, 1:], delta[:, h, :].rearrange("p (b l) -> p b l", b=GB)[:, :, 1:],
                                         ACT.Exp, scale=a_neg[:, h, s:s + 1])
                ins.then_inc(*act_scan.done(f"decay{s}"))

            def att(item, g, out_of):
                if item == "norm":
                    normalise("att", g)
                elif item == "xn2T":
                    act.wait_ge(*pe_att.at("xn2T", g))
                    act.activation(x2n_t[:], out_of("xn2T")[:], copy, scale=g_in).then_inc(*act_att.done("xnT"))
                elif item[0] == "q":
                    k = int(item[1:])
                    act.wait_ge(*pe_att.at(f"q{k}", g))
                    act.activation(q_t[:, k, :], out_of(f"q{k}")[:], copy,
                                   scale=DH ** -0.5).then_inc(*act_att.done(f"q{k}"))
                elif item == "k":
                    act.wait_ge(*pe_att.at("k", g))
                    act.activation(k_t[:], out_of("k")[:], copy).then_inc(*act_att.done("k"))
                elif item == "v":
                    act.wait_ge(*pe_att.at("v", g))
                    vn = out_of("v")[:, 0:GB * (DH + NH)].rearrange("p (b n) -> p b n", b=GB)
                    act.activation(v_a[:, :, 0:DH], vn[:, :, 0:DH], copy).then_inc(*act_att.done("v"))
                    act.activation(s_null[:], vn[:, :, DH:], copy).then_inc(*act_att.done("null"))
                elif item[0] == "P":
                    b = int(item[1:])
                    s = b % 2
                    act.wait_ge(*pool_att.at(f"sub_{b}", g))
                    act.activation(sc[:, s], sc[:, s], ACT.Exp).then_inc(*act_att.done(f"p_{b}"))
                    act.activation(p_null[:, s, :], p_null[:, s, :], ACT.Exp).then_inc(*act_att.done(f"pn_{b}"))
                elif item[0] == "T":
                    b = int(item[1:])
                    for i in range(4):
                        act.wait_ge(*pe_att.at(f"t{i}_{b}", g))
                        act.activation(p_t[:, 4 * i:4 * i + 4, :].rearrange("p h i -> p (h i)"),
                                       out_of(f"t{i}_{b}")[:], copy).then_inc(*act_att.done(f"t{i}_{b}"))
                elif item[0] == "V":
                    b = int(item[1:])
                    if b or not first(g):
                        act.wait_ge(*pe_att.at(f"o1_{(b - 1) % GB}", g if b else g - 1))
                    for i, (h0, h1) in enumerate(PV_HEADS):
                        act.wait_ge(*pe_att.at(f"pv{i}_{b}", g))
                        pv = out_of(f"pv{i}_{b}")[:, 0:(h1 - h0) * (DH + 1)].rearrange("p (h d) -> p h d", h=h1 - h0)
                        act.activation(o_n[:, h0:h1, :], pv[:, :, 0:DH], copy).then_inc(*act_att.done(f"pv{i}_{b}"))
                        act.activation(den[:, h0:h1], pv[:, :, DH], copy).then_inc(*act_att.done(f"sum{i}_{b}"))
                elif item[0] == "O":
                    b = int(item[1:])
                    for i in range(2):
                        act.wait_ge(*pe_att.at(f"o{i}_{b}", g))
                        act.activation(o_t[:, 4 * i:4 * i + 4, :].rearrange("p k i -> p (k i)"),
                                       out_of(f"o{i}_{b}")[:], copy).then_inc(*act_att.done(f"o{i}_{b}"))
                elif item[0] == "W":
                    b = int(item[1:])
                    act.wait_ge(*pe_att.at(f"wo_{b}", g))
                    act.activation(a_n[:, b, :], out_of(f"wo_{b}")[:, 0:P], copy).then_inc(*act_att.done(f"wo_{b}"))

            def ffn(item, g, out_of):
                if item == "keep":
                    if not first(g):
                        act.wait_ge(stored, 16 * g)
                    act.wait_ge(*dve_att.at("x2", g))
                    act.activation(x2_kept[:], x2_n[:], copy).then_inc(*act_ffn.done("keep"))
                elif item == "norm":
                    normalise("ffn", g)
                elif item == "xfT":
                    act.wait_ge(*pe_ffn.at("xfT", g))
                    act.activation(xf_t[:], out_of("xfT")[:], copy, scale=g_out).then_inc(*act_ffn.done("xfT"))
                elif item == "router":
                    act.wait_ge(*dve_ffn.at("ls", g))
                    act.activation(pr["ffn"][:, :, 0:ED], lg["ffn"][:, :, 0:ED], ACT.Exp).then_inc(*act_ffn.done("exp"))
                elif item == "cwD":
                    weights_t("ffn", "cwD", 3 * ED, out_of("cwD"), g)
                elif item == "z15":
                    act.wait_ge(*pe_ffn.at("z15", g))
                    act.activation(fh[:, 3, :], out_of("z15")[:], ACT.Relu, bias=sb1).then_inc(*act_ffn.done("h15"))
                elif item in FFN_EXPERTS:
                    e = int(item[1:])
                    act.wait_ge(*pe_ffn.at(f"z{e}", g))
                    if e >= 3:
                        act.wait_ge(*pe_ffn.at(f"acc{e - 3}", g))
                    elif e == 0 and not first(g):
                        act.wait_ge(*pe_ffn.at("fin", g - 1))
                    act.activation(fh[:, e % 3, :], out_of(f"z{e}")[:], ACT.Relu,
                                   bias=f_b1[:, e:e + 1]).then_inc(*act_ffn.done(f"h{e}"))
                elif item == "fin":
                    act.wait_ge(*pe_ffn.at("acc14", g))
                    act.activation(ff_t, ffn_sum[:], ACT.Identity, bias=sb2).then_inc(*act_ffn.done("ff"))

            todo = {"mix": mix, "pre": pre, "scan": scan, "att": att, "ffn": ffn}

            def body(i, banks, stages):
                for stage, item in SCHEDULE:
                    if stage in stages:
                        todo[stage](item, i + SHIFT[stage], lambda use: work[banks.bank[(stage, use)]])

            run_bodies(act, setup, body)

        @block.vector
        def _(dve):
            def setup(part):
                dve.wait_ge(*all_loaded(part))
                {-3: setup_mix, -2: setup_scan, -1: setup_last}[part]()

            def setup_mix():
                dve.wait_ge(consts, CONSTS)
                for tag, n, sel, width in (("n", 32, sel_bc[:], 0), ("a", EA, sel_a[:], 64), ("d", ED, sel_d[0:3 * ED, :], 0)):
                    dve.tensor_tensor(idn[0:3 * n, 0:n], ident[0:3 * n, 0:n], ident[0:3 * n, n:2 * n],
                                      ALU.add).then_inc(*dve_set.done(f"id{tag}0"))
                    dve.wait_ge(*dve_set.at(f"id{tag}0"))
                    dve.tensor_tensor(idn[0:3 * n, 32:32 + n], idn[0:3 * n, 0:n], ident[0:3 * n, 2 * n:3 * n],
                                      ALU.add).then_inc(*dve_set.done(f"id{tag}1"))
                    dve.wait_ge(*dve_set.at(f"id{tag}1"))
                    src = idn[0:3 * n, 32:32 + n]
                    name = {"n": "sel_bc", "a": "sel_a", "d": "sel_d"}[tag]
                    dve.tensor_copy(sel, src.unsqueeze(2).to_broadcast([3 * n, n, width]) if width else src
                                    ).then_inc(*dve_set.done(name))
                    dve.wait_ge(*dve_set.at(name))
                dve.wait_ge(*act_set.at("cond"))
                dve.tensor_tensor(cond_prod, cond_t[:].unsqueeze(2).to_broadcast([64, NB, EA]),
                                  wg_t[:].unsqueeze(1).to_broadcast([64, NB, EA]), ALU.mult).then_inc(*dve_set.done("prod"))

            def setup_scan():
                for i in range(8):
                    k, h = divmod(i, 2)
                    dve.tensor_scalar(conv_sc[:, k, h, :], in_n[:, h, :], conv_w[:, h, k:k + 1], None,
                                      ALU.mult).then_inc(*dve_set.done(f"conv{i}"))

            def setup_last():
                dve.wait_ge(consts, BIAS)
                dve.tensor_tensor(null_prod, w_q[:].rearrange("p (h d) -> p h d", h=NH),
                                  null_k.unsqueeze(1).to_broadcast([P, NH, DH]), ALU.mult).then_inc(*dve_set.done("null_p"))
                dve.wait_ge(*dve_set.at("null_p"))
                dve.tensor_reduce(null_sum[:], null_prod, AX.X, ALU.add).then_inc(*dve_set.done("null_s"))
                dve.wait_ge(*dve_set.at("null_s"))
                for quad in range(4):
                    h0 = head_at(4 * quad)
                    dve.tensor_scalar(w_vn[:, DH + 4 * quad:DH + 4 * quad + 4], null_sum[:, h0:h0 + 7:2], DH ** -0.5, None,
                                      ALU.mult).then_inc(*dve_set.done(f"wn{quad}"))
                dve.tensor_scalar(vn_row[:, 0:DH], vn_row[:, 0:DH], -1.0, None, ALU.mult).then_inc(*dve_set.done("neg_v"))
                dve.wait_ge(*act_set.at("eb_hi"))
                dve.tensor_tensor(eb_rest, eb2_r, eb2_p[:, 0, :], ALU.subtract).then_inc(*dve_set.done("eb_r"))
                dve.wait_ge(*act_set.at("eb_mid"))
                dve.tensor_tensor(eb2_p[:, 2, :], eb_rest, eb2_p[:, 1, :], ALU.subtract).then_inc(*dve_set.done("eb_lo"))

            def normalise(stage, src, g, gaps):
                mine, others = dve_s[stage], act_s[stage]
                for b in range(GB):
                    dve.bn_stats(stats[stage][:, b, :], src[:, b, :]).then_inc(*mine.done(f"st{b}"))
                dve.wait_ge(*mine.at(f"st{GB - 1}", g))
                dve.memset(gap[:, gaps:gaps + 1], 0.0)
                for b in range(GB):
                    dve.bn_aggr(mv[stage][:, b, :], stats[stage][:, b, :]).then_inc(*mine.done(f"mv{b}"))
                dve.wait_ge(*others.at("rstd", g))
                for b in range(GB):
                    dve.tensor_scalar(xn_n[stage][:, b, :], src[:, b, :], mv[stage][:, b, 0:1], rstd[stage][:, b:b + 1],
                                      ALU.subtract, ALU.mult).then_inc(*mine.done(f"xn{b}"))

            def router(stage, g, E, K, gaps):
                mine, others = dve_s[stage], act_s[stage]
                lg_, mx_, pr_, top_, rest_, zs_, cw_, cwr_, cw3_ = (
                    t[stage] for t in (lg, mx, pr, top8, rest, zs, cw, cwr, cw3))
                w = pr_.shape[2]
                dve.wait_ge(*mine.at("lg", g))
                dve.tensor_reduce(mx_[:], lg_[:, :, 0:E], AX.X, ALU.max).then_inc(*mine.done("mx"))
                dve.wait_ge(*mine.at("mx", g))
                dve.tensor_tensor(lg_[:, :, 0:E], lg_[:, :, 0:E], mx_[:].unsqueeze(2).to_broadcast([P, GB, E]),
                                  ALU.subtract).then_inc(*mine.done("ls"))
                dve.wait_ge(*others.at("exp", g))
                dve.memset(gap[:, gaps:gaps + 1], 0.0)
                for b in range(GB):
                    dve.max(top_[:, b, :], pr_[:, b, :]).then_inc(*mine.done(f"top{b}"))
                dve.wait_ge(*mine.at(f"top{GB - 1}", g))
                dve.memset(top_[:, :, K:8], SENT).then_inc(*mine.done("cut"))
                dve.wait_ge(*mine.at("cut", g))
                dve.memset(gap[:, gaps + 1:gaps + 2], 0.0)
                for b in range(GB):
                    dve.match_replace(rest_[:, b, 0:w], top_[:, b, :], pr_[:, b, :], 0.0).then_inc(*mine.done(f"rest{b}"))
                dve.wait_ge(*mine.at(f"rest{GB - 1}", g))
                dve.tensor_tensor(cw_[:, :, 0:E], pr_[:, :, 0:E], rest_[:, :, 0:E], ALU.subtract).then_inc(*mine.done("sel"))
                dve.tensor_reduce(zs_[:], pr_[:, :, 0:E], AX.X, ALU.add).then_inc(*mine.done("z"))
                if K == KA:
                    dve.wait_ge(*mine.at("z", g))
                    dve.tensor_reduce(ds_[:], cw_[:, :, 0:E], AX.X, ALU.add).then_inc(*mine.done("d"))
                    dve.wait_ge(*mine.at("d", g))
                    dve.scalar_tensor_tensor(out=zs_[:], in0=zs_[:], scalar=1e-20, in1=ds_[:], op0=ALU.mult,
                                             op1=ALU.add).then_inc(*mine.done("ds"))
                dve.wait_ge(*mine.at("ds" if K == KA else "z", g))
                dve.reciprocal(zs_[:], zs_[:]).then_inc(*mine.done("ri"))
                dve.wait_ge(*mine.at("ri", g))
                dve.tensor_tensor(cw_[:, :, 0:E], cw_[:, :, 0:E], zs_[:].unsqueeze(2).to_broadcast([P, GB, E]),
                                  ALU.mult).then_inc(*mine.done("cw"))
                dve.wait_ge(*mine.at("cw", g))
                dve.tensor_copy(cw3_[:, :, 0:E], cw_[:, :, 0:E]).then_inc(*mine.done("hi"))
                dve.wait_ge(*mine.at("hi", g))
                dve.tensor_tensor(cwr_[:, :, 0:E], cw_[:, :, 0:E], cw3_[:, :, 0:E], ALU.subtract).then_inc(*mine.done("r"))
                dve.wait_ge(*mine.at("r", g))
                dve.tensor_copy(cw3_[:, :, E:2 * E], cwr_[:, :, 0:E]).then_inc(*mine.done("mid"))
                dve.wait_ge(*mine.at("mid", g))
                dve.tensor_tensor(cw3_[:, :, 2 * E:3 * E], cwr_[:, :, 0:E], cw3_[:, :, E:2 * E],
                                  ALU.subtract).then_inc(*mine.done("lo"))

            def mix(item, g, out_of):
                if item == "lgA":
                    dve.wait_ge(*pe_mix.at("lgA", g))
                    dve.tensor_tensor(lg["mix"][:, :, 0:EA], out_of("lgA")[:, 0:GB * EA].rearrange("p (b e) -> p b e", b=GB),
                                      cond_logits[:, bass.ds(g * GB, GB), :], ALU.add).then_inc(*dve_mix.done("lg"))
                elif item == "router":
                    router("mix", g, EA, KA, 3)
                elif item in ("m0", "m1", "m2", "m3", "m4"):
                    k = int(item[1:])
                    dve.wait_ge(*act_mix.at(f"gate{k}", g))
                    dve.scalar_tensor_tensor(out=gate_s[:, k % 2, :], in0=out_of(f"gate{k}")[:], scalar=LEAK,
                                             in1=gate_s[:, k % 2, :], op0=ALU.mult,
                                             op1=ALU.max).then_inc(*dve_mix.done(f"lk{k}"))
                    dve.wait_ge(*dve_mix.at(f"lk{k}", g))
                    dve.wait_ge(*pe_mix.at(f"up{k}", g))
                    dst = gate_s[:, k % 2, :] if k < 4 else hid[:, 4, :]
                    dve.tensor_tensor(dst, gate_s[:, k % 2, :], out_of(f"up{k}")[:],
                                      ALU.mult).then_inc(*dve_mix.done(f"gu{k}" if k < 4 else "h4"))
                    if k < 4:
                        dve.wait_ge(*dve_mix.at(f"gu{k}", g))
                        dve.wait_ge(*pe_mix.at(f"wide{k}", g))
                        dve.tensor_tensor(hid[:, k, :], gate_s[:, k % 2, :], out_of(f"wide{k}")[:],
                                          ALU.mult).then_inc(*dve_mix.done(f"h{k}"))
                elif item == "norm":
                    dve.wait_ge(*act_mix.at("y", g))
                    normalise("mix", y_n, g, 0)

            def pre(item, g, out_of):
                if item == "bc":
                    dve.wait_ge(*act_pre.at("dt", g))
                    dve.tensor_tensor(bc_r, out_of("bc")[0:64, :], bc3[0:64, :],
                                      ALU.subtract).then_inc(*dve_pre.done("bc_r"))
                    dve.wait_ge(*act_pre.at("bc_mid", g))
                    dve.tensor_tensor(bc3[0:32, :], bc_dt[0:32, :], bc3[0:32, :],
                                      ALU.subtract).then_inc(*dve_pre.done("bc_lo"))
                elif item == "d":
                    for h in range(2):
                        dve.wait_ge(*pe_pre.at(f"d{h}", g))
                        dve.tensor_scalar(delta[:, h, :], out_of(f"d{h}")[:], dt_b[:, h:h + 1], CLAMP, ALU.add,
                                          ALU.min).then_inc(*dve_pre.done(f"cl{h}"))
                elif item == "sp":
                    for h in range(2):
                        dve.wait_ge(*act_pre.at(f"sp{h}", g))
                        dve.scalar_tensor_tensor(out=delta[:, h, :], in0=out_of(f"d{h}")[:], scalar=dt_b[:, h:h + 1],
                                                 in1=delta[:, h, :], op0=ALU.add,
                                                 op1=ALU.max).then_inc(*dve_pre.done(f"de{h}"))
                    dve.wait_ge(*dve_pre.at("de1", g))
                    dve.tensor_tensor(du[:], delta[:], u_c[:], ALU.mult).then_inc(*dve_pre.done("du"))

            def scan(item, g, out_of):
                def drive_of(s):
                    dve.wait_ge(*pe_scan.at(f"b{s}", g))
                    if s >= 3:
                        dve.wait_ge(*pool_scan.at(f"y{max(s - 3, 1)}", g))
                    dve.tensor_tensor(chain[:, s % 3, :].rearrange("p (h t) -> p h t", h=2), du[:],
                                      b_wide[:].unsqueeze(1).to_broadcast([P, 2, T]),
                                      ALU.mult).then_inc(*dve_scan.done(f"drive{s}"))

                if item == "start":
                    dve.wait_ge(*dve_pre.at("du", g))
                    drive_of(0)
                elif item[0] == "h":
                    s = int(item[1:])
                    dve.wait_ge(*dve_scan.at(f"drive{s}", g))
                    dve.wait_ge(*act_scan.at(f"decay{s}", g))
                    dve.tensor_tensor_scan(chain[:, s % 3, :], decay[:, s % 2, :], chain[:, s % 3, :], 0.0,
                                           ALU.mult, ALU.add).then_inc(*dve_scan.done(f"state{s}"))
                elif item[0] == "d":
                    if int(item[1:]) + 1 < NS:
                        drive_of(int(item[1:]) + 1)
                else:
                    s = int(item[1:])
                    dve.wait_ge(*dve_scan.at(f"state{s}", g))
                    dve.wait_ge(*pe_scan.at(f"c{s}", g))
                    dve.tensor_tensor(chain[:, s % 3, :].rearrange("p (h t) -> p h t", h=2),
                                      chain[:, s % 3, :].rearrange("p (h t) -> p h t", h=2),
                                      c_wide[:].unsqueeze(1).to_broadcast([P, 2, T]),
                                      ALU.mult).then_inc(*dve_scan.done(f"read{s}"))

            def maxima(b, s, i, g):
                dve.wait_ge(*dve_att.at(f"s{i}_{b}", g))
                dve.tensor_reduce(smax[:, s, 4 * i:4 * i + 4], sc[:, s, 4 * i:4 * i + 4, :], AX.X,
                                  ALU.max).then_inc(*dve_att.done(f"mx{i}_{b}"))

            def att(item, g, out_of):
                if item == "end":
                    dve.wait_ge(*pool_scan.at(f"y{NS - 1}", g))
                    for h in range(2):
                        dve.scalar_tensor_tensor(out=u_c[:, h, :], in0=u_c[:, h, :], scalar=d_skip[:, h:h + 1],
                                                 in1=y_sum[:, h * T:(h + 1) * T], op0=ALU.mult,
                                                 op1=ALU.add).then_inc(*dve_att.done(f"yd{h}"))
                    dve.wait_ge(*dve_att.at("yd1", g))
                    dve.tensor_tensor(u_c[:], u_c[:], res_s[:], ALU.mult).then_inc(*dve_att.done("yg"))
                elif item == "op":
                    dve.wait_ge(*pe_att.at("op", g))
                    dve.wait_ge(*pool_pre.at("xy", g))
                    if not first(g):
                        dve.wait_ge(*act_ffn.at("keep", g - 1))
                    dve.tensor_tensor(x2_n[:], out_of("op")[:].rearrange("p (b d) -> p b d", b=GB), xy[:],
                                      ALU.add).then_inc(*dve_att.done("x2"))
                elif item == "norm":
                    dve.wait_ge(*dve_att.at("x2", g))
                    normalise("att", x2_n, g, 1)
                elif item == "v":
                    dve.wait_ge(mask_loaded, 16 * (g + 1))
                    dve.tensor_scalar(key_mask[:], mask_u8[:], -1.0, -NEG, ALU.add,
                                      ALU.mult).then_inc(*dve_att.done("mask"))
                elif item[0] == "S":
                    b = int(item[1:])
                    s = b % 2
                    for i in range(4):
                        dve.wait_ge(*pe_att.at(f"s{i}_{b}", g))
                        dve.tensor_tensor(sc[:, s, 4 * i:4 * i + 4, :],
                                          out_of(f"s{i}_{b}")[:].rearrange("p (h j) -> p h j", h=4),
                                          bias[:, 4 * i:4 * i + 4, :], ALU.add).then_inc(*dve_att.done(f"s{i}_{b}"))
                        if i:
                            maxima(b, s, i - 1, g)
                    maxima(b, s, 3, g)
                    dve.wait_ge(*dve_att.at(f"mx3_{b}", g))
                    dve.wait_ge(*act_att.at("null", g))
                    dve.tensor_tensor(smax[:, s, :], smax[:, s, :], s_null[:, b, :],
                                      ALU.max).then_inc(*dve_att.done(f"mn_{b}"))
                elif item[0] == "V":
                    b = int(item[1:])
                    dve.wait_ge(*act_att.at(f"sum2_{b}", g))
                    dve.tensor_tensor(den[:], den[:], p_null[:, b % 2, :],
                                      ALU.add).then_inc(*dve_att.done(f"den_{b}"))
                    dve.wait_ge(*dve_att.at(f"den_{b}", g))
                    dve.reciprocal(den[:], den[:]).then_inc(*dve_att.done(f"rden_{b}"))

            def ffn(item, g, out_of):
                if item == "norm":
                    dve.wait_ge(*act_att.at(f"wo_{GB - 1}", g))
                    normalise("ffn", a_n, g, 2)
                elif item == "lgD":
                    dve.wait_ge(*pe_ffn.at("lgD", g))
                    dve.tensor_copy(lg["ffn"][:, :, 0:ED],
                                    out_of("lgD")[:, 0:GB * ED].rearrange("p (b e) -> p b e", b=GB)
                                    ).then_inc(*dve_ffn.done("lg"))
                elif item == "router":
                    router("ffn", g, ED, KD, 5)
                elif item in FFN_EXPERTS:
                    e = int(item[1:])
                    dve.wait_ge(*act_ffn.at(f"h{e}", g))
                    dve.wait_ge(*pe_ffn.at(f"cw{e}", g))
                    dve.tensor_tensor(fh[:, e % 3, :], fh[:, e % 3, :], out_of(f"cw{e}")[:],
                                      ALU.mult).then_inc(*dve_ffn.done(f"c{e}"))
                elif item == "fin":
                    dve.wait_ge(*pe_ffn.at("fin", g))
                    dve.wait_ge(*act_ffn.at("keep", g))
                    dve.tensor_tensor(x2_kept[:], out_of("fin")[:].rearrange("p (b d) -> p b d", b=GB), x2_kept[:],
                                      ALU.add).then_inc(*dve_ffn.done("out"))

            todo = {"mix": mix, "pre": pre, "scan": scan, "att": att, "ffn": ffn}

            def body(i, banks, stages):
                for stage, item in SCHEDULE:
                    if stage in stages:
                        todo[stage](item, i + SHIFT[stage], lambda use: work[banks.bank[(stage, use)]])

            run_bodies(dve, setup, body)

        @block.tensor
        def _(pe):
            def take(i, banks, stage, use):
                if banks.prev[(stage, use)]:
                    (before, name), between = banks.prev[(stage, use)]
                    steps, step = released[name]
                    pe.wait_ge(*steps.at(step, 0 if before == "set" else i + SHIFT[before] - between))
                return work[banks.bank[(stage, use)]]

            def transposes(part, use, items):
                o = set_claim(part, use)
                for dst, src, n in items(o):
                    ins = pe.transpose(dst, src, ident[0:n, 0:n])
                ins.then_inc(*pe_set.done(use))

            def set_claim(part, use):
                return take(part, banks_of[part], "set", use)

            def setup(part):
                pe.wait_ge(*all_loaded(part))
                if part == -3:
                    pe.wait_ge(consts, CONSTS)
                    transposes(part, "s_small", lambda o: ((o[:, 0:EA], wt_n[:], EA), (o[0:64, 128:128 + EA], wg_n[:], EA),
                                                           (o[0:64, 256:256 + NB], cond_n[:], NB)))
                    o = set_claim(part, "s_cond")
                    pe.wait_ge(*dve_set.at("prod"))
                    pe.matmul(o[:, 0:NB * EA], ones_64, cond_prod.rearrange("p b e -> p (b e)"), start=True,
                              stop=True).then_inc(*pe_set.done("s_cond"))
                elif part == -2:
                    for i in range(2):
                        pe.wait_ge(*dve_set.at(f"conv{4 * i + 3}"))
                        transposes(part, f"s_conv{i}", lambda o: [
                            (o[:, j * P:(j + 1) * P], conv_sc[:, (4 * i + j) // 2, (4 * i + j) % 2, :], P)
                            for j in range(4)])
                    transposes(part, "s_res", lambda o: [(o[:, h * P:(h + 1) * P], in_n[:, 2 + h, :], P) for h in range(2)])
                    transposes(part, "s_xp", lambda o: [(o[:, h * 104:(h + 1) * 104], xp_n[:, h, :], 104)
                                                        for h in range(2)])
                    transposes(part, "s_dt", lambda o: [(o[0:104, h * P:(h + 1) * P], dtw_n[:, h, :], P)
                                                        for h in range(2)])
                    pe.wait_ge(*act_set.at("dt"))
                else:
                    transposes(part, "s_out", lambda o: [(o[:, h * P:(h + 1) * P], out_n[:, h, :], P) for h in range(2)])
                    o = set_claim(part, "s_crow")
                    for k in range(8):
                        ins = pe.matmul(o[0:1, 0:P], null_v[:], w_o[:, k, :], start=(k == 0), stop=(k == 7))
                    ins.then_inc(*pe_set.done("s_crow"))
                    pe.wait_ge(*act_set.at("eb_mid"))
                    pe.wait_ge(*dve_set.at("eb_lo"))

            def seq(t, b):
                return t[:, b * P:(b + 1) * P]

            def to_features(o, src):
                for b in range(GB):
                    ins = pe.transpose(seq(o, b), src[:, b, :], ident[:])
                return ins

            def parts_to_rows(o, parts):
                for b in range(GB):
                    ins = pe.transpose(o[:].bitcast(BF16)[:, b * P:(b + 1) * P], parts[:, b, :], ident_bf[:])
                return ins

            def product(o, lhsT, rhs):
                return pe.matmul(o[:], lhsT, rhs, start=True, stop=True)

            def mix(item, g, claim):
                if item == "xT":
                    pe.wait_ge(x_loaded, 16 * (g + 1))
                    to_features(claim("xT"), x_n).then_inc(*pe_mix.done("xT"))
                elif item == "lgA":
                    o = claim("lgA")
                    pe.wait_ge(*act_mix.at("xT", g))
                    for b in range(GB):
                        ins = pe.matmul(o[:, b * EA:(b + 1) * EA], seq(x_t, b), wt_t[:], start=True, stop=True)
                    ins.then_inc(*pe_mix.done("lgA"))
                elif item == "cwA":
                    o = claim("cwA")
                    pe.wait_ge(*dve_mix.at("lo", g))
                    parts_to_rows(o, cw3["mix"]).then_inc(*pe_mix.done("cwA"))
                elif item in ("m0", "m1", "m2", "m3"):
                    k = int(item[1:])
                    pair = slice(2 * k, 2 * k + 2)
                    product(claim(f"gate{k}"), w_gate[:, pair, :].rearrange("p e m -> p (e m)"),
                            x_t[:]).then_inc(*pe_mix.done(f"gate{k}"))
                    product(claim(f"up{k}"), w_up[:, pair, :].rearrange("p e m -> p (e m)"),
                            x_t[:]).then_inc(*pe_mix.done(f"up{k}"))
                    o = claim(f"wide{k}")
                    pe.wait_ge(*act_mix.at("cw3", g))
                    product(o, sel_a[:, pair, :].rearrange("p e m -> p (e m)"),
                            cw3_t["mix"][:]).then_inc(*pe_mix.done(f"wide{k}"))
                elif item == "m4":
                    product(claim("gate4"), sw_gate[:], x_t[:]).then_inc(*pe_mix.done("gate4"))
                    product(claim("up4"), sw_up[:], x_t[:]).then_inc(*pe_mix.done("up4"))
                elif item == "moe":
                    o = claim("moe")
                    pe.wait_ge(*dve_mix.at("h4", g))
                    for b in range(GB):
                        for k in range(5):
                            ins = pe.matmul(seq(o, b), hid[:, k, b * P:(b + 1) * P],
                                            w_down[:, k, :] if k < 4 else sw_down[:], start=(k == 0), stop=(k == 4))
                    ins.then_inc(*pe_mix.done("moe"))
                elif item == "xnT":
                    o = claim("xnT")
                    pe.wait_ge(*dve_mix.at(f"xn{GB - 1}", g))
                    to_features(o, xn_n["mix"]).then_inc(*pe_mix.done("xnT"))

            def pre(item, g, claim):
                if item in ("u0", "u1"):
                    h = int(item[1:])
                    o = claim(item)
                    pe.wait_ge(*act_mix.at("xnT", g))
                    for k in range(TAPS):
                        ins = pe.matmul(o[:].rearrange("p (b s) -> p b s", b=GB), conv_t[:, k, h, :],
                                        xn_t[:, :, k:k + P], start=(k == 0), stop=(k == TAPS - 1))
                    ins.then_inc(*pe_pre.done(item))
                elif item in ("r0", "r1"):
                    o = claim(item)
                    pe.matmul(o[:].rearrange("p (b s) -> p b s", b=GB), res_t[:, int(item[1:]), :],
                              xn_t[:, :, TAPS - 1:], start=True, stop=True).then_inc(*pe_pre.done(item))
                elif item == "bc":
                    o = claim("bc")
                    pe.wait_ge(*act_pre.at("u1", g))
                    for h in range(2):
                        ins = pe.matmul(o[0:104, :], xp_t[:, h, :], u_c[:, h, :], start=(h == 0), stop=(h == 1))
                    ins.then_inc(*pe_pre.done("bc"))
                elif item == "d":
                    for h in range(2):
                        o = claim(f"d{h}")
                        pe.wait_ge(*act_pre.at("dt", g))
                        pe.matmul(o[:], dtw_t[96:104, h, :], dt_s, start=True, stop=True,
                                  tile_position=(96, 0)).then_inc(*pe_pre.done(f"d{h}"))

            def scan(item, g, claim):
                def widen(psum, name, row, read_by):
                    if read_by is not None:
                        pe.wait_ge(*read_by)
                    pe.matmul(psum[:], sel_bc[:, row:row + 1].to_broadcast([96, P]), bc3[:], start=True,
                              stop=True).then_inc(*pe_scan.done(name))

                if item == "start":
                    pe.wait_ge(*dve_pre.at("bc_lo", g))
                    widen(b_wide, "b0", 0, None if first(g) else dve_scan.at(f"drive{NS - 1}", g - 1))
                elif item[0] == "h":
                    s = int(item[1:])
                    if s + 1 < NS:
                        widen(b_wide, f"b{s + 1}", s + 1, dve_scan.at(f"drive{s}", g))
                elif item[0] == "d":
                    s = int(item[1:])
                    widen(c_wide, f"c{s}", NS + s, dve_scan.at(f"read{s - 1}", g) if s else
                          None if first(g) else dve_scan.at(f"read{NS - 1}", g - 1))

            def att(item, g, claim):
                if item == "op":
                    o = claim("op")
                    pe.wait_ge(*dve_att.at("yg", g))
                    for b in range(GB):
                        for h in range(2):
                            ins = pe.matmul(seq(o, b), u_c[:, h, b * P:(b + 1) * P], out_t[:, h, :],
                                            start=(h == 0), stop=(h == 1))
                    ins.then_inc(*pe_att.done("op"))
                elif item == "xn2T":
                    o = claim("xn2T")
                    pe.wait_ge(*dve_att.at(f"xn{GB - 1}", g))
                    to_features(o, xn_n["att"]).then_inc(*pe_att.done("xn2T"))
                elif item[0] == "q":
                    o = claim(item)
                    k = int(item[1:])
                    pe.wait_ge(*act_att.at("xnT", g))
                    product(o, w_q[:, k * P:(k + 1) * P], x2n_t[:]).then_inc(*pe_att.done(item))
                elif item == "k":
                    product(claim("k"), w_k2[:].rearrange("p a d -> p (a d)"), x2n_t[:]).then_inc(*pe_att.done("k"))
                elif item == "v":
                    o = claim("v")
                    n = DH + NH
                    for b in range(GB):
                        pe.matmul(o[:, b * n:(b + 1) * n], seq(x2n_t, b), w_vn[:], start=True, stop=False)
                        ins = pe.matmul(o[:, b * n:(b + 1) * n], ones_row[:], vn_row[:], start=False, stop=True)
                    ins.then_inc(*pe_att.done("v"))
                elif item[0] == "S":
                    b = int(item[1:])
                    tok = slice(b * P, (b + 1) * P)
                    for i in range(4):
                        o = claim(f"s{i}_{b}")
                        if b == 0 and i == 0:
                            pe.wait_ge(*act_att.at("k", g))
                            pe.wait_ge(*dve_att.at("mask", g))
                        r = 64 * (i % 2)
                        pe.matmul(o[:].rearrange("p (h j) -> p h j", h=4), ones_bf[r:r + 1, :],
                                  key_mask[r:r + 1, tok].unsqueeze(1).to_broadcast([1, 4, P]), start=True, stop=False)
                        for j in range(4):
                            ins = pe.matmul(o[:, j * P:(j + 1) * P], q_t[r:r + 64, head_at(4 * i + j) // 2, tok],
                                            k_t[r:r + 64, tok], start=False, stop=(j == 3))
                        ins.then_inc(*pe_att.done(f"s{i}_{b}"))
                elif item[0] == "T":
                    b = int(item[1:])
                    pe.wait_ge(*act_att.at(f"p_{b}", g))
                    for i in range(4):
                        o = claim(f"t{i}_{b}")
                        for j in range(4):
                            ins = pe.transpose(seq(o, j), sc[:, b % 2, 4 * i + j, :], ident[:])
                        ins.then_inc(*pe_att.done(f"t{i}_{b}"))
                elif item[0] == "V":
                    b = int(item[1:])
                    for i, (h0, h1) in enumerate(PV_HEADS):
                        o = claim(f"pv{i}_{b}")
                        pe.wait_ge(*act_att.at(f"t{(h1 - 1) // 4}_{b}", g))
                        for h in range(h0, h1):
                            ins = pe.matmul(o[:, (h - h0) * (DH + 1):(h - h0 + 1) * (DH + 1)], p_t[:, h, :],
                                            v_a[:, b, :], start=True, stop=True)
                        ins.then_inc(*pe_att.done(f"pv{i}_{b}"))
                elif item[0] == "O":
                    b = int(item[1:])
                    for i in range(2):
                        o = claim(f"o{i}_{b}")
                        pe.wait_ge(*pool_att.at(f"on_{b}", g))
                        for j in range(4):
                            k = 4 * i + j
                            ins = pe.transpose(seq(o, j), o_n[:, 2 * k:2 * k + 2, :].rearrange("p h d -> p (h d)"),
                                               ident[:])
                        ins.then_inc(*pe_att.done(f"o{i}_{b}"))
                elif item[0] == "W":
                    b = int(item[1:])
                    o = claim(f"wo_{b}")
                    pe.wait_ge(*act_att.at(f"o1_{b}", g))
                    for k in range(8):
                        pe.matmul(o[:, 0:P], o_t[:, k, :], w_o[:, k, :], start=(k == 0), stop=False)
                    pe.matmul(o[:, 0:P], ones_row[:], o_row[:], start=False, stop=True).then_inc(*pe_att.done(f"wo_{b}"))

            def ffn(item, g, claim):
                def accumulate(e):
                    pe.wait_ge(*dve_ffn.at(f"c{e}", g))
                    pe.matmul(ffn_sum[:], f_w2[:, e, :], fh[:, e % 3, :], start=False,
                              stop=(e == ED - 1)).then_inc(*pe_ffn.done(f"acc{e}"))

                if item == "xfT":
                    o = claim("xfT")
                    pe.wait_ge(*dve_ffn.at(f"xn{GB - 1}", g))
                    to_features(o, xn_n["ffn"]).then_inc(*pe_ffn.done("xfT"))
                elif item == "lgD":
                    o = claim("lgD")
                    pe.wait_ge(*act_ffn.at("xfT", g))
                    for b in range(GB):
                        pe.matmul(o[:, b * ED:(b + 1) * ED], seq(xf_t, b), r_w[:], start=True, stop=False)
                        ins = pe.matmul(o[:, b * ED:(b + 1) * ED], ones_row[:], r_b[:], start=False, stop=True)
                    ins.then_inc(*pe_ffn.done("lgD"))
                elif item == "cwD":
                    o = claim("cwD")
                    pe.wait_ge(*dve_ffn.at("lo", g))
                    parts_to_rows(o, cw3["ffn"]).then_inc(*pe_ffn.done("cwD"))
                elif item == "z15":
                    product(claim("z15"), fs_w1[:], xf_t[:]).then_inc(*pe_ffn.done("z15"))
                elif item == "acc-1":
                    if not first(g):
                        pe.wait_ge(*act_ffn.at("ff", g - 1))
                    pe.wait_ge(*act_ffn.at("cw3", g))
                    for part in range(3):
                        pe.matmul(ffn_sum[:], eb2_p[:, part, :], cw3_t["ffn"][:], start=(part == 0), stop=False)
                    pe.wait_ge(*act_ffn.at("h15", g))
                    pe.matmul(ffn_sum[:], fs_w2[:], fh[:, 3, :], start=False, stop=False).then_inc(*pe_ffn.done("acc-1"))
                elif item in FFN_EXPERTS:
                    e = int(item[1:])
                    product(claim(f"z{e}"), f_w1[:, e, :], xf_t[:]).then_inc(*pe_ffn.done(f"z{e}"))
                    product(claim(f"cw{e}"), sel_d[0:3 * ED, e:e + 1].to_broadcast([3 * ED, P]),
                            cw3_t["ffn"][:]).then_inc(*pe_ffn.done(f"cw{e}"))
                    if e:
                        accumulate(e - 1)
                elif item == "acc14":
                    accumulate(ED - 1)
                elif item == "fin":
                    o = claim("fin")
                    pe.wait_ge(*act_ffn.at("ff", g))
                    for b in range(GB):
                        ins = pe.transpose(seq(o, b), seq(ff_t, b), ident[:])
                    ins.then_inc(*pe_ffn.done("fin"))

            todo = {"mix": mix, "pre": pre, "scan": scan, "att": att, "ffn": ffn}

            def body(i, banks, stages):
                for stage, item in SCHEDULE:
                    if stage in stages:
                        todo[stage](item, i + SHIFT[stage], lambda use: take(i, banks, stage, use))

            run_bodies(pe, setup, body)


def kernel(**inputs):
    import numpy as _np
    import concourse.bacc as _bacc
    from concourse import mybir as _mybir
    from concourse.bass_utils import run_bass_kernel_spmd as _run

    nc = _bacc.Bacc("TRN2", target_bir_lowering=False, num_devices=1)
    arrays, args = {}, {}
    for name, value in inputs.items():
        a = _np.ascontiguousarray(value)
        arrays[f"in_{name}_dram"] = a
        args[name] = nc.dram_tensor(f"in_{name}_dram", a.shape, _mybir.dt.from_np(a.dtype), kind="ExternalInput").ap()
    shape = inputs["x"].shape
    out = nc.dram_tensor("out_0_dram", shape, _mybir.dt.from_np(_np.dtype("float32")), kind="ExternalOutput").ap()
    mixture_block_kernel(nc, args, out)
    r = _run(nc, [arrays], core_ids=[0])
    return r.results[0]["out_0_dram"]
```
